# Optimizing a Trainium2 kernel written in Bass

```python
import numpy as np
import jax
import jax.numpy as jnp

def _softmax(x, axis=-1):
    return jax.nn.softmax(x, axis=axis)

def _gelu(x):
    return jax.nn.gelu(x, approximate=True)

def _silu(x):
    return jax.nn.silu(x)

def _sigmoid(x):
    return jax.nn.sigmoid(x)

def _layernorm(x, axis=-1, eps=1e-05):
    m = jnp.mean(x, axis=axis, keepdims=True)
    v = jnp.var(x, axis=axis, keepdims=True)
    return (x - m) / jnp.sqrt(v + eps)

def _scatter_add(tgt, idx, src, axis=0):
    return tgt.at[idx].add(src)

def _segment_sum(src, seg, n):
    return jax.ops.segment_sum(src, seg, n)
kernel_name = 'mk_decoder_preln_d2_seqx_r8_2ca469'

def setup_inputs(seed: int=0):
    np.random.seed(seed)
    _w = jnp.asarray

    def _rec_inputs():
        import jax
        import jax.numpy as jnp
        _rk = jax.random.key(seed)
        x = -0.0005207 + 1.001 * jax.random.normal(jax.random.fold_in(_rk, 1), (8, 256, 256), jnp.float32)
        _lenS = 256 - jax.random.randint(jax.random.fold_in(_rk, 7), (8,), 0, max(1, 256 // 4) + 1, jnp.int32)
        _lenS2 = 64 - jax.random.randint(jax.random.fold_in(_rk, 8), (8,), 0, max(1, 64 // 4) + 1, jnp.int32)
        _ctx_2048P = jax.random.normal(jax.random.fold_in(_rk, 12), (8, 16, 256), jnp.float32)
        _ctx_2048c = jax.random.dirichlet(jax.random.fold_in(_rk, 512), 0.3 * jnp.ones((16,), jnp.float32), (8, 64))
        _ctx_2048t = jnp.einsum('bsk,bkd->bsd', _ctx_2048c, _ctx_2048P)
        _ctx_2048t = _ctx_2048t * jax.lax.rsqrt(jnp.mean(jnp.square(_ctx_2048t)) + 1e-12) * 0.953939
        ctx_2048 = -5.72187e-05 + 0.999849 * (_ctx_2048t + 0.3 * jax.random.normal(jax.random.fold_in(_rk, 612), (8, 64, 256), jnp.float32))
        _validS = jnp.arange(256)[None, :] < _lenS[:, None]
        _validS2 = jnp.arange(64)[None, :] < _lenS2[:, None]
        _causal = jnp.tril(jnp.ones((256, 256), dtype=bool))
        mask_BxSx4224_bf0 = jnp.logical_not(jnp.ones((8, 256, 528), dtype=bool))
        return (x, ctx_2048, mask_BxSx4224_bf0)
    x, ctx_2048, mask_BxSx4224_bf0 = _rec_inputs()

    def _L0_attn_setup():
        import jax, jax.numpy as jnp
        import numpy as np
        D_MODEL = 256
        N_HEADS = 16
        HEAD_DIM = D_MODEL // N_HEADS

        def _alibi_slopes(n_heads: int) -> jnp.ndarray:
            start = 2.0 ** (-8.0 / n_heads)
            return jnp.asarray([start * start ** i for i in range(n_heads)], dtype=jnp.float32)
        key = jax.random.key(seed)
        ks = jax.random.split(key, 9)
        B, S, D = (2, 256, D_MODEL)
        scale = 1.0 / np.sqrt(D)
        return {'x': jax.random.normal(ks[0], (B, S, D), dtype=jnp.float32), 'wq': jax.random.normal(ks[1], (D, D), dtype=jnp.float32) * scale, 'bq': jnp.zeros((D,), dtype=jnp.float32), 'wk': jax.random.normal(ks[2], (D, D), dtype=jnp.float32) * scale, 'bk': jnp.zeros((D,), dtype=jnp.float32), 'wv': jax.random.normal(ks[3], (D, D), dtype=jnp.float32) * scale, 'bv': jnp.zeros((D,), dtype=jnp.float32), 'wo': jax.random.normal(ks[4], (D, D), dtype=jnp.float32) * scale, 'bo': jnp.zeros((D,), dtype=jnp.float32)}
    _L0_attn_all = _L0_attn_setup()
    _L0_attn_in = {k: v for k, v in _L0_attn_all.items() if k in ('wq', 'bq', 'wk', 'bk', 'wv', 'bv', 'wo', 'bo')}
    del _L0_attn_all

    def _L0_xattn_setup():
        import jax, jax.numpy as jnp
        import numpy as np
        import math
        DIM = 256
        B, Q_LEN, KV_LEN = (8, 128, 512)
        key = jax.random.key(seed)
        ks = jax.random.split(key, 8)
        x = jax.random.normal(ks[0], (B, Q_LEN, DIM), dtype=jnp.float32)
        mask = jnp.zeros((B, Q_LEN, KV_LEN + Q_LEN), dtype=bool)
        k_cache = jax.random.normal(ks[1], (B, KV_LEN, DIM), dtype=jnp.float32)
        v_cache = jax.random.normal(ks[2], (B, KV_LEN, DIM), dtype=jnp.float32)
        scale = 1.0 / math.sqrt(DIM)
        wq = jax.random.normal(ks[3], (DIM, DIM), dtype=jnp.float32) * scale
        wk = jax.random.normal(ks[4], (DIM, DIM), dtype=jnp.float32) * scale
        wv = jax.random.normal(ks[5], (DIM, DIM), dtype=jnp.float32) * scale
        wo = jax.random.normal(ks[6], (DIM, DIM), dtype=jnp.float32) * scale
        return {'x': x, 'mask': mask, 'k_cache': k_cache, 'v_cache': v_cache, 'wq': wq, 'wk': wk, 'wv': wv, 'wo': wo}
    _L0_xattn_all = _L0_xattn_setup()
    _L0_xattn_in = {k: v for k, v in _L0_xattn_all.items() if k in ('wq', 'wk', 'wv', 'wo')}
    del _L0_xattn_all

    def _L0_ffn_setup():
        import jax, jax.numpy as jnp
        import numpy as np
        NUM_EXPERTS = 8
        TOP_K = 2
        key = jax.random.key(seed)
        ks = jax.random.split(key, 5)
        B, L, D, H = (2, 256, 256, 512)
        return {'layer_input': jax.random.normal(ks[0], (B, L, D), jnp.float32), 'router_weight': jax.random.normal(ks[1], (NUM_EXPERTS, D), jnp.float32) * 0.02, 'w_in': jax.random.normal(ks[2], (NUM_EXPERTS, 2 * H, D), jnp.float32) * 0.02, 'w_out': jax.random.normal(ks[3], (NUM_EXPERTS, D, H), jnp.float32) * 0.02, 'bias': jax.random.normal(ks[4], (D,), jnp.float32) * 0.02}
    _L0_ffn_all = _L0_ffn_setup()
    _L0_ffn_in = {k: v for k, v in _L0_ffn_all.items() if k in ('router_weight', 'w_in', 'w_out', 'bias')}
    del _L0_ffn_all

    def _L1_attn_setup():
        import jax, jax.numpy as jnp
        import numpy as np
        B, S, E, H, G = (2, 256, 256, 16, 4)
        D = E // H
        key = jax.random.key(seed)
        ks = jax.random.split(key, 7)
        scale = 1.0 / np.sqrt(E)
        x = jax.random.normal(ks[0], (B, S, E), dtype=jnp.float32)
        Wq = jax.random.normal(ks[1], (H, E, D), dtype=jnp.float32) * scale
        bq = jax.random.normal(ks[2], (H, D), dtype=jnp.float32) * 0.02
        Wk = jax.random.normal(ks[3], (G, E, D), dtype=jnp.float32) * scale
        bk = jax.random.normal(ks[4], (G, D), dtype=jnp.float32) * 0.02
        Wv = jax.random.normal(ks[5], (G, E, D), dtype=jnp.float32) * scale
        bv = jax.random.normal(ks[6], (G, D), dtype=jnp.float32) * 0.02
        return {'x': x, 'Wq': Wq, 'bq': bq, 'Wk': Wk, 'bk': bk, 'Wv': Wv, 'bv': bv}
    _L1_attn_all = _L1_attn_setup()
    _L1_attn_in = {k: v for k, v in _L1_attn_all.items() if k in ('Wq', 'bq', 'Wk', 'bk', 'Wv', 'bv')}
    del _L1_attn_all

    def _L1_xattn_setup():
        import jax, jax.numpy as jnp
        import numpy as np
        D_MODEL = 256
        NUM_HEADS = 16
        HEAD_DIM = D_MODEL // NUM_HEADS

        def _fq_sym(x, axis):
            s = jnp.max(jnp.abs(x), axis=axis, keepdims=True) / 127.0
            s = jnp.maximum(s, 1e-08)
            q = jnp.clip(jnp.round(x / s), -127.0, 127.0) * s
            return x + jax.lax.stop_gradient(q - x)

        def _fq_unsigned(x, axis):
            s = jnp.max(x, axis=axis, keepdims=True) / 255.0
            s = jnp.maximum(s, 1e-08)
            q = jnp.clip(jnp.round(x / s), 0.0, 255.0) * s
            return x + jax.lax.stop_gradient(q - x)
        key = jax.random.key(seed)
        ks = jax.random.split(key, 8)
        B, N, M, C = (2, 256, 64, D_MODEL)
        return {'x': jax.random.normal(ks[0], (B, N, C), jnp.float32), 'cond': jax.random.normal(ks[1], (B, M, C), jnp.float32), 'Wq': jax.random.normal(ks[2], (C, C), jnp.float32) * 0.02, 'bq': jnp.zeros((C,), jnp.float32), 'Wkv': jax.random.normal(ks[3], (C, 2 * C), jnp.float32) * 0.02, 'bkv': jnp.zeros((2 * C,), jnp.float32), 'Wp': jax.random.normal(ks[4], (C, C), jnp.float32) * 0.02, 'bp': jnp.zeros((C,), jnp.float32)}
    _L1_xattn_all = _L1_xattn_setup()
    _L1_xattn_in = {k: v for k, v in _L1_xattn_all.items() if k in ('Wq', 'bq', 'Wkv', 'bkv', 'Wp', 'bp')}
    del _L1_xattn_all

    def _L1_ffn_setup():
        import jax, jax.numpy as jnp
        import numpy as np
        TOP_K = 4
        key = jax.random.key(seed)
        ks = jax.random.split(key, 8)
        B, S, D, E, H, HS = (2, 256, 256, 16, 128, 512)
        scaled = lambda k, shape, fan: jax.random.normal(k, shape, jnp.float32) * fan ** (-0.5)
        return {'x': jax.random.normal(ks[0], (B, S, D), jnp.float32), 'w_router': scaled(ks[1], (D, E), D), 'we1': scaled(ks[2], (E, D, H), D), 'we3': scaled(ks[3], (E, D, H), D), 'we2': scaled(ks[4], (E, H, D), H), 'ws1': scaled(ks[5], (D, HS), D), 'ws3': scaled(ks[6], (D, HS), D), 'ws2': scaled(ks[7], (HS, D), HS)}
    _L1_ffn_all = _L1_ffn_setup()
    _L1_ffn_in = {k: v for k, v in _L1_ffn_all.items() if k in ('w_router', 'we1', 'we3', 'we2', 'ws1', 'ws3', 'ws2')}
    del _L1_ffn_all
    return {'x': x, 'ctx_2048': ctx_2048, 'mask_BxSx4224_bf0': mask_BxSx4224_bf0, 'L0_attn_wq': _L0_attn_in['wq'], 'L0_attn_bq': _L0_attn_in['bq'], 'L0_attn_wk': _L0_attn_in['wk'], 'L0_attn_bk': _L0_attn_in['bk'], 'L0_attn_wv': _L0_attn_in['wv'], 'L0_attn_bv': _L0_attn_in['bv'], 'L0_attn_wo': _L0_attn_in['wo'], 'L0_attn_bo': _L0_attn_in['bo'], 'L0_xattn_wq': _L0_xattn_in['wq'], 'L0_xattn_wk': _L0_xattn_in['wk'], 'L0_xattn_wv': _L0_xattn_in['wv'], 'L0_xattn_wo': _L0_xattn_in['wo'], 'L0_ffn_router_weight': _L0_ffn_in['router_weight'], 'L0_ffn_w_in': _L0_ffn_in['w_in'], 'L0_ffn_w_out': _L0_ffn_in['w_out'], 'L0_ffn_bias': _L0_ffn_in['bias'], 'L1_attn_Wq': _L1_attn_in['Wq'], 'L1_attn_bq': _L1_attn_in['bq'], 'L1_attn_Wk': _L1_attn_in['Wk'], 'L1_attn_bk': _L1_attn_in['bk'], 'L1_attn_Wv': _L1_attn_in['Wv'], 'L1_attn_bv': _L1_attn_in['bv'], 'L1_xattn_Wq': _L1_xattn_in['Wq'], 'L1_xattn_bq': _L1_xattn_in['bq'], 'L1_xattn_Wkv': _L1_xattn_in['Wkv'], 'L1_xattn_bkv': _L1_xattn_in['bkv'], 'L1_xattn_Wp': _L1_xattn_in['Wp'], 'L1_xattn_bp': _L1_xattn_in['bp'], 'L1_ffn_w_router': _L1_ffn_in['w_router'], 'L1_ffn_we1': _L1_ffn_in['we1'], 'L1_ffn_we3': _L1_ffn_in['we3'], 'L1_ffn_we2': _L1_ffn_in['we2'], 'L1_ffn_ws1': _L1_ffn_in['ws1'], 'L1_ffn_ws3': _L1_ffn_in['ws3'], 'L1_ffn_ws2': _L1_ffn_in['ws2']}

def reference(x, ctx_2048, mask_BxSx4224_bf0, L0_attn_wq, L0_attn_bq, L0_attn_wk, L0_attn_bk, L0_attn_wv, L0_attn_bv, L0_attn_wo, L0_attn_bo, L0_xattn_wq, L0_xattn_wk, L0_xattn_wv, L0_xattn_wo, L0_ffn_router_weight, L0_ffn_w_in, L0_ffn_w_out, L0_ffn_bias, L1_attn_Wq, L1_attn_bq, L1_attn_Wk, L1_attn_bk, L1_attn_Wv, L1_attn_bv, L1_xattn_Wq, L1_xattn_bq, L1_xattn_Wkv, L1_xattn_bkv, L1_xattn_Wp, L1_xattn_bp, L1_ffn_w_router, L1_ffn_we1, L1_ffn_we3, L1_ffn_we2, L1_ffn_ws1, L1_ffn_ws3, L1_ffn_ws2):
    import jax
    import jax.numpy as jnp

    def _L0_attn_ref(x, wq, bq, wk, bk, wv, bv, wo, bo):
        import jax, jax.numpy as jnp
        import numpy as np
        D_MODEL = 256
        N_HEADS = 16
        HEAD_DIM = D_MODEL // N_HEADS

        def _alibi_slopes(n_heads: int) -> jnp.ndarray:
            start = 2.0 ** (-8.0 / n_heads)
            return jnp.asarray([start * start ** i for i in range(n_heads)], dtype=jnp.float32)
        B, S, D = x.shape
        H, hd = (N_HEADS, HEAD_DIM)

        def heads(y):
            return y.reshape(B, S, H, hd).transpose(0, 2, 1, 3)
        q = heads(x @ wq + bq)
        k = heads(x @ wk + bk)
        v = heads(x @ wv + bv)
        scores = jnp.einsum('bhqd,bhkd->bhqk', q, k) / jnp.sqrt(jnp.float32(hd))
        pos = jnp.arange(S)
        rel = pos[None, :] - pos[:, None]
        slopes = _alibi_slopes(H)
        bias = slopes[:, None, None] * rel.astype(jnp.float32)
        causal = jnp.where(rel > 0, -jnp.inf, 0.0).astype(jnp.float32)
        scores = scores + (bias + causal)[None]
        attn = jax.nn.softmax(scores, axis=-1)
        out = jnp.einsum('bhqk,bhkd->bhqd', attn, v)
        out = out.transpose(0, 2, 1, 3).reshape(B, S, D)
        return out @ wo + bo

    def _L0_xattn_ref(x, mask, k_cache, v_cache, wq, wk, wv, wo):
        import jax, jax.numpy as jnp
        import numpy as np
        import math
        DIM = 256
        B, Q_LEN, KV_LEN = (8, 128, 512)
        q = jnp.einsum('bsd,ed->bse', x, wq)
        k_new = jnp.einsum('bsd,ed->bse', x, wk)
        v_new = jnp.einsum('bsd,ed->bse', x, wv)
        k = jnp.concatenate([k_cache, k_new], axis=1)
        v = jnp.concatenate([v_cache, v_new], axis=1)
        scale = 1.0 / math.sqrt(q.shape[-1])
        scores = jnp.einsum('bqd,bkd->bqk', q, k) * scale
        attn = jax.nn.softmax(scores, axis=-1)
        out = jnp.einsum('bqk,bkd->bqd', attn, v)
        return jnp.einsum('bqd,ed->bqe', out, wo)

    def _L0_ffn_ref(layer_input, router_weight, w_in, w_out, bias):
        import jax, jax.numpy as jnp
        import numpy as np
        NUM_EXPERTS = 8
        TOP_K = 2
        B, L, D = layer_input.shape
        x = layer_input.reshape(-1, D)
        T = x.shape[0]
        logits = (x @ router_weight.T).astype(jnp.float32)
        top_vals, top_idx = jax.lax.top_k(logits, TOP_K)
        top_gates = jax.nn.softmax(top_vals, axis=1).astype(x.dtype)
        dense_gates = jnp.zeros((T, NUM_EXPERTS), x.dtype)
        dense_gates = dense_gates.at[jnp.arange(T)[:, None], top_idx].set(top_gates)

        def expert_step(acc, ew):
            wi, wo, g = ew
            h = x @ wi.T
            a, b = jnp.split(h, 2, axis=-1)
            o = jax.nn.silu(a) * b @ wo.T
            return (acc + g[:, None] * o, None)
        acc, _ = jax.lax.scan(expert_step, jnp.zeros_like(x), (w_in, w_out, dense_gates.T))
        return acc.reshape(B, L, D) + bias

    def _L1_attn_ref(x, Wq, bq, Wk, bk, Wv, bv):
        import jax, jax.numpy as jnp
        import numpy as np
        B, S, E, H, G = (2, 256, 256, 16, 4)
        D = E // H
        h, e, d = Wq.shape
        g = Wk.shape[0]
        per = h // g
        s = x.shape[1]
        q = jnp.einsum('bse,hed->bhsd', x, Wq) + bq[None, :, None, :]
        kg = jnp.einsum('bse,ged->bgsd', x, Wk) + bk[None, :, None, :]
        vg = jnp.einsum('bse,ged->bgsd', x, Wv) + bv[None, :, None, :]
        k = jnp.repeat(kg, per, axis=1)
        v = jnp.repeat(vg, per, axis=1)
        scores = jnp.einsum('bhqd,bhkd->bhqk', q, k) * (1.0 / np.sqrt(d))
        causal = jnp.triu(jnp.ones((s, s), dtype=bool), k=1)
        scores = jnp.where(causal[None, None, :, :], -jnp.inf, scores)
        attn = jax.nn.softmax(scores, axis=-1)
        out = jnp.einsum('bhqk,bhkd->bhqd', attn, v)
        return out.transpose(0, 2, 1, 3).reshape(x.shape[0], s, h * d)

    def _L1_xattn_ref(x, cond, Wq, bq, Wkv, bkv, Wp, bp):
        import jax, jax.numpy as jnp
        import numpy as np
        D_MODEL = 256
        NUM_HEADS = 16
        HEAD_DIM = D_MODEL // NUM_HEADS

        def _fq_sym(x, axis):
            s = jnp.max(jnp.abs(x), axis=axis, keepdims=True) / 127.0
            s = jnp.maximum(s, 1e-08)
            q = jnp.clip(jnp.round(x / s), -127.0, 127.0) * s
            return x + jax.lax.stop_gradient(q - x)

        def _fq_unsigned(x, axis):
            s = jnp.max(x, axis=axis, keepdims=True) / 255.0
            s = jnp.maximum(s, 1e-08)
            q = jnp.clip(jnp.round(x / s), 0.0, 255.0) * s
            return x + jax.lax.stop_gradient(q - x)
        B, N, C = x.shape
        H, hd = (NUM_HEADS, HEAD_DIM)
        q = (x @ Wq + bq).reshape(1, B * N, H, hd)
        kv = (cond @ Wkv + bkv).reshape(1, -1, 2, H, hd)
        k, v = (kv[:, :, 0], kv[:, :, 1])
        scale = 1.0 / np.sqrt(hd).astype(np.float32)
        q = jnp.transpose(q * scale, (0, 2, 1, 3))
        k = jnp.transpose(k, (0, 2, 1, 3))
        v = jnp.transpose(v, (0, 2, 1, 3))
        q = _fq_sym(q, axis=-1)
        k = _fq_sym(k, axis=-1)
        v = _fq_sym(v, axis=2)
        attn = jnp.einsum('bhqd,bhkd->bhqk', q, k)
        attn = jax.nn.softmax(attn.astype(jnp.float32), axis=-1)
        attn = _fq_unsigned(attn, axis=-1)
        out = jnp.einsum('bhqk,bhkd->bhqd', attn, v)
        out = jnp.transpose(out, (0, 2, 1, 3)).reshape(B, N, C)
        return out @ Wp + bp

    def _L1_ffn_ref(x, w_router, we1, we3, we2, ws1, ws3, ws2):
        import jax, jax.numpy as jnp
        import numpy as np
        TOP_K = 4
        B, S, D = x.shape
        T = B * S
        E = w_router.shape[1]
        xt = x.reshape(T, D)
        probs = jax.nn.softmax(xt @ w_router, axis=-1)
        top_w, top_i = jax.lax.top_k(probs, TOP_K)
        top_w = top_w / jnp.sum(top_w, axis=-1, keepdims=True)
        cw = jnp.zeros((T, E), xt.dtype).at[jnp.arange(T)[:, None], top_i].add(top_w)
        g = jax.nn.silu(jnp.einsum('td,edh->teh', xt, we1)) * jnp.einsum('td,edh->teh', xt, we3)
        g = g * cw[:, :, None]
        moe_out = jnp.einsum('teh,ehd->td', g, we2)
        shared = jax.nn.silu(xt @ ws1) * (xt @ ws3) @ ws2
        k = TOP_K
        out = shared / (k + 1) + moe_out * (k / (k + 1))
        return out.reshape(B, S, D)
    x = x + _L0_attn_ref(_layernorm(x, axis=-1), L0_attn_wq, L0_attn_bq, L0_attn_wk, L0_attn_bk, L0_attn_wv, L0_attn_bv, L0_attn_wo, L0_attn_bo)
    x = x + _L0_xattn_ref(_layernorm(x, axis=-1), mask_BxSx4224_bf0, ctx_2048, ctx_2048, L0_xattn_wq, L0_xattn_wk, L0_xattn_wv, L0_xattn_wo)
    x = x + _L0_ffn_ref(_layernorm(x, axis=-1), L0_ffn_router_weight, L0_ffn_w_in, L0_ffn_w_out, L0_ffn_bias)
    x = x + _L1_attn_ref(_layernorm(x, axis=-1), L1_attn_Wq, L1_attn_bq, L1_attn_Wk, L1_attn_bk, L1_attn_Wv, L1_attn_bv)
    x = x + _L1_xattn_ref(_layernorm(x, axis=-1), ctx_2048, L1_xattn_Wq, L1_xattn_bq, L1_xattn_Wkv, L1_xattn_bkv, L1_xattn_Wp, L1_xattn_bp)
    x = x + _L1_ffn_ref(_layernorm(x, axis=-1), L1_ffn_w_router, L1_ffn_we1, L1_ffn_we3, L1_ffn_we2, L1_ffn_ws1, L1_ffn_ws3, L1_ffn_ws2)
    return x

_drawn_inputs = setup_inputs


def setup_inputs(seed=0):
    import zlib

    import numpy as np

    out = dict(_drawn_inputs(seed))
    spreads = {'L0_attn_bq': (0.0, 0.1),
     'L0_attn_bk': (0.0, 2.0),
     'L0_attn_bv': (0.0, 0.1),
     'L0_attn_bo': (0.0, 0.1),
     'L1_xattn_bq': (0.0, 0.8),
     'L1_xattn_bkv': (0.0, 0.1),
     'L1_xattn_bp': (0.0, 0.1)}
    factors = {'L0_ffn_router_weight': 7.266,
     'L1_attn_bq': 7.886,
     'L1_attn_bk': 64.0,
     'L1_xattn_Wq': 8.0,
     'L1_xattn_Wkv': 2.674}
    for name, (base, spread) in spreads.items():
        noise = np.random.default_rng([zlib.crc32(name.encode()), seed]).standard_normal(out[name].shape)
        drawn = base * np.exp(spread * noise) if base else spread * noise
        out[name] = jnp.asarray(drawn.astype(out[name].dtype))
    for name, factor in factors.items():
        out[name] = (out[name] * factor).astype(out[name].dtype)
    return out
```

```python
from contextlib import ExitStack

import numpy as np

import concourse.bass as bass
from concourse import mybir

F32 = mybir.dt.float32
BF = mybir.dt.bfloat16
ALU = mybir.AluOpType
ACT = mybir.ActivationFunctionType
AX = mybir.AxisListType.X
MAGIC = 12582912.0
BIG = 3.0e38
LN255 = float(np.log(255.0))

B, S, D, H, T = 8, 256, 256, 16, 16
POS = ((0, 3, 5), (1, 4), (2,))


class Prog:

    ENG = ("tensor", "vector", "scalar", "gpsimd", "sync")

    def __init__(self, nc, ctx):
        self.nc, self.ctx = nc, ctx
        self.q = {e: [] for e in self.ENG}
        self.sem = {e: ctx.enter_context(nc.semaphore("s_" + e)) for e in self.ENG}
        self.count = {e: 0 for e in self.ENG}
        self.seen = {e: {} for e in self.ENG}
        self.groups = []

    def wait(self, e, after):
        for t in after:
            if not t:
                continue
            if type(t) is list:
                self.wait(e, t)
                continue
            name, s, v = t
            if self.seen[e].get(name, 0) < v:
                self.seen[e][name] = v
                self.q[e].append(lambda eng, s=s, v=v: eng.wait_ge(s, v))

    def put(self, e, fn, after=(), sig=True):
        self.wait(e, after)
        if not sig:
            self.q[e].append(fn)
            return None
        self.count[e] += 1
        s = self.sem[e]
        self.q[e].append(lambda eng: fn(eng).then_inc(s, 1))
        return (e, s, self.count[e])

    def group(self, name):
        g = [name, self.ctx.enter_context(self.nc.semaphore("d_" + name)), 0]
        self.groups.append(g)
        return g

    def dma(self, e, g, out, in_, after=()):
        self.wait(e, after)
        g[2] += 16
        s = g[1]
        self.q[e].append(lambda eng: eng.dma_start(out, in_).then_inc(s, 16))

    def landed(self, g):
        return (g[0], g[1], g[2])

    def emit(self):
        with self.nc.Block() as block:
            def body(e):
                def run(eng):
                    for f in self.q[e]:
                        f(eng)
                return run
            block.tensor(body("tensor"))
            block.vector(body("vector"))
            block.scalar(body("scalar"))
            block.gpsimd(body("gpsimd"))
            block.sync(body("sync"))


def bc(ap, dim, n):
    shape = list(ap.shape)
    ix = tuple(slice(None) for _ in range(dim)) + (None,)
    return ap[ix].to_broadcast(shape[:dim] + [n] + shape[dim:])


def decoder(nc, I, out, upto=6):
    with ExitStack() as ctx:
        P = Prog(nc, ctx)

        def sb(name, shape, dt=F32):
            return ctx.enter_context(nc.sbuf_tensor(name, shape, dt))

        PS = [ctx.enter_context(nc.psum_tensor(f"ps{i}", [128, 512], F32)) for i in range(8)]
        PB = [p[:, :].bitcast(BF) for p in PS]
        bfree = [[] for _ in range(8)]

        class Ring:
            def __init__(self, banks):
                self.banks, self.n = banks, 0

            def take(self):
                b = self.banks[self.n % len(self.banks)]
                self.n += 1
                return b

        x = sb("x", [128, T, D])
        xnT = sb("xnT", [128, 2, T * 128])
        xn = sb("xn", [128, 2, D])
        st = sb("st", [128, T, 6])
        mv = sb("mv", [128, T, 2])
        ve = sb("ve", [128, T])
        rstd = sb("rstd", [128, T])
        half = sb("half", [128, 1])
        idf = sb("idf", [128, 128])
        idb = sb("idb", [128, 128], BF)
        maskQ = sb("maskQ", [128, 128], BF)
        maskK = sb("maskK", [128, 128], BF)
        E = sb("E", [48, H, 128], BF)
        W = sb("W", [128, 24736])
        ctxT = sb("ctxT", [128, 2, 512])
        ctxN = sb("ctxN", [64, 8, D])
        work = sb("work", [128, 9700])
        wof = [0]

        def wk(n, dt=F32):
            a = wof[0]
            wof[0] += n
            assert wof[0] <= 9700, wof[0]
            v = work[:, a:a + n]
            return v if dt is F32 else v.bitcast(dt)

        gx = [P.group(f"x{i}") for i in range(4)]
        gc, gw0, gb = P.group("c"), P.group("w0"), P.group("b")
        xd = I["x"].rearrange("(t p) d -> p t d", p=128)
        for i in range(4):
            P.dma("sync", gx[i], x[:, 4 * i:4 * i + 4, :], xd[:, 4 * i:4 * i + 4, :])
        SM = sb("SM", [128, 5392])
        so = [0]

        def small(name, g, shape, src, e="sync"):
            n = int(np.prod(shape))
            a = so[0]
            so[0] += n
            assert so[0] <= 5392
            P.dma(e, g, SM[:, a:a + n].rearrange("p (a b) -> p a b", b=shape[-1]) if len(shape) == 2 else SM[:, a:a + n], src)
            v = SM[:, a:a + n]
            return v.rearrange("p (a b) -> p a b", b=shape[-1]) if len(shape) == 2 else v

        def bcast(v):
            return bass.AP(v.tensor, v.offset, [[0, 128]] + [list(p) for p in v.ap])

        def weight(name, g, n):
            return small(name, g, [2, n], I[name].rearrange("(k p) n -> p k n", p=128))

        xf = xnT[:, :, :].rearrange("p k n -> p (k n)")
        P.dma("sync", gc, W[:, 0:384], I["c_sq"])
        P.dma("sync", gc, xf[:, 0:2048], I["c_ali"])
        P.dma("sync", gc, xf[0:48, 2048:4096], I["c_E"])
        wA = [weight("w_att0", gw0, 768)]
        wo0 = weight("w_o0", gw0, 256)
        bA = [small("b_att0", gb, [768], bcast(I["b_att0"]))]
        bo0 = small("b_o0", gb, [256], bcast(I["b_o0"]))

        z0 = P.put("vector", lambda e: e.memset(half[:, :], -0.5))
        tid = P.put("vector", lambda e: e.tensor_copy(idf[:, :], W[:, 0:128]), [P.landed(gc)])
        P.put("vector", lambda e: e.tensor_copy(idb[:, :], W[:, 0:128]))
        P.put("vector", lambda e: e.tensor_copy(maskQ[:, :], W[:, 128:256]))
        P.put("vector", lambda e: e.tensor_copy(maskK[:, :], W[:, 256:384]))
        tE = P.put("vector", lambda e: e.tensor_copy(E[:, :, :], xf[0:48, 2048:4096].rearrange("p (h k) -> p h k", h=H)))
        t_ali = P.landed(gc)

        gxa = P.group("xa")
        wxa = weight("w_xa0", gxa, 1024)
        P.dma("sync", gxa, ctxT[:, :, :], I["ctxT"].rearrange("(k p) n -> p k n", p=128))
        P.dma("sync", gxa, ctxN[:, :, :], I["ctxN"])
        gm0 = P.group("m0")
        win0 = W[:, 0:16384].rearrange("p (k n) -> p k n", k=2)
        wout0 = W[:, 16384:24576].rearrange("p (c n) -> p c n", c=32)
        win_d = I["w_in0"].rearrange("(k p) n -> p k n", p=128)
        P.dma("sync", gm0, win0[:, 0, :], win_d[:, 0, :], [tE])
        P.dma("sync", gm0, win0[:, 1, 0:4096], win_d[:, 1, 0:4096])
        wr0 = weight("w_r0", gm0, 8)
        bm0 = small("b_m0", gm0, [256], bcast(I["b_m0"]))
        gat1 = P.group("at1")
        wA.append(W[:, 18464:19232].rearrange("p (k n) -> p k n", k=2))
        bA.append(W[:, 19232:19616])
        gx1 = P.group("cr1")

        xt = [P.landed(gx[t // 4]) for t in range(T)]
        xnT_rd = [[] for _ in range(T)]
        xnT_wr = [None] * T
        xn_rd = [None, None]
        prev = {"wk": []}

        def layernorm(pair, ring):
            b = ring.take()
            for j in (0, 1):
                t = 2 * pair + j
                a = P.put("vector", lambda e, t=t: e.bn_stats(st[:, t, :], x[:, t, :]), [xt[t], xn_rd[j]])
                a = P.put("vector", lambda e, t=t: e.bn_aggr(mv[:, t, :], st[:, t, :]), [a])
                a1 = P.put("vector", lambda e, t=t: e.tensor_scalar(ve[:, t:t + 1], mv[:, t, 1:2], 1e-5, None, ALU.add), [a])
                a2 = P.put("gpsimd", lambda e, t=t: e.tensor_tensor(rstd[:, t:t + 1], ve[:, t:t + 1], half[:, :], ALU.pow), [a1, z0])
                a3 = P.put("vector", lambda e, t=t, j=j: e.tensor_scalar(
                    xn[:, j, :], x[:, t, :], mv[:, t, 0:1], rstd[:, t:t + 1], ALU.subtract, ALU.mult), [a2, a])
                for k in (0, 1):
                    a4 = P.put("tensor", lambda e, j=j, k=k, b=b: e.transpose(
                        PS[b][:, 256 * k + 128 * j:256 * k + 128 * j + 128], xn[:, j, 128 * k:128 * k + 128], idf[:, :]),
                        [a3, tid, bfree[b]])
                xn_rd[j] = a4
            a5 = P.put("scalar", lambda e, b=b, pair=pair: e.copy(
                xnT[:, :, 256 * pair:256 * pair + 256], PS[b][:, :].rearrange("p (k n) -> p k n", k=2)),
                [a4, xnT_rd[2 * pair], xnT_rd[2 * pair + 1]])
            bfree[b] = [a5]
            for t in (2 * pair, 2 * pair + 1):
                xnT_wr[t], xnT_rd[t] = a5, []

        def mms(out_, pairs, after, start=True, **kw):
            n = len(pairs)
            for i, (l, r) in enumerate(pairs):
                tok = P.put("tensor", lambda e, l=l, r=r, i=i: e.matmul(
                    out_, l, r, start=start and i == 0, stop=i == n - 1, skip_group_check=True),
                    after if i == 0 else (), sig=i == n - 1)
            return tok

        def attn_phase(L):
            wof[0] = 0
            NK = 16 if L == 0 else 4
            per = H // NK
            NW = 768 if L == 0 else 384
            QK = 256 + NK * 16
            Wt, bias = wA[L], bA[L]
            wtok = [P.landed(gw0), P.landed(gb)] if L == 0 else [P.landed(gat1)]
            base = prev["wk"]
            wo_ = [12288 if L == 0 else 19616]

            def wb(n, h):
                a = wo_[0]
                wo_[0] += n * h // 2
                return W[:, a:a + n * h // 2].bitcast(BF).rearrange("p (h c) -> p h c", h=h)

            if L == 0:
                QR = [wb(128, H) for _ in range(2)]
                KR = [wb(128, NK) for _ in range(2)]
            else:
                QR = [wk(1024, BF).rearrange("p (h c) -> p h c", c=128) for _ in range(2)]
                KR = [wk(NK * 64, BF).rearrange("p (h c) -> p h c", c=128) for _ in range(2)]
            qs = [wb(256, H) for _ in range(2)]
            ks = [wb(256, NK) for _ in range(2)]
            qkf = wk(512)
            p1 = wk(256, BF)
            p2 = wk(256, BF)
            p3 = wk(256, BF)
            Vt = [[wk(NK * 32).rearrange("p (h c) -> p h c", c=32) for _ in range(2)] for _ in range(2)]
            m = wk(32).rearrange("p (j h) -> p j h", j=2)
            mr = wk(32).rearrange("p (j h) -> p j h", j=2)
            NP = wk(48, BF).rearrange("p (j c h) -> p j c h", j=2, c=3)
            mT = wk(128, BF)[0:48, :]
            PT = [wk(512) for _ in range(4)]
            OT = wk(1024).rearrange("p (g n) -> p g n", g=4)
            rc = wk(16)
            On = wk(256)
            OnT = wk(256).rearrange("p (k n) -> p k n", k=2)
            zt = []
            for j in range(2):
                z = P.put("vector", lambda e, j=j: e.memset(QR[j][:, :, 96:128], 0.0), base)
                zt.append(z)
                zt.append(P.put("vector", lambda e, j=j: e.memset(KR[j][:, :, 96:128], 0.0)))
                if L == 0:
                    for R, o in ((QR, 0), (KR, 1024)):
                        zt.append(P.put("vector", lambda e, j=j, R=R, o=o: e.tensor_copy(
                            R[j][:, :, 96:128],
                            xf[:, o + 512 * j:o + 512 * j + 512].rearrange("p (h c) -> p h c", c=32)), [z, zt[-1], t_ali]))
                for i in range(2):
                    z2 = P.put("gpsimd", lambda e, i=i, j=j: e.memset(Vt[i][j], 0.0), base)
                    zt.append(P.put("gpsimd", lambda e, i=i, j=j: e.memset(Vt[i][j][:, :, 16:17], 1.0), [z2]))
            if L == 0:
                xnT_rd[0], xnT_rd[1] = [tE] + zt, [tE] + zt
                for t in range(2, T):
                    xnT_rd[t] = [tE] + zt
            rp = Ring([0, 1])
            rs = Ring([2, 3, 4, 5])
            ro = Ring([6, 7])
            st_ = {"qkf": [], "p": [], "m": [], "NP": [], "mT": [], "PT": [[] for _ in PT], "OT": [], "On": [], "OnT": [],
                   "QR": [[], []], "qs": [[], []], "V": [[[], []], [[], []]], "rc": []}
            nPT = [0]
            S_ = [dict() for _ in range(B)]

            def project(b):
                layernorm(b, rp)
                for j in range(2):
                    t = 2 * b + j
                    lh = [xnT[:, k, 128 * t:128 * t + 128] for k in range(2)]
                    ba = rp.take()
                    qk = mms(PS[ba][:, 0:min(NW, 512)], [(lh[k], Wt[:, k, 0:min(NW, 512)]) for k in range(2)],
                             [xnT_wr[t], wtok, bfree[ba]])
                    if L == 0:
                        bb = rp.take()
                        vv = mms(PS[bb][:, 0:256], [(lh[k], Wt[:, k, 512:768]) for k in range(2)], [bfree[bb]])
                        vp, vo = PS[bb][:, 0:256], 512
                    else:
                        vv, vp, vo = qk, PS[ba][:, QK:NW], QK
                    xnT_rd[t] = [vv]
                    a = P.put("vector", lambda e, ba=ba: e.tensor_tensor(qkf[:, 0:QK], PS[ba][:, 0:QK], bias[:, 0:QK], ALU.add),
                              [qk, wtok, st_["qkf"], base])
                    v = P.put("vector", lambda e, vp=vp, vo=vo, b=b, j=j: e.tensor_tensor(
                        Vt[b % 2][j][:, :, 0:16], vp.rearrange("p (h d) -> p h d", d=16),
                        bias[:, vo:vo + NK * 16].rearrange("p (h d) -> p h d", d=16), ALU.add),
                        [vv, zt, st_["V"][b % 2][j]])
                    bfree[ba] = [a, v]
                    if L == 0:
                        bfree[bb] = [v]
                    S_[b]["V", j] = v
                    c1 = P.put("scalar", lambda e: e.copy(p1[:, 0:QK], qkf[:, 0:QK]), [a, st_["p"], base])
                    r1 = P.put("vector", lambda e: e.tensor_tensor(qkf[:, 0:QK], qkf[:, 0:QK], p1[:, 0:QK], ALU.subtract), [c1])
                    c2 = P.put("scalar", lambda e: e.copy(p2[:, 0:QK], qkf[:, 0:QK]), [r1])
                    c3 = P.put("vector", lambda e: e.tensor_tensor(p3[:, 0:QK], qkf[:, 0:QK], p2[:, 0:QK], ALU.subtract), [c2])
                    st_["qkf"] = [c3]
                    w = []
                    Q6 = QR[j][:, :, 0:96].rearrange("p h (c d) -> p h c d", d=16)
                    K6 = KR[j][:, :, 0:96].rearrange("p h (c d) -> p h c d", d=16)
                    part = [p_[:, 0:QK] for p_ in (p1, p2, p3)]

                    def cp(dst, src, n, eng="vector"):
                        s = src.rearrange("p (h d) -> p h d", d=16)
                        if n > 1:
                            s = bc(s, 2, n)
                        if eng == "vector":
                            w.append(P.put("vector", lambda e: e.tensor_copy(dst, s), [c3, st_["QR"][j], zt]))
                        else:
                            w.append(P.put("scalar", lambda e: e.copy(dst, s), [c3, st_["QR"][j], zt]))
                    for c in (0, 3):
                        pass
                    cp(Q6[:, :, 0:4:3, :], part[0][:, 0:256], 2)
                    cp(Q6[:, :, 1:5:3, :], part[1][:, 0:256], 2)
                    cp(Q6[:, :, 2, :], part[2][:, 0:256], 1)
                    cp(Q6[:, :, 5, :], part[0][:, 0:256], 1)
                    cp(K6[:, :, 0:3, :], part[0][:, 256:QK], 3)
                    cp(K6[:, :, 3:5, :], part[1][:, 256:QK], 2)
                    cp(K6[:, :, 5, :], part[2][:, 256:QK], 1)
                    st_["p"] = w
                    S_[b]["R", j] = w

            def transposes(b):
                tk = []
                for j in range(2):
                    rd = []
                    for R, dst, n in ((QR, qs, H), (KR, ks, NK)):
                        for c in range(0, n, 8):
                            m_ = min(8, n - c)
                            bk = rp.take()
                            for h in range(m_):
                                tr = P.put("tensor", lambda e, R=R, j=j, c=c, h=h, bk=bk: e.transpose(
                                    PB[bk][:, 128 * h:128 * h + 128], R[j][:, c + h, :], idb[:, :]),
                                    [S_[b]["R", j], bfree[bk], tE] if h == 0 else (), sig=h == m_ - 1)
                            rd.append(tr)
                            src = PB[bk][:, 0:128 * m_].rearrange("p (h n) -> p h n", h=m_)
                            dd = dst[b % 2][:, c:c + m_, 128 * j:128 * j + 128]
                            if c == 0:
                                ev = P.put("scalar", lambda e, dd=dd, src=src: e.copy(dd, src), [tr, st_["qs"][b % 2]])
                            else:
                                ev = P.put("vector", lambda e, dd=dd, src=src: e.tensor_copy(dd, src), [tr, st_["qs"][b % 2]])
                            bfree[bk] = [ev]
                            tk.append(ev)
                    st_["QR"][j] = rd
                S_[b]["qs"] = tk

            def scores(b):
                q, k_ = qs[b % 2], ks[b % 2]
                last = []
                for j in range(2):
                    n = 4 if j == 0 else 2
                    w_ = 512 // n
                    for h0 in range(0, H, n):
                        bk = rs.take()
                        for i in range(n):
                            h = h0 + i
                            P.put("tensor", lambda e, h=h, i=i, bk=bk, w_=w_, j=j: e.matmul(
                                PS[bk][:, w_ * i:w_ * i + w_], q[:, h, 128 * j:128 * j + 128], k_[:, h // per, 0:w_],
                                start=i == 0, stop=False, skip_group_check=True),
                                [S_[b]["qs"], bfree[bk]] if i == 0 else (), sig=False)
                        ov = PS[bk][:, :].rearrange("p (i n) -> p i n", i=n)
                        mm = P.put("tensor", lambda e, ov=ov, n=n, w_=w_: e.matmul(
                            ov[:, :, w_ - 128:w_], idb[:, :], bc(maskQ[:, :], 1, n), start=False, stop=True,
                            skip_group_check=True))
                        mx = P.put("vector", lambda e, ov=ov, j=j, h0=h0, n=n: e.tensor_reduce(
                            m[:, j, h0:h0 + n], ov, AX, ALU.max), [mm, st_["m"] if not last else (), base])
                        bfree[bk] = [mx]
                        last.append(mx)
                S_[b]["S"] = mm
                a = P.put("vector", lambda e: e.tensor_scalar(NP[:, :, 0, :], m, -1.0, None, ALU.mult), [mx, st_["NP"]])
                a = P.put("vector", lambda e: e.scalar_tensor_tensor(
                    out=mr, in0=m, scalar=-1.0, in1=NP[:, :, 0, :], op0=ALU.mult, op1=ALU.subtract), [a])
                st_["m"] = [a]
                a2 = P.put("vector", lambda e: e.tensor_copy(NP[:, :, 1, :], mr), [a])
                a3 = P.put("vector", lambda e: e.tensor_tensor(NP[:, :, 2, :], mr, NP[:, :, 1, :], ALU.subtract), [a2])
                S_[b]["NP"] = a3

            def fold(b):
                bk = rp.take()
                for j in range(2):
                    tr = P.put("tensor", lambda e, j=j, bk=bk: e.transpose(
                        PB[bk][0:48, 128 * j:128 * j + 128], NP[:, j, :, :].rearrange("p c h -> p (c h)"), idb[:, :]),
                        [S_[b]["NP"], bfree[bk]] if j == 0 else (), sig=j == 1)
                st_["NP"] = [tr]
                ev = P.put("vector", lambda e, bk=bk: e.tensor_copy(mT, PB[bk][0:48, 0:256]), [tr, st_["mT"]])
                bfree[bk] = [ev]
                S_[b]["mT"] = ev

            def attend(b):
                q, k_ = qs[b % 2], ks[b % 2]
                bo = None
                for g in range(4):
                    pts = []
                    for kind in range(3):
                        bk = rs.take()
                        hs = [4 * g + 2 * kind, 4 * g + 2 * kind + 1] if kind < 2 else [4 * g + i for i in range(4)]
                        w_, kt, q0 = (256, 0, 0) if kind < 2 else (128, 1, 128)
                        for i, h in enumerate(hs):
                            P.put("tensor", lambda e, h=h, i=i, bk=bk, w_=w_, kt=kt, q0=q0: e.matmul(
                                PS[bk][:, w_ * i:w_ * i + w_], k_[:, h // per, 128 * kt:128 * kt + 128], q[:, h, q0:256],
                                start=i == 0, stop=False, skip_group_check=True),
                                [S_[b]["mT"], tE, bfree[bk]] if i == 0 else (), sig=False)
                            P.put("tensor", lambda e, h=h, i=i, bk=bk, w_=w_, q0=q0: e.matmul(
                                PS[bk][:, w_ * i:w_ * i + w_], E[0:48, h, :], mT[:, q0:256],
                                start=False, stop=False, skip_group_check=True), sig=False)
                        ov = PS[bk][:, :].rearrange("p (i n) -> p i n", i=len(hs))
                        mm = P.put("tensor", lambda e, ov=ov, n=len(hs): e.matmul(
                            ov[:, :, 0:128], idb[:, :], bc(maskK[:, :], 1, n), start=False, stop=True,
                            skip_group_check=True))
                        pi = nPT[0] % 4
                        nPT[0] += 1
                        ex = P.put("scalar", lambda e, pi=pi, bk=bk: e.activation(
                            PT[pi], PS[bk][:, :], ACT.Exp, scale=0.25), [mm, st_["PT"][pi], base])
                        bfree[bk] = [ex]
                        pts.append((pi, ex))
                    if g % 2 == 0:
                        bo = ro.take()
                    o0 = 256 * (g % 2)
                    for i in range(4):
                        h = 4 * g + i
                        pi, ex = pts[i // 2]
                        P.put("tensor", lambda e, i=i, h=h, pi=pi, bo=bo, o0=o0: e.matmul(
                            PS[bo][32 * i:32 * i + 32, o0:o0 + 256], Vt[b % 2][0][:, h // per, :],
                            PT[pi][:, 256 * (i % 2):256 * (i % 2) + 256], start=True, stop=False, skip_group_check=True),
                            [ex, S_[b]["V", 0], S_[b]["V", 1], bfree[bo] if g % 2 == 0 else ()], sig=False)
                    pi2, ex2 = pts[2]
                    for i in range(4):
                        h = 4 * g + i
                        pv = P.put("tensor", lambda e, i=i, h=h, pi2=pi2, bo=bo, o0=o0: e.matmul(
                            PS[bo][32 * i:32 * i + 32, o0 + 128:o0 + 256], Vt[b % 2][1][:, h // per, :],
                            PT[pi2][:, 128 * i:128 * i + 128], start=False, stop=True, skip_group_check=True),
                            [ex2], sig=i == 3)
                    for pi, _ in pts:
                        st_["PT"][pi] = [pv]
                    if g % 2 == 1:
                        ev = P.put("vector" if g == 1 else "scalar", (lambda e, bo=bo, g=g: e.tensor_copy(
                            OT[:, g - 1:g + 1, :], PS[bo][:, :].rearrange("p (g n) -> p g n", g=2))) if g == 1 else
                            (lambda e, bo=bo, g=g: e.copy(
                                OT[:, g - 1:g + 1, :], PS[bo][:, :].rearrange("p (g n) -> p g n", g=2))), [pv, st_["OT"]])
                        bfree[bo] = [ev]
                        S_[b]["OT", g] = ev
                st_["qs"][b % 2] = [pv]
                st_["mT"] = [pv]
                st_["V"][b % 2] = [[pv], [pv]]

            def finish(b):
                for j in range(2):
                    t = 2 * b + j
                    bk = rp.take()
                    for g in range(4):
                        tr = P.put("tensor", lambda e, g=g, j=j, bk=bk: e.transpose(
                            PS[bk][:, 128 * g:128 * g + 128], OT[:, g, 128 * j:128 * j + 128], idf[:, :]),
                            [S_[b]["OT", 1], S_[b]["OT", 3], bfree[bk]] if g == 0 else (), sig=g == 3)
                    ov = PS[bk][:, :].rearrange("p (h c) -> p h c", c=32)
                    r = P.put("vector", lambda e, ov=ov: e.reciprocal(rc, ov[:, :, 16]), [tr, st_["rc"]])
                    o = P.put("vector", lambda e, ov=ov: e.tensor_tensor(
                        On.rearrange("p (h d) -> p h d", d=16), ov[:, :, 0:16], bc(rc, 2, 16), ALU.mult),
                        [r, st_["On"]])
                    st_["rc"] = [o]
                    bfree[bk] = [o]
                    if L == 1:
                        xt[t] = P.put("vector", lambda e, t=t: e.tensor_tensor(x[:, t, :], x[:, t, :], On, ALU.add), [o, xt[t]])
                        st_["On"] = [xt[t]]
                        continue
                    bk = rp.take()
                    for k in range(2):
                        tr2 = P.put("tensor", lambda e, k=k, bk=bk: e.transpose(
                            PS[bk][:, 128 * k:128 * k + 128], On[:, 128 * k:128 * k + 128], idf[:, :]),
                            [o, bfree[bk]] if k == 0 else (), sig=k == 1)
                    st_["On"] = [tr2]
                    ev = P.put("scalar", lambda e, bk=bk: e.copy(OnT, PS[bk][:, 0:256].rearrange("p (k n) -> p k n", k=2)),
                               [tr2, st_["OnT"]])
                    bfree[bk] = [ev]
                    bk = rp.take()
                    mo = mms(PS[bk][:, 0:256], [(OnT[:, k, :], wo0[:, k, :]) for k in range(2)], [ev, bfree[bk]])
                    st_["OnT"] = [mo]
                    xa = P.put("gpsimd", lambda e, t=t: e.tensor_tensor(x[:, t, :], x[:, t, :], bo0, ALU.add),
                               [xt[t], P.landed(gb), xnT_wr[t]])
                    xt[t] = P.put("vector", lambda e, t=t, bk=bk: e.tensor_tensor(
                        x[:, t, :], x[:, t, :], PS[bk][:, 0:256], ALU.add), [mo, xa])
                    bfree[bk] = [xt[t]]
                st_["OT"] = [tr]

            project(0)
            transposes(0)
            for b in range(B):
                if b + 1 < B:
                    project(b + 1)
                scores(b)
                if b + 1 < B:
                    transposes(b + 1)
                fold(b)
                attend(b)
                finish(b)
            prev["wk"] = [xt[t] for t in range(T)] + [st_["OT"][0], st_["qs"][1][0]]

        def cross0():
            wof[0] = 0
            base = prev["wk"]
            qT = wk(512).rearrange("p (k n) -> p k n", k=2)
            kT = wk(512).rearrange("p (k n) -> p k n", k=2)
            V = wk(512).rearrange("p (j n) -> p j n", j=2)
            Pm = [wk(320) for _ in range(2)]
            PTn = wk(512).rearrange("p (c n) -> p c n", c=2)
            PTc = wk(256)[0:64, :]
            OTs = wk(512).rearrange("p (m n) -> p m n", m=2)
            sm = wk(16)
            st_ = {k: [] for k in ("qT", "kT", "V", "PTn", "OTs", "sm0", "sm1", "P0", "P1")}
            r1, r2 = Ring([0, 1, 2, 3]), Ring([4, 5, 6, 7])
            wt = P.landed(gxa)
            S_ = [dict() for _ in range(B)]

            def front(b):
                layernorm(b, r1)
                xs = [xnT[:, k, 256 * b:256 * b + 256] for k in range(2)]
                wx = [xnT_wr[2 * b], wt]
                for o, dst, nm in ((0, qT, "qT"), (256, kT, "kT")):
                    bk = r1.take()
                    for mt in range(2):
                        tk = mms(PS[bk][:, 256 * mt:256 * mt + 256],
                                 [(wxa[:, k, o + 128 * mt:o + 128 * mt + 128], xs[k]) for k in range(2)], [wx, bfree[bk]])
                    src = PS[bk][:, :].rearrange("p (k n) -> p k n", k=2)
                    ev = P.put("scalar", lambda e, dst=dst, src=src: e.copy(dst, src), [tk, st_[nm], base])
                    bfree[bk] = [ev]
                    S_[b][nm] = ev
                bk = r1.take()
                for j in range(2):
                    t = 2 * b + j
                    tk = mms(PS[bk][:, 256 * j:256 * j + 256],
                             [(xnT[:, k, 128 * t:128 * t + 128], wxa[:, k, 512:768]) for k in range(2)], [wx, bfree[bk]])
                    xnT_rd[t] = [tk]
                ev = P.put("vector", lambda e, bk=bk: e.tensor_copy(V, PS[bk][:, :].rearrange("p (k n) -> p k n", k=2)),
                           [tk, st_["V"], base])
                bfree[bk] = [ev]
                S_[b]["V"] = ev

            def back(b):
                for j in range(2):
                    bk = r2.take()
                    lq = [qT[:, k, 128 * j:128 * j + 128] for k in range(2)]
                    for k in range(2):
                        P.put("tensor", lambda e, k=k, bk=bk, lq=lq: e.matmul(
                            PS[bk][:, 0:64], lq[k], ctxT[:, k, 64 * b:64 * b + 64], start=k == 0, stop=False,
                            skip_group_check=True), [S_[b]["qT"], S_[b]["kT"], bfree[bk]], sig=False)
                        tk = P.put("tensor", lambda e, k=k, bk=bk, lq=lq: e.matmul(
                            PS[bk][:, 64:320], lq[k], kT[:, k, :], start=False, stop=k == 1,
                            skip_group_check=True), sig=k == 1)
                    o = 8 * j
                    mx = P.put("vector", lambda e, bk=bk, o=o: e.tensor_reduce(sm[:, o:o + 1], PS[bk][:, 0:320], AX, ALU.max),
                               [tk, st_[f"sm{j}"], base])
                    nb = P.put("vector", lambda e, o=o: e.tensor_scalar(sm[:, o + 1:o + 2], sm[:, o:o + 1], -0.0625, None, ALU.mult), [mx])
                    ex = P.put("scalar", lambda e, bk=bk, o=o, j=j: e.activation(
                        Pm[j], PS[bk][:, 0:320], ACT.Exp, bias=sm[:, o + 1:o + 2], scale=0.0625,
                        accum_out=sm[:, o + 2:o + 3]), [nb, st_[f"P{j}"]])
                    bfree[bk] = [ex, mx]
                    S_[b]["rc", j] = P.put("vector", lambda e, o=o: e.reciprocal(sm[:, o + 3:o + 4], sm[:, o + 2:o + 3]), [ex])
                    S_[b]["P", j] = ex
                st_["qT"] = st_["kT"] = [tk]
                bn, bc_ = r2.take(), r2.take()
                for j in range(2):
                    P.put("tensor", lambda e, j=j: e.transpose(
                        PS[bc_][0:64, 128 * j:128 * j + 128], Pm[j][:, 0:64], idf[:, :]),
                        [S_[b]["P", j], bfree[bc_]], sig=False)
                    for c in range(2):
                        tr = P.put("tensor", lambda e, j=j, c=c: e.transpose(
                            PS[bn][:, 256 * c + 128 * j:256 * c + 128 * j + 128], Pm[j][:, 64 + 128 * c:192 + 128 * c], idf[:, :]),
                            [bfree[bn]], sig=c == 1)
                    st_[f"P{j}"] = [tr]
                e1 = P.put("scalar", lambda e: e.copy(PTn, PS[bn][:, :].rearrange("p (c n) -> p c n", c=2)), [tr, st_["PTn"], base])
                e2 = P.put("vector", lambda e: e.tensor_copy(PTc, PS[bc_][0:64, 0:256]), [tr, st_["PTn"], base])
                bfree[bn], bfree[bc_] = [e1], [e2]
                bk = r2.take()
                for mt in range(2):
                    ms = slice(128 * mt, 128 * mt + 128)
                    tk = mms(PS[bk][:, 256 * mt:256 * mt + 256],
                             [(ctxN[0:64, b, ms], PTc), (V[:, 0, ms], PTn[:, 0, :]), (V[:, 1, ms], PTn[:, 1, :])],
                             [e1, e2, S_[b]["V"], bfree[bk]])
                st_["V"] = st_["PTn"] = [tk]
                ev = P.put("scalar", lambda e, bk=bk: e.copy(OTs, PS[bk][:, :].rearrange("p (k n) -> p k n", k=2)),
                           [tk, st_["OTs"], base])
                bfree[bk] = [ev]
                bk = r2.take()
                for j in range(2):
                    tk = mms(PS[bk][:, 256 * j:256 * j + 256],
                             [(OTs[:, mt, 128 * j:128 * j + 128], wxa[:, mt, 768:1024]) for mt in range(2)], [ev, bfree[bk]])
                st_["OTs"] = [tk]
                for j in range(2):
                    t = 2 * b + j
                    xt[t] = P.put("vector", lambda e, j=j, t=t, bk=bk: e.scalar_tensor_tensor(
                        out=x[:, t, :], in0=PS[bk][:, 256 * j:256 * j + 256], scalar=sm[:, 8 * j + 3:8 * j + 4],
                        in1=x[:, t, :], op0=ALU.mult, op1=ALU.add), [tk, S_[b]["rc", j], xt[t], xnT_wr[t]])
                    st_[f"sm{j}"] = [xt[t]]
                bfree[bk] = [xt[2 * b], xt[2 * b + 1]]

            for b in range(B):
                front(b)
                back(b)
            prev["wk"] = [xt[t] for t in range(T)] + [st_["OTs"][0]]

        def gates(NE, TOPK, wr, wtok, G, tmp, ring, factor):
            Lg, Rp, v8, rep, s1 = tmp
            base = prev["wk"]
            z = P.put("vector", lambda e: e.memset(rep, BIG), base)
            bk = ring.take()
            for t in range(T):
                tk = mms(PS[bk][:, NE * t:NE * t + NE],
                         [(xnT[:, k, 128 * t:128 * t + 128], wr[:, k, :]) for k in range(2)],
                         [xnT_wr[t], wtok, bfree[bk]], start=True)
            a = P.put("vector", lambda e: e.tensor_copy(Lg.rearrange("p t e -> p (t e)"), PS[bk][:, 0:T * NE]), [tk, base])
            bfree[bk] = [a]
            for t in range(T):
                m8 = P.put("vector", lambda e, t=t: e.max(v8[:, t, :], Lg[:, t, :]), [a])
            c = P.put("vector", lambda e: e.tensor_copy(rep[:, :, 0:TOPK], v8[:, :, 0:TOPK]), [m8, z])
            for t in range(T):
                mr_ = P.put("vector", lambda e, t=t: e.match_replace(
                    out=Rp[:, t, :], in_to_replace=rep[:, t, :], in_values=Lg[:, t, :], imm_value=-BIG), [c])
            se = P.put("vector", lambda e: e.tensor_tensor(Rp, Rp, Lg, ALU.not_equal), [mr_])
            su = P.put("vector", lambda e: e.tensor_tensor(Lg, Lg, v8[:, :, 0:1].to_broadcast([128, T, NE]), ALU.subtract), [se])
            ex = P.put("scalar", lambda e: e.activation(Lg, Lg, ACT.Exp), [su])
            mu = P.put("vector", lambda e: e.tensor_tensor(G, Lg, Rp, ALU.mult), [ex])
            sm_ = P.put("vector", lambda e: e.tensor_reduce(s1[:, 0, :], G, AX, ALU.add), [mu])
            rc_ = P.put("vector", lambda e: e.reciprocal(s1[:, 1, :], s1[:, 0, :]), [sm_])
            return P.put("vector", lambda e: e.scalar_tensor_tensor(
                out=G, in0=G, scalar=factor, in1=bc(s1[:, 1, :], 2, NE), op0=ALU.mult, op1=ALU.mult), [rc_])

        def experts(L):
            wof[0] = 0
            NE, TOPK = (8, 2) if L == 0 else (16, 4)
            NC = 4 if L == 0 else 1
            gm = P.landed(gm0 if L == 0 else gm1)
            base = prev["wk"]
            G = wk(T * NE).rearrange("p (t e) -> p t e", e=NE)
            tmp = (wk(T * NE).rearrange("p (t e) -> p t e", e=NE), wk(T * NE).rearrange("p (t e) -> p t e", e=NE),
                   wk(T * 8).rearrange("p (t e) -> p t e", e=8), wk(T * 8).rearrange("p (t e) -> p t e", e=8),
                   wk(2 * T).rearrange("p (a t) -> p a t", a=2))
            sil = [wk(512) for _ in range(2)]
            U = [[wk(512) for _ in range(4)] for _ in range(2)]
            f_s, f_U = [[], []], [[], []]
            rh, ro_, rl = Ring([0, 1, 2, 3]), Ring([4, 5, 6]), Ring([7])
            for b in range(B):
                layernorm(b, rl)
            tg = gates(NE, TOPK, wr0 if L == 0 else wr1, gm, G, tmp, rl, 1.0 if L == 0 else 0.8)
            if L == 0:
                for t in range(T):
                    xt[t] = P.put("gpsimd", lambda e, t=t: e.tensor_tensor(x[:, t, :], x[:, t, :], bm0, ALU.add),
                                  [xt[t], gm, xnT_wr[t]])
            nu, ns = [0], [0]
            jobs = [("e", e_, NC) for e_ in range(NE)] + ([("s", 0, 4)] if L == 1 else [])

            def hidden(blk, job):
                kind, e_, nch = job
                u = nu[0] % 2
                nu[0] += 1
                toks = []
                for c in range(nch):
                    if L == 0:
                        wa = [win0[:, k, 1024 * e_ + 128 * c:1024 * e_ + 128 * c + 128] for k in range(2)]
                        wb = [win0[:, k, 1024 * e_ + 512 + 128 * c:1024 * e_ + 512 + 128 * c + 128] for k in range(2)]
                    elif kind == "e":
                        wa = [we1[:, k, 128 * e_:128 * e_ + 128] for k in range(2)]
                        wb = [we3[:, k, 128 * e_:128 * e_ + 128] for k in range(2)]
                    else:
                        wa = [ws13[:, k, 128 * c:128 * c + 128] for k in range(2)]
                        wb = [ws13[:, k, 512 + 128 * c:512 + 128 * c + 128] for k in range(2)]
                    ba, bb = rh.take(), rh.take()
                    xs = [xnT[:, k, 512 * blk:512 * blk + 512] for k in range(2)]
                    dep = [xnT_wr[4 * blk], xnT_wr[4 * blk + 2], gm]
                    ta = mms(PS[ba][:, :], list(zip(wa, xs)), [dep, bfree[ba]])
                    tb = mms(PS[bb][:, :], list(zip(wb, xs)), [bfree[bb]])
                    si = ns[0] % 2
                    ns[0] += 1
                    s_ = P.put("scalar", lambda e, si=si, ba=ba: e.activation(sil[si], PS[ba][:, :], ACT.Silu), [ta, f_s[si], base])
                    m_ = P.put("vector", lambda e, si=si, bb=bb, u=u, c=c: e.tensor_tensor(U[u][c], sil[si], PS[bb][:, :], ALU.mult),
                               [s_, tb, f_U[u], base])
                    bfree[ba], bfree[bb] = [s_], [m_]
                    f_s[si] = [m_]
                    toks.append(m_)
                for t in range(4 * blk, 4 * blk + 4):
                    xnT_rd[t] = [tb]
                return u, toks

            def down(blk, job, u, toks):
                kind, e_, nch = job
                for tl in range(4):
                    t = 4 * blk + tl
                    if L == 0:
                        ws = [wout0[:, 4 * e_ + c, :] for c in range(4)]
                    elif kind == "e":
                        ws = [we2[:, e_, :]]
                    else:
                        ws = [ws2[:, c, :] for c in range(4)]
                    bk = ro_.take()
                    tk = mms(PS[bk][:, 0:256], [(U[u][c][:, 128 * tl:128 * tl + 128], ws[c]) for c in range(nch)],
                             [toks, bfree[bk]])
                    sc = G[:, t, e_:e_ + 1] if kind == "e" else 0.2
                    xt[t] = P.put("vector", lambda e, t=t, bk=bk, sc=sc: e.scalar_tensor_tensor(
                        out=x[:, t, :], in0=PS[bk][:, 0:256], scalar=sc, in1=x[:, t, :], op0=ALU.mult, op1=ALU.add),
                        [tk, tg, xt[t], xnT_wr[t]])
                    bfree[bk] = [xt[t]]
                f_U[u] = [tk]

            pend = None
            for blk in range(4):
                for job in jobs:
                    u, toks = hidden(blk, job)
                    if pend:
                        down(*pend)
                    pend = (blk, job, u, toks)
            down(*pend)
            prev["wk"] = [xt[t] for t in range(T)] + f_U[0] + f_U[1]
            return f_U[0] + f_U[1]

        def cross1():
            wof[0] = 0
            base = prev["wk"]
            gt = P.landed(gx1)
            kM = kMt
            kv = wk(512)
            am = wk(16)
            sk = wk(16)
            rk = wk(16)
            K3 = wk(512, BF).rearrange("p (h c) -> p h c", c=64)
            vT = wk(1024).rearrange("p (m n) -> p m n", m=2)
            sv = wk(4)
            vq = wk(512, BF).rearrange("p (m n) -> p m n", m=2)
            Vq = wk(512, BF).rearrange("p (c n) -> p c n", c=4)
            qf = wk(256)
            Q3 = wk(512, BF).rearrange("p (h c) -> p h c", c=64)
            q3T = [wk(512, BF).rearrange("p (g n) -> p g n", g=8) for _ in range(2)]
            sq = [wk(16) for _ in range(2)]
            rq = wk(16)
            mm_ = wk(16)
            nb = wk(16)
            se = [wk(16) for _ in range(2)]
            rs_ = wk(16)
            ee = [wk(512) for _ in range(3)]
            ei = [wk(256, BF) for _ in range(3)]
            aT = [wk(512, BF) for _ in range(2)]
            On = wk(256)
            OnT = wk(256).rearrange("p (k n) -> p k n", k=2)
            r1, r2, r3 = Ring([0, 1]), Ring([2, 3, 4]), Ring([5, 6])
            bO = 7

            zk = P.put("gpsimd", lambda e: e.memset(kM[:, :, :], 0.0), base)
            z3 = P.put("vector", lambda e: e.memset(K3, 0.0), base)
            zq = P.put("vector", lambda e: e.memset(Q3, 0.0), base)

            def quant(src, n, s, r, dst, after, rd_dst):
                a = P.put("vector", lambda e: e.tensor_reduce(am, src.rearrange("p (h d) -> p h d", d=16), AX, ALU.max,
                                                              apply_absolute_value=True), after)
                a = P.put("vector", lambda e: e.tensor_scalar(s, am, 1.0 / 127.0, 1e-8, ALU.mult, ALU.max), [a])
                a = P.put("vector", lambda e: e.reciprocal(r, s), [a])
                a2 = P.put("vector", lambda e: e.tensor_tensor(src.rearrange("p (h d) -> p h d", d=16),
                                                               src.rearrange("p (h d) -> p h d", d=16), bc(r, 2, 16), ALU.mult), [a])
                a3 = P.put("vector", lambda e: e.tensor_scalar(src, src, MAGIC, MAGIC, ALU.add, ALU.subtract), [a2])
                return P.put("vector", lambda e: e.tensor_scalar(dst, src, 127.0, -127.0, ALU.min, ALU.max), [a3] + rd_dst)

            bv = [r3.take(), r3.take()]
            fK3, fkv, kMw = [z3], [], []
            for c in range(4):
                bk = r1.take()
                tk = mms(PS[bk][:, :], [(ctxT[:, k, 128 * c:128 * c + 128], wkv[:, k, :]) for k in range(2)],
                         [gt, P.landed(gxa), bfree[bk]])
                a = P.put("vector", lambda e, bk=bk: e.tensor_tensor(kv, PS[bk][:, :], bkv, ALU.add), [tk, fkv, base])
                bfree[bk] = [a]
                for m_ in range(2):
                    tv = P.put("tensor", lambda e, m_=m_, c=c: e.transpose(
                        PS[bv[m_]][:, 128 * c:128 * c + 128], kv[:, 256 + 128 * m_:384 + 128 * m_], idf[:, :]),
                        [a, bfree[bv[m_]]])
                kk = kv[:, 0:256]
                a = quant(kk, 16, sk, rk, kk, [a], [])
                k3 = kk.rearrange("p (h d) -> p h d", d=16)
                a = P.put("vector", lambda e: e.tensor_tensor(k3, k3, bc(sk, 2, 16), ALU.mult), [a])
                a = P.put("vector", lambda e: e.tensor_copy(K3[:, :, 0:16], k3), [a] + fK3)
                a = P.put("vector", lambda e: e.tensor_tensor(k3, k3, K3[:, :, 0:16], ALU.subtract), [a])
                a = P.put("vector", lambda e: e.tensor_copy(K3[:, :, 16:32], k3), [a])
                a = P.put("vector", lambda e: e.tensor_tensor(K3[:, :, 32:48], k3, K3[:, :, 16:32], ALU.subtract), [a])
                fkv = [a, tv]
                bk = r1.take()
                for g in range(8):
                    tr = P.put("tensor", lambda e, g=g, bk=bk: e.transpose(
                        PB[bk][:, 128 * g:128 * g + 128], K3[:, 2 * g:2 * g + 2, :].rearrange("p h c -> p (h c)"), idb[:, :]),
                        [a, bfree[bk]] if g == 0 else (), sig=g == 7)
                fK3 = [tr]
                evs = []
                for o in range(2):
                    evs.append(P.put("vector", lambda e, o=o, bk=bk, c=c: e.tensor_copy(
                        kM[64 * o:64 * o + 64, o::2, 128 * c:128 * c + 128],
                        PB[bk][64 * o:64 * o + 64, :].rearrange("p (g n) -> p g n", g=8)), [tr, zk]))
                bfree[bk] = evs
                kMw += evs
            for m_ in range(2):
                a = P.put("vector", lambda e, m_=m_: e.tensor_copy(vT[:, m_, :], PS[bv[m_]][:, :]), [tv, base])
                bfree[bv[m_]] = [a]
            a = P.put("vector", lambda e: e.tensor_reduce(sv[:, 0:2], vT, AX, ALU.max, apply_absolute_value=True), [a])
            a = P.put("vector", lambda e: e.tensor_scalar(sv[:, 0:2], sv[:, 0:2], 1.0 / 127.0, 1e-8, ALU.mult, ALU.max), [a])
            tsv = P.put("vector", lambda e: e.reciprocal(sv[:, 2:4], sv[:, 0:2]), [a])
            for m_ in range(2):
                a = P.put("vector", lambda e, m_=m_: e.tensor_scalar(vT[:, m_, :], vT[:, m_, :], sv[:, 2 + m_:3 + m_], None, ALU.mult), [tsv])
            a = P.put("vector", lambda e: e.tensor_scalar(vT, vT, MAGIC, MAGIC, ALU.add, ALU.subtract), [a])
            a = P.put("vector", lambda e: e.tensor_scalar(vq, vT, 127.0, -127.0, ALU.min, ALU.max), [a, base])
            bk = r1.take()
            for c in range(4):
                for m_ in range(2):
                    tr = P.put("tensor", lambda e, m_=m_, c=c, bk=bk: e.transpose(
                        PB[bk][:, 256 * c + 128 * m_:256 * c + 128 * m_ + 128], vq[:, m_, 128 * c:128 * c + 128], idb[:, :]),
                        [a, bfree[bk]])
            tV = P.put("vector", lambda e, bk=bk: e.tensor_copy(Vq, PB[bk].rearrange("p (c n) -> p c n", c=4)), [tr, base])
            bfree[bk] = [tV]

            fq = {"qf": [], "Q3": [zq], "q3T": [[], []], "sq": [[], []], "m": [], "se": [[], []], "ee": [[], [], []],
                  "ei": [[], [], []], "aT": [[], []], "On": [], "OnT": [], "rs": []}
            n_e = [0]
            n_a = [0]
            S_ = [dict() for _ in range(T)]

            def queries(t):
                if t % 2 == 0:
                    layernorm(t // 2, r1)
                bk = r1.take()
                tk = mms(PS[bk][:, 0:256], [(xnT[:, k, 128 * t:128 * t + 128], wq1[:, k, :]) for k in range(2)],
                         [xnT_wr[t], gt, bfree[bk]])
                xnT_rd[t] = [tk]
                a = P.put("vector", lambda e, bk=bk: e.tensor_tensor(qf, PS[bk][:, 0:256], bq1, ALU.add), [tk, fq["qf"], base])
                bfree[bk] = [a]
                a = P.put("vector", lambda e: e.tensor_scalar(qf, qf, 0.25, None, ALU.mult), [a])
                qd = bc(qf.rearrange("p (h d) -> p h d", d=16), 2, 3)
                s_ = sq[t % 2]
                dst = Q3[:, :, 0:48].rearrange("p h (c d) -> p h c d", d=16)
                a = P.put("vector", lambda e: e.tensor_reduce(am, qf.rearrange("p (h d) -> p h d", d=16), AX, ALU.max,
                                                              apply_absolute_value=True), [a])
                a = P.put("vector", lambda e: e.tensor_scalar(s_, am, 1.0 / 127.0, 1e-8, ALU.mult, ALU.max), [a, fq["sq"][t % 2], base])
                a = P.put("vector", lambda e: e.reciprocal(rq, s_), [a])
                q3 = qf.rearrange("p (h d) -> p h d", d=16)
                a = P.put("vector", lambda e: e.tensor_tensor(q3, q3, bc(rq, 2, 16), ALU.mult), [a])
                a = P.put("vector", lambda e: e.tensor_scalar(qf, qf, MAGIC, MAGIC, ALU.add, ALU.subtract), [a])
                a = P.put("vector", lambda e: e.tensor_scalar(dst, qd, 127.0, -127.0, ALU.min, ALU.max), [a, fq["Q3"]])
                fq["qf"] = [a]
                bk = r1.take()
                for g in range(8):
                    tr = P.put("tensor", lambda e, g=g, bk=bk: e.transpose(
                        PB[bk][:, 128 * g:128 * g + 128], Q3[:, 2 * g:2 * g + 2, :].rearrange("p h c -> p (h c)"), idb[:, :]),
                        [a, bfree[bk]] if g == 0 else (), sig=g == 7)
                fq["Q3"] = [tr]
                ev = P.put("scalar", lambda e, bk=bk, t=t: e.copy(q3T[t % 2], PB[bk].rearrange("p (g n) -> p g n", g=8)),
                           [tr, fq["q3T"][t % 2], base])
                bfree[bk] = [ev]
                S_[t]["q"] = ev

            units = [(t, h) for t in range(T) for h in range(H)]
            U_ = {}

            def u_scores(t, h):
                bk = r2.take()
                tk = P.put("tensor", lambda e: e.matmul(PS[bk][:, :], q3T[t % 2][:, h // 2, :], kM[:, h, :], start=True, stop=True),
                           [S_[t]["q"], kMw, zk, bfree[bk]])
                if h == H - 1:
                    fq["q3T"][t % 2] = [tk]
                mx = P.put("vector", lambda e: e.tensor_reduce(mm_[:, h:h + 1], PS[bk][:, :], AX, ALU.max),
                           [tk, fq["m"][h] if fq["m"] else (), base])
                U_[t, h] = [bk, mx]

            def u_exp(t, h):
                bk, mx = U_[t, h]
                i = n_e[0] % 3
                n_e[0] += 1
                a = P.put("vector", lambda e: e.scalar_tensor_tensor(
                    out=nb[:, h:h + 1], in0=mm_[:, h:h + 1], scalar=-1.0, in1=sq[t % 2][:, h:h + 1], op0=ALU.mult, op1=ALU.mult),
                    [mx, fq["nb"][h] if "nb" in fq else ()])
                a = P.put("vector", lambda e: e.tensor_scalar(nb[:, h:h + 1], nb[:, h:h + 1], LN255, None, ALU.add), [a])
                fm = fq.setdefault("mlist", {})
                fm[h] = [a]
                fq["m"] = [fm.get(i_, []) for i_ in range(H)]
                ex = P.put("scalar", lambda e: e.activation(
                    ee[i], PS[bk][:, :], ACT.Exp, bias=nb[:, h:h + 1], scale=sq[t % 2][:, h:h + 1],
                    accum_out=se[t % 2][:, h:h + 1]), [a, fq["ee"][i], fq["se"][t % 2]])
                fn = fq.setdefault("nlist", {})
                fn[h] = [ex]
                fq["nb"] = [fn.get(i_, []) for i_ in range(H)]
                bfree[bk] = [ex, mx]
                if h == H - 1:
                    fq["sq"][t % 2] = [ex]
                ro2 = P.put("vector", lambda e: e.tensor_scalar(ei[i], ee[i], MAGIC, MAGIC, ALU.add, ALU.subtract), [ex, fq["ei"][i]])
                fq["ee"][i] = [ro2]
                U_[t, h] = [i, ro2, ex]

            def u_tr(t, h):
                if h % 2 == 0:
                    U_["bank"] = r3.take()
                bk = U_["bank"]
                i, ro2, ex = U_[t, h]
                for c in range(4):
                    tr = P.put("tensor", lambda e, c=c: e.transpose(
                        PB[bk][:, 512 * (h % 2) + 128 * c:512 * (h % 2) + 128 * c + 128], ei[i][:, 128 * c:128 * c + 128], idb[:, :]),
                        [ro2, bfree[bk] if h % 2 == 0 else ()], sig=c == 3)
                fq["ei"][i] = [tr]
                if h % 2 == 1:
                    i2 = n_a[0] % 2
                    n_a[0] += 1
                    if (h // 2) % 4 == 3:
                        ev = P.put("vector", lambda e: e.tensor_copy(aT[i2], PB[bk]), [tr, fq["aT"][i2]])
                    else:
                        ev = P.put("scalar", lambda e: e.copy(aT[i2], PB[bk]), [tr, fq["aT"][i2]])
                    bfree[bk] = [ev]
                    U_["a", t, h // 2] = (i2, ev)

            def u_pv(t, hp):
                i2, ev = U_["a", t, hp]
                for h in (2 * hp, 2 * hp + 1):
                    for c in range(4):
                        pv = P.put("tensor", lambda e, h=h, c=c: e.matmul(
                            PS[bO][:, 16 * h:16 * h + 16], aT[i2][:, 512 * (h % 2) + 128 * c:512 * (h % 2) + 128 * c + 128],
                            Vq[:, c, 16 * h:16 * h + 16], start=h == 0 and c == 0, stop=c == 3, skip_group_check=True),
                            [ev, tV, bfree[bO] if h == 0 else ()], sig=c == 3 and h % 2 == 1)
                fq["aT"][i2] = [pv]
                if hp == 7:
                    done(t, pv)

            def done(t, pv):
                ex = U_[t, H - 1][2]
                r = P.put("vector", lambda e: e.reciprocal(rs_, se[t % 2]), [ex, fq["rs"]])
                fq["se"][t % 2] = [r]
                o = P.put("vector", lambda e: e.tensor_tensor(
                    On.rearrange("p (h d) -> p h d", d=16), PS[bO][:, 0:256].rearrange("p (h d) -> p h d", d=16),
                    bc(rs_, 2, 16), ALU.mult), [r, pv, fq["On"]])
                fq["rs"] = [o]
                bfree[bO] = [o]
                bk = r1.take()
                for k in range(2):
                    tr = P.put("tensor", lambda e, k=k: e.transpose(
                        PS[bk][:, 128 * k:128 * k + 128], On[:, 128 * k:128 * k + 128], idf[:, :]),
                        [o, bfree[bk]] if k == 0 else (), sig=k == 1)
                fq["On"] = [tr]
                for k in range(2):
                    ev = P.put("vector", lambda e, k=k: e.tensor_scalar(
                        OnT[:, k, :], PS[bk][:, 128 * k:128 * k + 128], sv[:, k:k + 1], None, ALU.mult), [tr, fq["OnT"]])
                bfree[bk] = [ev]
                bk2 = r1.take()
                mo = mms(PS[bk2][:, 0:256], [(OnT[:, k, :], wp1[:, k, :]) for k in range(2)], [ev, bfree[bk2]])
                fq["OnT"] = [mo]
                xa = P.put("gpsimd", lambda e: e.tensor_tensor(x[:, t, :], x[:, t, :], bp1, ALU.add), [xt[t], gt, xnT_wr[t]])
                xt[t] = P.put("vector", lambda e: e.tensor_tensor(x[:, t, :], x[:, t, :], PS[bk2][:, 0:256], ALU.add), [mo, xa])
                bfree[bk2] = [xt[t]]

            queries(0)
            N = len(units)
            for i in range(N + 4):
                if i < N:
                    t, h = units[i]
                    if h == 6 and t + 1 < T:
                        queries(t + 1)
                    u_scores(t, h)
                if 1 <= i <= N:
                    pend_exp = units[i - 1]
                    u_exp(*pend_exp)
                if 2 <= i <= N + 1:
                    u_tr(*units[i - 2])
                if i >= 4 and units[i - 4][1] % 2 == 1:
                    u_pv(units[i - 4][0], units[i - 4][1] // 2)
            prev["wk"] = [xt[t] for t in range(T)] + fq["q3T"][0] + fq["q3T"][1] + fq["OnT"]

        def out_all():
            go = P.group("out")
            od = out.rearrange("(t p) d -> p t d", p=128)
            for t in range(T):
                P.dma("sync", go, od[:, t, :], x[:, t, :], [xt[t]])
            P.wait("sync", [P.landed(go)])

        attn_phase(0)
        P.dma("sync", gm0, win0[:, 1, 4096:8192], win_d[:, 1, 4096:8192], [prev["wk"]])
        P.dma("sync", gm0, wout0, I["w_out0"].rearrange("(c p) n -> p c n", p=128))
        if upto >= 2:
            cross0()
        if upto >= 3:
            fU = experts(0)
            gm1 = P.group("m1")
            we1 = W[:, 0:4096].rearrange("p (k n) -> p k n", k=2)
            we3 = W[:, 4096:8192].rearrange("p (k n) -> p k n", k=2)
            we2 = W[:, 8192:12288].rearrange("p (c n) -> p c n", c=16)
            ws13 = W[:, 12288:14336].rearrange("p (k n) -> p k n", k=2)
            ws2 = W[:, 14336:15360].rearrange("p (c n) -> p c n", c=4)
            wr1 = W[:, 15360:15392].rearrange("p (k n) -> p k n", k=2)
            kMt = W[:, 19616:23712].bitcast(BF).rearrange("p (h n) -> p h n", h=H)
            P.dma("sync", gm1, we1, I["we1"].rearrange("(k p) n -> p k n", p=128), fU)
            P.dma("sync", gm1, we3, I["we3"].rearrange("(k p) n -> p k n", p=128))
            P.dma("sync", gm1, we2, I["we2"].rearrange("(c p) n -> p c n", p=128))
            P.dma("sync", gm1, ws13, I["ws13"].rearrange("(k p) n -> p k n", p=128))
            P.dma("sync", gm1, ws2, I["ws2"].rearrange("(c p) n -> p c n", p=128))
            P.dma("sync", gm1, wr1, I["w_r1"].rearrange("(k p) n -> p k n", p=128))
            o = 15392
            wq1 = W[:, o:o + 512].rearrange("p (k n) -> p k n", k=2)
            wkv = W[:, o + 512:o + 1536].rearrange("p (k n) -> p k n", k=2)
            wp1 = W[:, o + 1536:o + 2048].rearrange("p (k n) -> p k n", k=2)
            bq1, bkv, bp1 = W[:, o + 2048:o + 2304], W[:, o + 2304:o + 2816], W[:, o + 2816:o + 3072]
            P.dma("sync", gat1, wA[1], I["w_att1"].rearrange("(k p) n -> p k n", p=128))
            P.dma("sync", gat1, bA[1], bcast(I["b_att1"]))
            P.dma("sync", gx1, wq1, I["w_q1"].rearrange("(k p) n -> p k n", p=128))
            P.dma("sync", gx1, wkv, I["w_kv1"].rearrange("(k p) n -> p k n", p=128))
            P.dma("sync", gx1, wp1, I["w_p1"].rearrange("(k p) n -> p k n", p=128))
            for v, n in ((bq1, "b_q1"), (bkv, "b_kv1"), (bp1, "b_p1")):
                P.dma("sync", gx1, v, bcast(I[n]))
        if upto >= 4:
            attn_phase(1)
        if upto >= 5:
            cross1()
        if upto >= 6:
            experts(1)
        out_all()
        for g in P.groups:
            if g[2]:
                P.wait("sync", [P.landed(g)])
        P.emit()


def constants():
    i = np.arange(128)
    sq = np.zeros((128, 384), np.float32)
    sq[:, 0:128] = np.eye(128)
    sq[:, 128:256] = np.where(i[None, :] > i[:, None], -1e30, 0.0)
    sq[:, 256:384] = np.where(i[:, None] > i[None, :], -1e30, 0.0)
    E = np.zeros((48, H, 128), np.float32)
    for h in range(H):
        for c in range(3):
            E[16 * c + h, h, :] = 1.0

    def part(v):
        out, r = [], v.astype(np.float32)
        for _ in range(3):
            b = r.view(np.uint32)
            b = ((b + 0x7FFF + ((b >> 16) & 1)) & 0xFFFF0000).astype(np.uint32).view(np.float32)
            out.append(b)
            r = (r - b).astype(np.float32)
        return out

    start = 2.0 ** (-8.0 / H)
    slopes = np.array([start * start ** h for h in range(H)], np.float32) * np.float32(4)
    ali = np.zeros((128, 2, 2, H, 32), np.float32)
    for j in range(2):
        pos = (128 * j + i).astype(np.float32)
        for c in range(3):
            ali[:, 0, j, :, c] = 1.0
            ali[:, 0, j, :, 3 + c] = pos[:, None]
            ali[:, 1, j, :, c] = part(slopes[None, :] * pos[:, None])[c]
            ali[:, 1, j, :, 3 + c] = -part(slopes)[c][None, :]
    return {"c_sq": sq, "c_E": E.reshape(48, H * 128), "c_ali": ali.reshape(128, 2048)}


_OUT = ((2048, 256), "float32")


def layout(inp):
    c = np.ascontiguousarray
    cat = np.concatenate
    a = {k: np.asarray(v) for k, v in inp.items()}
    m = {"x": c(a["x"].reshape(2048, 256))}
    m["w_att0"] = cat([a["L0_attn_wq"], a["L0_attn_wk"], a["L0_attn_wv"]], 1)
    m["b_att0"] = cat([a["L0_attn_bq"], a["L0_attn_bk"], a["L0_attn_bv"]])
    m["w_o0"], m["b_o0"] = a["L0_attn_wo"], a["L0_attn_bo"]
    m["w_xa0"] = cat([a[f"L0_xattn_{n}"].T for n in ("wq", "wk", "wv", "wo")], 1)
    ctx = a["ctx_2048"]
    m["ctxT"] = c(ctx.reshape(512, 256).T)
    m["ctxN"] = c(ctx.transpose(1, 0, 2))
    m["w_in0"] = c(a["L0_ffn_w_in"].transpose(2, 0, 1).reshape(256, 8192))
    m["w_out0"] = c(a["L0_ffn_w_out"].transpose(0, 2, 1).reshape(4096, 256))
    m["w_r0"] = c(a["L0_ffn_router_weight"].T)
    m["b_m0"] = a["L0_ffn_bias"]
    flat = lambda w: w.transpose(1, 0, 2).reshape(256, -1)
    m["w_att1"] = cat([flat(a[f"L1_attn_W{n}"]) for n in "qkv"], 1)
    m["b_att1"] = cat([a[f"L1_attn_b{n}"].reshape(-1) for n in "qkv"])
    m["w_q1"], m["w_kv1"], m["w_p1"] = a["L1_xattn_Wq"], a["L1_xattn_Wkv"], a["L1_xattn_Wp"]
    m["b_q1"], m["b_kv1"], m["b_p1"] = a["L1_xattn_bq"], a["L1_xattn_bkv"], a["L1_xattn_bp"]
    m["we1"], m["we3"] = c(flat(a["L1_ffn_we1"])), c(flat(a["L1_ffn_we3"]))
    m["we2"] = a["L1_ffn_we2"].reshape(2048, 256)
    m["ws13"] = cat([a["L1_ffn_ws1"], a["L1_ffn_ws3"]], 1)
    m["ws2"] = a["L1_ffn_ws2"]
    m["w_r1"] = a["L1_ffn_w_router"]
    m.update(constants())
    return {k: c(v) for k, v in m.items()}


def kernel(**inputs):
    import concourse.bacc as _bacc
    from concourse.bass_utils import run_bass_kernel_spmd as _run

    nc = _bacc.Bacc("TRN2", target_bir_lowering=False, num_devices=1)
    arrays = layout(inputs)
    I = {k: nc.dram_tensor(f"in_{k}", v.shape, mybir.dt.from_np(v.dtype), kind="ExternalInput").ap()
         for k, v in arrays.items()}
    out = nc.dram_tensor("out_0", _OUT[0], F32, kind="ExternalOutput").ap()
    decoder(nc, I, out)
    r = _run(nc, [{f"in_{k}": v for k, v in arrays.items()}], core_ids=[0])
    return r.results[0]["out_0"].reshape(8, 256, 256)
```

```python
from contextlib import ExitStack

import numpy as np

import concourse.bass as bass
from concourse import mybir

F32 = mybir.dt.float32
BF = mybir.dt.bfloat16
ALU = mybir.AluOpType
ACT = mybir.ActivationFunctionType
AX = mybir.AxisListType.X
MAGIC = 12582912.0
BIG = 3.0e38
LN255 = float(np.log(255.0))

B, S, D, H, T = 8, 256, 256, 16, 16
POS = ((0, 3, 5), (1, 4), (2,))


class Prog:

    ENG = ("tensor", "vector", "scalar", "gpsimd", "sync")

    def __init__(self, nc, ctx):
        self.nc, self.ctx = nc, ctx
        self.q = {e: [] for e in self.ENG}
        self.sem = {e: ctx.enter_context(nc.semaphore("s_" + e)) for e in self.ENG}
        self.count = {e: 0 for e in self.ENG}
        self.seen = {e: {} for e in self.ENG}
        self.groups = []

    def wait(self, e, after):
        for t in after:
            if not t:
                continue
            if type(t) is list:
                self.wait(e, t)
                continue
            name, s, v = t
            if self.seen[e].get(name, 0) < v:
                self.seen[e][name] = v
                self.q[e].append(lambda eng, s=s, v=v: eng.wait_ge(s, v))

    def put(self, e, fn, after=(), sig=True):
        self.wait(e, after)
        if not sig:
            self.q[e].append(fn)
            return None
        self.count[e] += 1
        s = self.sem[e]
        self.q[e].append(lambda eng: fn(eng).then_inc(s, 1))
        return (e, s, self.count[e])

    def group(self, name):
        g = [name, self.ctx.enter_context(self.nc.semaphore("d_" + name)), 0]
        self.groups.append(g)
        return g

    def dma(self, e, g, out, in_, after=()):
        self.wait(e, after)
        g[2] += 16
        s = g[1]
        self.q[e].append(lambda eng: eng.dma_start(out, in_).then_inc(s, 16))

    def landed(self, g):
        return (g[0], g[1], g[2])

    def emit(self):
        with self.nc.Block() as block:
            def body(e):
                def run(eng):
                    for f in self.q[e]:
                        f(eng)
                return run
            block.tensor(body("tensor"))
            block.vector(body("vector"))
            block.scalar(body("scalar"))
            block.gpsimd(body("gpsimd"))
            block.sync(body("sync"))


def bc(ap, dim, n):
    shape = list(ap.shape)
    ix = tuple(slice(None) for _ in range(dim)) + (None,)
    return ap[ix].to_broadcast(shape[:dim] + [n] + shape[dim:])


def decoder(nc, I, out, upto=6):
    with ExitStack() as ctx:
        P = Prog(nc, ctx)

        def sb(name, shape, dt=F32):
            return ctx.enter_context(nc.sbuf_tensor(name, shape, dt))

        PS = [ctx.enter_context(nc.psum_tensor(f"ps{i}", [128, 512], F32)) for i in range(8)]
        PB = [p[:, :].bitcast(BF) for p in PS]
        bfree = [[] for _ in range(8)]

        class Ring:
            def __init__(self, banks):
                self.banks, self.n = banks, 0

            def take(self):
                b = self.banks[self.n % len(self.banks)]
                self.n += 1
                return b

        x = sb("x", [128, T, D])
        xnT = sb("xnT", [128, 2, T * 128])
        xn = sb("xn", [128, 2, D])
        st = sb("st", [128, T, 6])
        mv = sb("mv", [128, T, 2])
        ve = sb("ve", [128, T])
        rstd = sb("rstd", [128, T])
        half = sb("half", [128, 1])
        idf = sb("idf", [128, 128])
        idb = sb("idb", [128, 128], BF)
        maskQ = sb("maskQ", [128, 128], BF)
        maskK = sb("maskK", [128, 128], BF)
        E = sb("E", [48, H, 128], BF)
        W = sb("W", [128, 24736])
        ctxT = sb("ctxT", [128, 2, 512])
        ctxN = sb("ctxN", [64, 8, D])
        work = sb("work", [128, 9700])
        wof = [0]

        def wk(n, dt=F32):
            a = wof[0]
            wof[0] += n
            assert wof[0] <= 9700, wof[0]
            v = work[:, a:a + n]
            return v if dt is F32 else v.bitcast(dt)

        gx = [P.group(f"x{i}") for i in range(4)]
        gc, gw0, gb = P.group("c"), P.group("w0"), P.group("b")
        xd = I["x"].rearrange("(t p) d -> p t d", p=128)
        for i in range(4):
            P.dma("sync", gx[i], x[:, 4 * i:4 * i + 4, :], xd[:, 4 * i:4 * i + 4, :])
        SM = sb("SM", [128, 5392])
        so = [0]

        def small(name, g, shape, src, e="sync"):
            n = int(np.prod(shape))
            a = so[0]
            so[0] += n
            assert so[0] <= 5392
            P.dma(e, g, SM[:, a:a + n].rearrange("p (a b) -> p a b", b=shape[-1]) if len(shape) == 2 else SM[:, a:a + n], src)
            v = SM[:, a:a + n]
            return v.rearrange("p (a b) -> p a b", b=shape[-1]) if len(shape) == 2 else v

        def bcast(v):
            return bass.AP(v.tensor, v.offset, [[0, 128]] + [list(p) for p in v.ap])

        def weight(name, g, n):
            return small(name, g, [2, n], I[name].rearrange("(k p) n -> p k n", p=128))

        xf = xnT[:, :, :].rearrange("p k n -> p (k n)")
        P.dma("sync", gc, W[:, 0:384], I["c_sq"])
        P.dma("sync", gc, xf[:, 0:2048], I["c_ali"])
        P.dma("sync", gc, xf[0:48, 2048:4096], I["c_E"])
        wA = [weight("w_att0", gw0, 768)]
        wo0 = weight("w_o0", gw0, 256)
        bA = [small("b_att0", gb, [768], bcast(I["b_att0"]))]
        bo0 = small("b_o0", gb, [256], bcast(I["b_o0"]))

        z0 = P.put("vector", lambda e: e.memset(half[:, :], -0.5))
        tid = P.put("vector", lambda e: e.tensor_copy(idf[:, :], W[:, 0:128]), [P.landed(gc)])
        P.put("vector", lambda e: e.tensor_copy(idb[:, :], W[:, 0:128]))
        P.put("vector", lambda e: e.tensor_copy(maskQ[:, :], W[:, 128:256]))
        P.put("vector", lambda e: e.tensor_copy(maskK[:, :], W[:, 256:384]))
        tE = P.put("vector", lambda e: e.tensor_copy(E[:, :, :], xf[0:48, 2048:4096].rearrange("p (h k) -> p h k", h=H)))
        t_ali = P.landed(gc)

        gxa = P.group("xa")
        wxa = weight("w_xa0", gxa, 1024)
        P.dma("sync", gxa, ctxT[:, :, :], I["ctxT"].rearrange("(k p) n -> p k n", p=128))
        P.dma("sync", gxa, ctxN[:, :, :], I["ctxN"])
        gm0 = P.group("m0")
        win0 = W[:, 0:16384].rearrange("p (k n) -> p k n", k=2)
        wout0 = W[:, 16384:24576].rearrange("p (c n) -> p c n", c=32)
        win_d = I["w_in0"].rearrange("(k p) n -> p k n", p=128)
        P.dma("sync", gm0, win0[:, 0, :], win_d[:, 0, :], [tE])
        P.dma("sync", gm0, win0[:, 1, 0:4096], win_d[:, 1, 0:4096])
        wr0 = weight("w_r0", gm0, 8)
        bm0 = small("b_m0", gm0, [256], bcast(I["b_m0"]))
        gat1 = P.group("at1")
        wA.append(W[:, 18464:19232].rearrange("p (k n) -> p k n", k=2))
        bA.append(W[:, 19232:19616])
        gx1 = P.group("cr1")

        xt = [P.landed(gx[t // 4]) for t in range(T)]
        xnT_rd = [[] for _ in range(T)]
        xnT_wr = [None] * T
        xn_rd = [None, None]
        prev = {"wk": []}

        def layernorm_steps(pair, ring):
            a2 = []
            for t in (2 * pair, 2 * pair + 1):
                a = P.put("vector", lambda e, t=t: e.bn_stats(st[:, t, :], x[:, t, :]), [xt[t]])
                a = P.put("vector", lambda e, t=t: e.bn_aggr(mv[:, t, :], st[:, t, :]), [a])
                a1 = P.put("vector", lambda e, t=t: e.tensor_scalar(ve[:, t:t + 1], mv[:, t, 1:2], 1e-5, None, ALU.add), [a])
                a2.append(P.put("gpsimd", lambda e, t=t: e.tensor_tensor(rstd[:, t:t + 1], ve[:, t:t + 1], half[:, :], ALU.pow), [a1, z0]))
            yield
            a3 = []
            for j in (0, 1):
                t = 2 * pair + j
                a3.append(P.put("vector", lambda e, t=t, j=j: e.tensor_scalar(
                    xn[:, j, :], x[:, t, :], mv[:, t, 0:1], rstd[:, t:t + 1], ALU.subtract, ALU.mult), [a2[j], a1, xn_rd[j]]))
            yield
            b = ring.take()
            for j in (0, 1):
                for k in (0, 1):
                    a4 = P.put("tensor", lambda e, j=j, k=k: e.transpose(
                        PS[b][:, 256 * k + 128 * j:256 * k + 128 * j + 128], xn[:, j, 128 * k:128 * k + 128], idf[:, :]),
                        [a3[j], tid, bfree[b]])
                xn_rd[j] = a4
            a5 = P.put("scalar", lambda e: e.copy(
                xnT[:, :, 256 * pair:256 * pair + 256], PS[b][:, :].rearrange("p (k n) -> p k n", k=2)),
                [a4, xnT_rd[2 * pair], xnT_rd[2 * pair + 1]])
            bfree[b] = [a5]
            for t in (2 * pair, 2 * pair + 1):
                xnT_wr[t], xnT_rd[t] = a5, []

        def layernorm(pair, ring):
            for _ in layernorm_steps(pair, ring):
                pass

        def mms(out_, pairs, after, start=True, **kw):
            n = len(pairs)
            for i, (l, r) in enumerate(pairs):
                tok = P.put("tensor", lambda e, l=l, r=r, i=i: e.matmul(
                    out_, l, r, start=start and i == 0, stop=i == n - 1, skip_group_check=True),
                    after if i == 0 else (), sig=i == n - 1)
            return tok

        def attn_phase(L):
            wof[0] = 0
            NK = 16 if L == 0 else 4
            per = H // NK
            NW = 768 if L == 0 else 384
            NR = H + NK
            QK = NR * 16
            Wt, bias = wA[L], bA[L]
            wtok = [P.landed(gw0), P.landed(gb)] if L == 0 else [P.landed(gat1)]
            base = prev["wk"]
            wo_ = [12288 if L == 0 else 19616]

            def wb(n, h):
                a = wo_[0]
                wo_[0] += n * h // 2
                return W[:, a:a + n * h // 2].bitcast(BF).rearrange("p (h c) -> p h c", h=h)

            if L == 0:
                R = [wb(128, NR) for _ in range(2)]
            else:
                R = [wk(NR * 64, BF).rearrange("p (h c) -> p h c", c=128) for _ in range(2)]
            qs = [wb(256, H) for _ in range(2)]
            ks = [wb(256, NK) for _ in range(2)]
            qkf = [wk(512) for _ in range(2)]
            Vt = [[wk(NK * 32).rearrange("p (h c) -> p h c", c=32) for _ in range(2)] for _ in range(2)]
            m = wk(32).rearrange("p (j h) -> p j h", j=2)
            mr = wk(32).rearrange("p (j h) -> p j h", j=2)
            NP = wk(48, BF).rearrange("p (j c h) -> p j c h", j=2, c=3)
            mT = wk(128, BF)[0:48, :]
            PT = [wk(512) for _ in range(6)]
            OT = wk(1024).rearrange("p (g n) -> p g n", g=4)
            rc = [wk(16) for _ in range(2)]
            On = [wk(256) for _ in range(2)]
            OnT = [wk(256).rearrange("p (k n) -> p k n", k=2) for _ in range(2)]
            zt = []
            for j in range(2):
                z = P.put("vector", lambda e, j=j: e.memset(R[j][:, :, 96:128], 0.0), base)
                zt.append(z)
                if L == 0:
                    zt.append(P.put("vector", lambda e, j=j: e.tensor_copy(
                        R[j][:, 0:16, 96:128], xf[:, 512 * j:512 * j + 512].rearrange("p (h c) -> p h c", c=32)), [z, t_ali]))
                    zt.append(P.put("vector", lambda e, j=j: e.tensor_copy(
                        R[j][:, 16:32, 96:128], xf[:, 1024 + 512 * j:1536 + 512 * j].rearrange("p (h c) -> p h c", c=32)), [z]))
                for i in range(2):
                    z2 = P.put("gpsimd", lambda e, i=i, j=j: e.memset(Vt[i][j], 0.0), base)
                    zt.append(P.put("gpsimd", lambda e, i=i, j=j: e.memset(Vt[i][j][:, :, 16:17], 1.0), [z2]))
            if L == 0:
                for t in range(T):
                    xnT_rd[t] = [tE] + zt
            rp = Ring([0, 1, 6])
            rs = Ring([2, 3, 4, 5])
            ro = Ring([7])
            st_ = {"m": [], "NP": [], "mT": [], "PT": [[] for _ in PT], "OT": [], "On": [[], []], "OnT": [[], []],
                   "R": [[], []], "qs": [[], []], "V": [[[], []], [[], []]], "rc": [[], []], "qkf": [[], []]}
            nPT = [0]
            S_ = [dict() for _ in range(B)]

            def proj(b, j):
                t = 2 * b + j
                lh = [xnT[:, k, 128 * t:128 * t + 128] for k in range(2)]
                ba = rp.take()
                qk = mms(PS[ba][:, 0:min(NW, 512)], [(lh[k], Wt[:, k, 0:min(NW, 512)]) for k in range(2)],
                         [xnT_wr[t], wtok, bfree[ba]])
                if L == 0:
                    bb = rp.take()
                    vv = mms(PS[bb][:, 0:256], [(lh[k], Wt[:, k, 512:768]) for k in range(2)], [bfree[bb]])
                    S_[b]["pj", j] = (ba, qk, bb, vv, PS[bb][:, 0:256], 512)
                else:
                    vv = qk
                    S_[b]["pj", j] = (ba, qk, ba, vv, PS[ba][:, QK:NW], QK)
                xnT_rd[t] = [vv]

            def split_a(b, j):
                ba, qk, bb, vv, vp, vo = S_[b]["pj", j]
                f = qkf[j]
                a = P.put("vector", lambda e: e.tensor_tensor(f[:, 0:QK], PS[ba][:, 0:QK], bias[:, 0:QK], ALU.add),
                          [qk, wtok, st_["qkf"][j], base])
                v = P.put("vector", lambda e: e.tensor_tensor(
                    Vt[b % 2][j][:, :, 0:16], vp.rearrange("p (h d) -> p h d", d=16),
                    bias[:, vo:vo + NK * 16].rearrange("p (h d) -> p h d", d=16), ALU.add),
                    [vv, zt, st_["V"][b % 2][j]])
                bfree[ba] = [a, v]
                bfree[bb] = [a, v]
                S_[b]["V", j] = v
                R6 = R[j][:, :, 0:96].rearrange("p h (c d) -> p h c d", d=16)
                f3 = f[:, 0:QK].rearrange("p (h d) -> p h d", d=16)
                c1 = P.put("scalar", lambda e: e.copy(R6[:, :, 0, :], f3), [a, st_["R"][j], zt])
                S_[b]["c1", j] = c1

            def split_b(b, j):
                R6 = R[j][:, :, 0:96].rearrange("p h (c d) -> p h c d", d=16)
                f3 = qkf[j][:, 0:QK].rearrange("p (h d) -> p h d", d=16)
                c1 = S_[b]["c1", j]
                r1 = P.put("vector", lambda e: e.tensor_tensor(f3, f3, R6[:, :, 0, :], ALU.subtract), [c1])
                c2 = P.put("scalar", lambda e: e.copy(R6[:, :, 4, :], f3), [r1])
                w = [c1, c2]
                w.append(P.put("vector", lambda e: e.tensor_copy(R6[:, 0:16, 3:6:2, :], bc(R6[:, 0:16, 0, :], 2, 2)), [c1]))
                w.append(P.put("vector", lambda e: e.tensor_copy(R6[:, 16:NR, 1:3, :], bc(R6[:, 16:NR, 0, :], 2, 2))))
                S_[b]["w", j] = w

            def split_c(b, j):
                R6 = R[j][:, :, 0:96].rearrange("p h (c d) -> p h c d", d=16)
                f3 = qkf[j][:, 0:QK].rearrange("p (h d) -> p h d", d=16)
                w = S_[b]["w", j]
                c2 = w[1]
                w.append(P.put("gpsimd", lambda e: e.tensor_copy(R6[:, 0:16, 1, :], R6[:, 0:16, 4, :]), [c2]))
                w.append(P.put("gpsimd", lambda e: e.tensor_copy(R6[:, 16:NR, 3, :], R6[:, 16:NR, 4, :])))
                w.append(P.put("vector", lambda e: e.tensor_tensor(R6[:, 0:16, 2, :], f3[:, 0:16, :], R6[:, 0:16, 4, :], ALU.subtract), [c2]))
                w.append(P.put("vector", lambda e: e.tensor_tensor(R6[:, 16:NR, 5, :], f3[:, 16:NR, :], R6[:, 16:NR, 4, :], ALU.subtract)))
                st_["qkf"][j] = [w[-1], w[-2]]
                S_[b]["R", j] = w

            def stack(b, j):
                tk, rd = [], []
                for h0, dst, n in ((0, qs, H), (H, ks, NK)):
                    for c in range(0, n, 8):
                        m_ = min(8, n - c)
                        bk = rp.take()
                        for h in range(m_):
                            tr = P.put("tensor", lambda e, c=c, h=h, bk=bk, h0=h0: e.transpose(
                                PB[bk][:, 128 * h:128 * h + 128], R[j][:, h0 + c + h, :], idb[:, :]),
                                [S_[b]["R", j], bfree[bk], tE] if h == 0 else (), sig=h == m_ - 1)
                        rd.append(tr)
                        src = PB[bk][:, 0:128 * m_].rearrange("p (h n) -> p h n", h=m_)
                        dd = dst[b % 2][:, c:c + m_, 128 * j:128 * j + 128]
                        if c == 0:
                            ev = P.put("scalar", lambda e, dd=dd, src=src: e.copy(dd, src), [tr, st_["qs"][b % 2]])
                        else:
                            ev = P.put("vector", lambda e, dd=dd, src=src: e.tensor_copy(dd, src), [tr, st_["qs"][b % 2]])
                        bfree[bk] = [ev]
                        tk.append(ev)
                st_["R"][j] = rd
                S_[b]["qs", j] = tk

            def scores(b, j):
                q, k_ = qs[b % 2], ks[b % 2]
                n = 4 if j == 0 else 2
                w_ = 512 // n
                for h0 in range(0, H, n):
                    bk = rs.take()
                    for i in range(n):
                        h = h0 + i
                        P.put("tensor", lambda e, h=h, i=i, bk=bk: e.matmul(
                            PS[bk][:, w_ * i:w_ * i + w_], q[:, h, 128 * j:128 * j + 128], k_[:, h // per, 0:w_],
                            start=i == 0, stop=False, skip_group_check=True),
                            [S_[b]["qs", 0], S_[b]["qs", j], bfree[bk]] if i == 0 else (), sig=False)
                    ov = PS[bk][:, :].rearrange("p (i n) -> p i n", i=n)
                    mm = P.put("tensor", lambda e, ov=ov: e.matmul(
                        ov[:, :, w_ - 128:w_], idb[:, :], bc(maskQ[:, :], 1, n), start=False, stop=True,
                        skip_group_check=True))
                    mx = P.put("vector", lambda e, ov=ov, h0=h0: e.tensor_reduce(
                        m[:, j, h0:h0 + n], ov, AX, ALU.max), [mm, st_["m"], base])
                    bfree[bk] = [mx]
                if j == 0:
                    return
                a = P.put("vector", lambda e: e.tensor_scalar(NP[:, :, 0, :], m, -1.0, None, ALU.mult), [mx, st_["NP"]])
                a = P.put("vector", lambda e: e.scalar_tensor_tensor(
                    out=mr, in0=m, scalar=-1.0, in1=NP[:, :, 0, :], op0=ALU.mult, op1=ALU.subtract), [a])
                st_["m"] = [a]
                a2 = P.put("vector", lambda e: e.tensor_copy(NP[:, :, 1, :], mr), [a])
                a3 = P.put("vector", lambda e: e.tensor_tensor(NP[:, :, 2, :], mr, NP[:, :, 1, :], ALU.subtract), [a2])
                S_[b]["NP"] = a3

            def fold(b):
                bk = rp.take()
                for j in range(2):
                    tr = P.put("tensor", lambda e, j=j: e.transpose(
                        PB[bk][0:48, 128 * j:128 * j + 128], NP[:, j, :, :].rearrange("p c h -> p (c h)"), idb[:, :]),
                        [S_[b]["NP"], bfree[bk]] if j == 0 else (), sig=j == 1)
                st_["NP"] = [tr]
                ev = P.put("vector", lambda e: e.tensor_copy(mT, PB[bk][0:48, 0:256]), [tr, st_["mT"], base])
                bfree[bk] = [ev]
                S_[b]["mT"] = ev

            def attend_s(b, g):
                q, k_ = qs[b % 2], ks[b % 2]
                pts = []
                for kind in range(3):
                    bk = rs.take()
                    hs = [4 * g + 2 * kind, 4 * g + 2 * kind + 1] if kind < 2 else [4 * g + i for i in range(4)]
                    w_, kt, q0 = (256, 0, 0) if kind < 2 else (128, 1, 128)
                    for i, h in enumerate(hs):
                        P.put("tensor", lambda e, h=h, i=i, bk=bk, w_=w_, kt=kt, q0=q0: e.matmul(
                            PS[bk][:, w_ * i:w_ * i + w_], k_[:, h // per, 128 * kt:128 * kt + 128], q[:, h, q0:256],
                            start=i == 0, stop=False, skip_group_check=True),
                            [S_[b]["mT"], tE, bfree[bk]] if i == 0 else (), sig=False)
                        P.put("tensor", lambda e, h=h, i=i, bk=bk, w_=w_, q0=q0: e.matmul(
                            PS[bk][:, w_ * i:w_ * i + w_], E[0:48, h, :], mT[:, q0:256],
                            start=False, stop=False, skip_group_check=True), sig=False)
                    ov = PS[bk][:, :].rearrange("p (i n) -> p i n", i=len(hs))
                    mm = P.put("tensor", lambda e, ov=ov, n=len(hs): e.matmul(
                        ov[:, :, 0:128], idb[:, :], bc(maskK[:, :], 1, n), start=False, stop=True,
                        skip_group_check=True))
                    pi = nPT[0] % 6
                    nPT[0] += 1
                    ex = P.put("scalar", lambda e, pi=pi, bk=bk: e.activation(
                        PT[pi], PS[bk][:, :], ACT.Exp, scale=0.25), [mm, st_["PT"][pi], base])
                    bfree[bk] = [ex]
                    pts.append((pi, ex))
                if g == 3:
                    st_["qs"][b % 2] = [mm]
                    st_["mT"] = [mm]
                S_[b]["pts", g] = pts

            def attend_v(b, g):
                pts = S_[b]["pts", g]
                if g % 2 == 0:
                    S_[b]["bo"] = ro.take()
                bo = S_[b]["bo"]
                o0 = 256 * (g % 2)
                for i in range(4):
                    h = 4 * g + i
                    pi, ex = pts[i // 2]
                    P.put("tensor", lambda e, i=i, h=h, pi=pi: e.matmul(
                        PS[bo][32 * i:32 * i + 32, o0:o0 + 256], Vt[b % 2][0][:, h // per, :],
                        PT[pi][:, 256 * (i % 2):256 * (i % 2) + 256], start=True, stop=False, skip_group_check=True),
                        [ex, S_[b]["V", 0], S_[b]["V", 1], bfree[bo] if g % 2 == 0 else ()], sig=False)
                pi2, ex2 = pts[2]
                for i in range(4):
                    h = 4 * g + i
                    pv = P.put("tensor", lambda e, i=i, h=h: e.matmul(
                        PS[bo][32 * i:32 * i + 32, o0 + 128:o0 + 256], Vt[b % 2][1][:, h // per, :],
                        PT[pi2][:, 128 * i:128 * i + 128], start=False, stop=True, skip_group_check=True),
                        [ex2], sig=i == 3)
                for pi, _ in pts:
                    st_["PT"][pi] = [pv]
                if g % 2 == 1:
                    ev = P.put("scalar", lambda e: e.copy(
                        OT[:, g - 1:g + 1, :], PS[bo][:, :].rearrange("p (g n) -> p g n", g=2)), [pv, st_["OT"], base])
                    bfree[bo] = [ev]
                    S_[b]["OT", g] = ev
                if g == 3:
                    st_["V"][b % 2] = [[pv], [pv]]

            def fin1(b, j):
                t = 2 * b + j
                bk = rp.take()
                for g in range(4):
                    tr = P.put("tensor", lambda e, g=g: e.transpose(
                        PS[bk][:, 128 * g:128 * g + 128], OT[:, g, 128 * j:128 * j + 128], idf[:, :]),
                        [S_[b]["OT", 1], S_[b]["OT", 3], bfree[bk]] if g == 0 else (), sig=g == 3)
                ov = PS[bk][:, :].rearrange("p (h c) -> p h c", c=32)
                r = P.put("vector", lambda e: e.reciprocal(rc[j], ov[:, :, 16]), [tr, st_["rc"][j], base])
                o = P.put("vector", lambda e: e.tensor_tensor(
                    On[j].rearrange("p (h d) -> p h d", d=16), ov[:, :, 0:16], bc(rc[j], 2, 16), ALU.mult),
                    [r, st_["On"][j]])
                st_["rc"][j] = [o]
                bfree[bk] = [o]
                if L == 1:
                    xt[t] = P.put("gpsimd", lambda e: e.tensor_tensor(x[:, t, :], x[:, t, :], On[j], ALU.add),
                                  [o, xt[t], xnT_wr[t]])
                    st_["On"][j] = [xt[t]]
                if j == 1:
                    st_["OT"] = [tr]
                S_[b]["f1", j] = o

            def fin2(b, j):
                bk = rp.take()
                for k in range(2):
                    tr = P.put("tensor", lambda e, k=k: e.transpose(
                        PS[bk][:, 128 * k:128 * k + 128], On[j][:, 128 * k:128 * k + 128], idf[:, :]),
                        [S_[b]["f1", j], bfree[bk]] if k == 0 else (), sig=k == 1)
                st_["On"][j] = [tr]
                ev = P.put("scalar", lambda e: e.copy(OnT[j], PS[bk][:, 0:256].rearrange("p (k n) -> p k n", k=2)),
                           [tr, st_["OnT"][j], base])
                bfree[bk] = [ev]
                S_[b]["f2", j] = ev
                t = 2 * b + j
                S_[b]["xa", j] = P.put("gpsimd", lambda e: e.tensor_tensor(x[:, t, :], x[:, t, :], bo0, ALU.add),
                                       [xt[t], P.landed(gb), xnT_wr[t]])

            def fin3(b, j):
                t = 2 * b + j
                bk = rp.take()
                mo = mms(PS[bk][:, 0:256], [(OnT[j][:, k, :], wo0[:, k, :]) for k in range(2)], [S_[b]["f2", j], bfree[bk]])
                st_["OnT"][j] = [mo]
                xt[t] = P.put("vector", lambda e: e.tensor_tensor(
                    x[:, t, :], x[:, t, :], PS[bk][:, 0:256], ALU.add), [mo, S_[b]["xa", j]])
                bfree[bk] = [xt[t]]

            layernorm(0, rp)
            layernorm(1, rp)
            for j in range(2):
                proj(0, j)
                split_a(0, j)
                split_b(0, j)
                split_c(0, j)
                stack(0, j)
            for b in range(B + 1):
                n, f = b + 1 < B, b >= 1

                def fin(step, b=b, f=f):
                    if f and (L == 0 or step is fin1):
                        step(b - 1, 0)
                        step(b - 1, 1)
                if b == B:
                    for step in (fin1, fin2, fin3):
                        fin(step)
                    break
                scores(b, 0)
                scores(b, 1)
                fin(fin1)
                if n:
                    proj(b + 1, 0)
                fold(b)
                if n:
                    split_a(b + 1, 0)
                attend_s(b, 0)
                if n:
                    split_b(b + 1, 0)
                fin(fin2)
                attend_s(b, 1)
                attend_v(b, 0)
                if n:
                    split_c(b + 1, 0)
                    proj(b + 1, 1)
                attend_s(b, 2)
                if n:
                    split_a(b + 1, 1)
                attend_v(b, 1)
                fin(fin3)
                if n:
                    split_b(b + 1, 1)
                attend_s(b, 3)
                attend_v(b, 2)
                if n:
                    split_c(b + 1, 1)
                    stack(b + 1, 0)
                if b + 2 < B:
                    layernorm(b + 2, rp)
                attend_v(b, 3)
                if n:
                    stack(b + 1, 1)
            prev["wk"] = [xt[t] for t in range(T)] + [st_["OT"][0], st_["qs"][1][0]] + st_["PT"][0] + st_["PT"][5]

        def cross0():
            wof[0] = 0
            base = prev["wk"]
            qT_, kT_, V_ = [[wk(512).rearrange("p (k n) -> p k n", k=2) for _ in range(2)] for _ in range(3)]
            Pm = [wk(320) for _ in range(2)]
            PTn = wk(512).rearrange("p (c n) -> p c n", c=2)
            PTc = wk(256)[0:64, :]
            OTs = wk(512).rearrange("p (m n) -> p m n", m=2)
            sm = wk(16)
            st_ = {k: [] for k in ("PTn", "OTs", "sm0", "sm1", "P0", "P1")}
            st_.update({(k, i): [] for k in ("qT", "kT", "V") for i in range(2)})
            r1, r2 = Ring([0, 1, 2, 3]), Ring([4, 5, 6, 7])
            wt = P.landed(gxa)
            S_ = [dict() for _ in range(B)]

            def front(b):
                qT, kT, V = qT_[b % 2], kT_[b % 2], V_[b % 2]
                xs = [xnT[:, k, 256 * b:256 * b + 256] for k in range(2)]
                wx = [xnT_wr[2 * b], wt]
                for o, dst, nm in ((0, qT, "qT"), (256, kT, "kT")):
                    bk = r1.take()
                    for mt in range(2):
                        tk = mms(PS[bk][:, 256 * mt:256 * mt + 256],
                                 [(wxa[:, k, o + 128 * mt:o + 128 * mt + 128], xs[k]) for k in range(2)], [wx, bfree[bk]])
                    src = PS[bk][:, :].rearrange("p (k n) -> p k n", k=2)
                    ev = P.put("scalar", lambda e, dst=dst, src=src: e.copy(dst, src), [tk, st_[nm, b % 2], base])
                    bfree[bk] = [ev]
                    S_[b][nm] = ev
                bk = r1.take()
                for j in range(2):
                    t = 2 * b + j
                    tk = mms(PS[bk][:, 256 * j:256 * j + 256],
                             [(xnT[:, k, 128 * t:128 * t + 128], wxa[:, k, 512:768]) for k in range(2)], [wx, bfree[bk]])
                    xnT_rd[t] = [tk]
                ev = P.put("vector", lambda e, bk=bk: e.tensor_copy(V, PS[bk][:, :].rearrange("p (k n) -> p k n", k=2)),
                           [tk, st_["V", b % 2], base])
                bfree[bk] = [ev]
                S_[b]["V"] = ev

            def back(b):
                qT, kT, V = qT_[b % 2], kT_[b % 2], V_[b % 2]
                for j in range(2):
                    bk = r2.take()
                    lq = [qT[:, k, 128 * j:128 * j + 128] for k in range(2)]
                    for k in range(2):
                        P.put("tensor", lambda e, k=k, bk=bk, lq=lq: e.matmul(
                            PS[bk][:, 0:64], lq[k], ctxT[:, k, 64 * b:64 * b + 64], start=k == 0, stop=False,
                            skip_group_check=True), [S_[b]["qT"], S_[b]["kT"], bfree[bk]], sig=False)
                        tk = P.put("tensor", lambda e, k=k, bk=bk, lq=lq: e.matmul(
                            PS[bk][:, 64:320], lq[k], kT[:, k, :], start=False, stop=k == 1,
                            skip_group_check=True), sig=k == 1)
                    o = 8 * j
                    mx = P.put("vector", lambda e, bk=bk, o=o: e.tensor_reduce(sm[:, o:o + 1], PS[bk][:, 0:320], AX, ALU.max),
                               [tk, st_[f"sm{j}"], base])
                    nb = P.put("vector", lambda e, o=o: e.tensor_scalar(sm[:, o + 1:o + 2], sm[:, o:o + 1], -0.0625, None, ALU.mult), [mx])
                    ex = P.put("scalar", lambda e, bk=bk, o=o, j=j: e.activation(
                        Pm[j], PS[bk][:, 0:320], ACT.Exp, bias=sm[:, o + 1:o + 2], scale=0.0625,
                        accum_out=sm[:, o + 2:o + 3]), [nb, st_[f"P{j}"]])
                    bfree[bk] = [ex, mx]
                    S_[b]["rc", j] = P.put("vector", lambda e, o=o: e.reciprocal(sm[:, o + 3:o + 4], sm[:, o + 2:o + 3]), [ex])
                    S_[b]["P", j] = ex
                st_["qT", b % 2] = st_["kT", b % 2] = [tk]
                if b + 1 < B:
                    front(b + 1)
                if b + 2 < B:
                    layernorm(b + 2, r1)
                bn, bc_ = r2.take(), r2.take()
                for j in range(2):
                    P.put("tensor", lambda e, j=j: e.transpose(
                        PS[bc_][0:64, 128 * j:128 * j + 128], Pm[j][:, 0:64], idf[:, :]),
                        [S_[b]["P", j], bfree[bc_]], sig=False)
                    for c in range(2):
                        tr = P.put("tensor", lambda e, j=j, c=c: e.transpose(
                            PS[bn][:, 256 * c + 128 * j:256 * c + 128 * j + 128], Pm[j][:, 64 + 128 * c:192 + 128 * c], idf[:, :]),
                            [bfree[bn]], sig=c == 1)
                    st_[f"P{j}"] = [tr]
                e1 = P.put("scalar", lambda e: e.copy(PTn, PS[bn][:, :].rearrange("p (c n) -> p c n", c=2)), [tr, st_["PTn"], base])
                e2 = P.put("vector", lambda e: e.tensor_copy(PTc, PS[bc_][0:64, 0:256]), [tr, st_["PTn"], base])
                bfree[bn], bfree[bc_] = [e1], [e2]
                bk = r2.take()
                for mt in range(2):
                    ms = slice(128 * mt, 128 * mt + 128)
                    tk = mms(PS[bk][:, 256 * mt:256 * mt + 256],
                             [(ctxN[0:64, b, ms], PTc), (V[:, 0, ms], PTn[:, 0, :]), (V[:, 1, ms], PTn[:, 1, :])],
                             [e1, e2, S_[b]["V"], bfree[bk]])
                st_["V", b % 2] = st_["PTn"] = [tk]
                ev = P.put("scalar", lambda e, bk=bk: e.copy(OTs, PS[bk][:, :].rearrange("p (k n) -> p k n", k=2)),
                           [tk, st_["OTs"], base])
                bfree[bk] = [ev]
                bk = r2.take()
                for j in range(2):
                    tk = mms(PS[bk][:, 256 * j:256 * j + 256],
                             [(OTs[:, mt, 128 * j:128 * j + 128], wxa[:, mt, 768:1024]) for mt in range(2)], [ev, bfree[bk]])
                st_["OTs"] = [tk]
                for j in range(2):
                    t = 2 * b + j
                    xt[t] = P.put("vector", lambda e, j=j, t=t, bk=bk: e.scalar_tensor_tensor(
                        out=x[:, t, :], in0=PS[bk][:, 256 * j:256 * j + 256], scalar=sm[:, 8 * j + 3:8 * j + 4],
                        in1=x[:, t, :], op0=ALU.mult, op1=ALU.add), [tk, S_[b]["rc", j], xt[t], xnT_wr[t]])
                    st_[f"sm{j}"] = [xt[t]]
                bfree[bk] = [xt[2 * b], xt[2 * b + 1]]

            layernorm(0, r1)
            layernorm(1, r1)
            front(0)
            for b in range(B):
                back(b)
            prev["wk"] = [xt[t] for t in range(T)] + [st_["OTs"][0]]

        def gates(NE, TOPK, wr, wtok, G, tmp, ring, factor):
            Lg, Rp, v8, rep, s1 = tmp
            base = prev["wk"]
            z = P.put("vector", lambda e: e.memset(rep, BIG), base)
            bk = ring.take()
            for t in range(T):
                tk = mms(PS[bk][:, NE * t:NE * t + NE],
                         [(xnT[:, k, 128 * t:128 * t + 128], wr[:, k, :]) for k in range(2)],
                         [xnT_wr[t], wtok, bfree[bk]], start=True)
            a = P.put("vector", lambda e: e.tensor_copy(Lg.rearrange("p t e -> p (t e)"), PS[bk][:, 0:T * NE]), [tk, base])
            bfree[bk] = [a]
            for t in range(T):
                m8 = P.put("vector", lambda e, t=t: e.max(v8[:, t, :], Lg[:, t, :]), [a])
            c = P.put("vector", lambda e: e.tensor_copy(rep[:, :, 0:TOPK], v8[:, :, 0:TOPK]), [m8, z])
            for t in range(T):
                mr_ = P.put("vector", lambda e, t=t: e.match_replace(
                    out=Rp[:, t, :], in_to_replace=rep[:, t, :], in_values=Lg[:, t, :], imm_value=-BIG), [c])
            se = P.put("vector", lambda e: e.tensor_tensor(Rp, Rp, Lg, ALU.not_equal), [mr_])
            su = P.put("vector", lambda e: e.tensor_tensor(Lg, Lg, v8[:, :, 0:1].to_broadcast([128, T, NE]), ALU.subtract), [se])
            ex = P.put("scalar", lambda e: e.activation(Lg, Lg, ACT.Exp), [su])
            mu = P.put("vector", lambda e: e.tensor_tensor(G, Lg, Rp, ALU.mult), [ex])
            sm_ = P.put("vector", lambda e: e.tensor_reduce(s1[:, 0, :], G, AX, ALU.add), [mu])
            rc_ = P.put("vector", lambda e: e.reciprocal(s1[:, 1, :], s1[:, 0, :]), [sm_])
            return P.put("vector", lambda e: e.scalar_tensor_tensor(
                out=G, in0=G, scalar=factor, in1=bc(s1[:, 1, :], 2, NE), op0=ALU.mult, op1=ALU.mult), [rc_])

        def experts(L):
            wof[0] = 0
            NE, TOPK = (8, 2) if L == 0 else (16, 4)
            NC = 4 if L == 0 else 1
            gm = P.landed(gm0 if L == 0 else gm1)
            base = prev["wk"]
            G = wk(T * NE).rearrange("p (t e) -> p t e", e=NE)
            tmp = (wk(T * NE).rearrange("p (t e) -> p t e", e=NE), wk(T * NE).rearrange("p (t e) -> p t e", e=NE),
                   wk(T * 8).rearrange("p (t e) -> p t e", e=8), wk(T * 8).rearrange("p (t e) -> p t e", e=8),
                   wk(2 * T).rearrange("p (a t) -> p a t", a=2))
            sil = [wk(512) for _ in range(2)]
            U = [[wk(512) for _ in range(4)] for _ in range(2)]
            f_s, f_U = [[], []], [[], []]
            rh, ro_, rl = Ring([0, 1, 2, 3]), Ring([4, 5, 6]), Ring([7])
            for b in range(B):
                layernorm(b, rl)
            tg = gates(NE, TOPK, wr0 if L == 0 else wr1, gm, G, tmp, rl, 1.0 if L == 0 else 0.8)
            if L == 0:
                for t in range(T):
                    xt[t] = P.put("gpsimd", lambda e, t=t: e.tensor_tensor(x[:, t, :], x[:, t, :], bm0, ALU.add),
                                  [xt[t], gm, xnT_wr[t]])
            nu, ns = [0], [0]
            jobs = [("e", e_, NC) for e_ in range(NE)] + ([("s", 0, 4)] if L == 1 else [])

            def hidden(blk, job):
                kind, e_, nch = job
                u = nu[0] % 2
                nu[0] += 1
                toks = []
                for c in range(nch):
                    if L == 0:
                        wa = [win0[:, k, 1024 * e_ + 128 * c:1024 * e_ + 128 * c + 128] for k in range(2)]
                        wb = [win0[:, k, 1024 * e_ + 512 + 128 * c:1024 * e_ + 512 + 128 * c + 128] for k in range(2)]
                    elif kind == "e":
                        wa = [we1[:, k, 128 * e_:128 * e_ + 128] for k in range(2)]
                        wb = [we3[:, k, 128 * e_:128 * e_ + 128] for k in range(2)]
                    else:
                        wa = [ws13[:, k, 128 * c:128 * c + 128] for k in range(2)]
                        wb = [ws13[:, k, 512 + 128 * c:512 + 128 * c + 128] for k in range(2)]
                    ba, bb = rh.take(), rh.take()
                    xs = [xnT[:, k, 512 * blk:512 * blk + 512] for k in range(2)]
                    dep = [xnT_wr[4 * blk], xnT_wr[4 * blk + 2], gm]
                    ta = mms(PS[ba][:, :], list(zip(wa, xs)), [dep, bfree[ba]])
                    tb = mms(PS[bb][:, :], list(zip(wb, xs)), [bfree[bb]])
                    si = ns[0] % 2
                    ns[0] += 1
                    s_ = P.put("scalar", lambda e, si=si, ba=ba: e.activation(sil[si], PS[ba][:, :], ACT.Silu), [ta, f_s[si], base])
                    m_ = P.put("vector", lambda e, si=si, bb=bb, u=u, c=c: e.tensor_tensor(U[u][c], sil[si], PS[bb][:, :], ALU.mult),
                               [s_, tb, f_U[u], base])
                    bfree[ba], bfree[bb] = [s_], [m_]
                    f_s[si] = [m_]
                    toks.append(m_)
                for t in range(4 * blk, 4 * blk + 4):
                    xnT_rd[t] = [tb]
                return u, toks

            def down(blk, job, u, toks):
                kind, e_, nch = job
                for tl in range(4):
                    t = 4 * blk + tl
                    if L == 0:
                        ws = [wout0[:, 4 * e_ + c, :] for c in range(4)]
                    elif kind == "e":
                        ws = [we2[:, e_, :]]
                    else:
                        ws = [ws2[:, c, :] for c in range(4)]
                    bk = ro_.take()
                    tk = mms(PS[bk][:, 0:256], [(U[u][c][:, 128 * tl:128 * tl + 128], ws[c]) for c in range(nch)],
                             [toks, bfree[bk]])
                    sc = G[:, t, e_:e_ + 1] if kind == "e" else 0.2
                    xt[t] = P.put("vector", lambda e, t=t, bk=bk, sc=sc: e.scalar_tensor_tensor(
                        out=x[:, t, :], in0=PS[bk][:, 0:256], scalar=sc, in1=x[:, t, :], op0=ALU.mult, op1=ALU.add),
                        [tk, tg, xt[t], xnT_wr[t]])
                    bfree[bk] = [xt[t]]
                f_U[u] = [tk]

            pend = None
            for blk in range(4):
                for job in jobs:
                    u, toks = hidden(blk, job)
                    if pend:
                        down(*pend)
                    pend = (blk, job, u, toks)
            down(*pend)
            prev["wk"] = [xt[t] for t in range(T)] + f_U[0] + f_U[1]
            return f_U[0] + f_U[1]

        def cross1():
            wof[0] = 0
            base = prev["wk"]
            gt = P.landed(gx1)
            kM = kMt
            kv = wk(512)
            am = wk(16)
            sk = wk(16)
            rk = wk(16)
            K3 = wk(512, BF).rearrange("p (h c) -> p h c", c=64)
            vT = wk(1024).rearrange("p (m n) -> p m n", m=2)
            sv = wk(4)
            vq = wk(512, BF).rearrange("p (m n) -> p m n", m=2)
            Vq = wk(512, BF).rearrange("p (c n) -> p c n", c=4)
            qf = wk(256)
            Q3 = wk(512, BF).rearrange("p (h c) -> p h c", c=64)
            q3T = [wk(512, BF).rearrange("p (g n) -> p g n", g=8) for _ in range(2)]
            sq = [wk(16) for _ in range(2)]
            nsq = [wk(16) for _ in range(2)]
            rq = wk(16)
            s4 = wk(16)
            mm_ = wk(16)
            nb = wk(16)
            se = [wk(16) for _ in range(2)]
            rs_ = wk(16)
            ee = [wk(512) for _ in range(4)]
            ei = [wk(256, BF) for _ in range(3)]
            aT = [wk(512, BF) for _ in range(2)]
            On = wk(256)
            OnT = wk(256).rearrange("p (k n) -> p k n", k=2)
            r1, r2, r3 = Ring([0, 1]), Ring([2, 3, 4]), Ring([5, 6])
            bO = 7

            zk = P.put("gpsimd", lambda e: e.memset(kM[:, :, :], 0.0), base)
            z3 = P.put("vector", lambda e: e.memset(K3, 0.0), base)
            zq = P.put("vector", lambda e: e.memset(Q3, 0.0), base)

            def quant(src, n, s, r, dst, after, rd_dst):
                a = P.put("vector", lambda e: e.tensor_reduce(am, src.rearrange("p (h d) -> p h d", d=16), AX, ALU.max,
                                                              apply_absolute_value=True), after)
                a = P.put("vector", lambda e: e.tensor_scalar(s, am, 1.0 / 127.0, 1e-8, ALU.mult, ALU.max), [a])
                a = P.put("vector", lambda e: e.reciprocal(r, s), [a])
                a2 = P.put("vector", lambda e: e.tensor_tensor(src.rearrange("p (h d) -> p h d", d=16),
                                                               src.rearrange("p (h d) -> p h d", d=16), bc(r, 2, 16), ALU.mult), [a])
                a3 = P.put("vector", lambda e: e.tensor_scalar(src, src, MAGIC, MAGIC, ALU.add, ALU.subtract), [a2])
                return P.put("vector", lambda e: e.tensor_scalar(dst, src, 127.0, -127.0, ALU.min, ALU.max), [a3] + rd_dst)

            bv = [r3.take(), r3.take()]
            fK3, fkv, kMw = [z3], [], []
            for c in range(4):
                bk = r1.take()
                tk = mms(PS[bk][:, :], [(ctxT[:, k, 128 * c:128 * c + 128], wkv[:, k, :]) for k in range(2)],
                         [gt, P.landed(gxa), bfree[bk]])
                a = P.put("vector", lambda e, bk=bk: e.tensor_tensor(kv, PS[bk][:, :], bkv, ALU.add), [tk, fkv, base])
                bfree[bk] = [a]
                for m_ in range(2):
                    tv = P.put("tensor", lambda e, m_=m_, c=c: e.transpose(
                        PS[bv[m_]][:, 128 * c:128 * c + 128], kv[:, 256 + 128 * m_:384 + 128 * m_], idf[:, :]),
                        [a, bfree[bv[m_]]])
                kk = kv[:, 0:256]
                a = quant(kk, 16, sk, rk, kk, [a], [])
                k3 = kk.rearrange("p (h d) -> p h d", d=16)
                a = P.put("vector", lambda e: e.tensor_tensor(k3, k3, bc(sk, 2, 16), ALU.mult), [a])
                a = P.put("vector", lambda e: e.tensor_copy(K3[:, :, 0:16], k3), [a] + fK3)
                a = P.put("vector", lambda e: e.tensor_tensor(k3, k3, K3[:, :, 0:16], ALU.subtract), [a])
                a = P.put("vector", lambda e: e.tensor_copy(K3[:, :, 16:32], k3), [a])
                a = P.put("vector", lambda e: e.tensor_tensor(K3[:, :, 32:48], k3, K3[:, :, 16:32], ALU.subtract), [a])
                fkv = [a, tv]
                bk = r1.take()
                for g in range(8):
                    tr = P.put("tensor", lambda e, g=g, bk=bk: e.transpose(
                        PB[bk][:, 128 * g:128 * g + 128], K3[:, 2 * g:2 * g + 2, :].rearrange("p h c -> p (h c)"), idb[:, :]),
                        [a, bfree[bk]] if g == 0 else (), sig=g == 7)
                fK3 = [tr]
                evs = []
                for o in range(2):
                    evs.append(P.put("vector", lambda e, o=o, bk=bk, c=c: e.tensor_copy(
                        kM[64 * o:64 * o + 64, o::2, 128 * c:128 * c + 128],
                        PB[bk][64 * o:64 * o + 64, :].rearrange("p (g n) -> p g n", g=8)), [tr, zk]))
                bfree[bk] = evs
                kMw += evs
            for m_ in range(2):
                a = P.put("vector", lambda e, m_=m_: e.tensor_copy(vT[:, m_, :], PS[bv[m_]][:, :]), [tv, base])
                bfree[bv[m_]] = [a]
            a = P.put("vector", lambda e: e.tensor_reduce(sv[:, 0:2], vT, AX, ALU.max, apply_absolute_value=True), [a])
            a = P.put("vector", lambda e: e.tensor_scalar(sv[:, 0:2], sv[:, 0:2], 1.0 / 127.0, 1e-8, ALU.mult, ALU.max), [a])
            tsv = P.put("vector", lambda e: e.reciprocal(sv[:, 2:4], sv[:, 0:2]), [a])
            for m_ in range(2):
                a = P.put("vector", lambda e, m_=m_: e.tensor_scalar(vT[:, m_, :], vT[:, m_, :], sv[:, 2 + m_:3 + m_], None, ALU.mult), [tsv])
            a = P.put("vector", lambda e: e.tensor_scalar(vT, vT, MAGIC, MAGIC, ALU.add, ALU.subtract), [a])
            a = P.put("vector", lambda e: e.tensor_scalar(vq, vT, 127.0, -127.0, ALU.min, ALU.max), [a, base])
            bk = r1.take()
            for c in range(4):
                for m_ in range(2):
                    tr = P.put("tensor", lambda e, m_=m_, c=c, bk=bk: e.transpose(
                        PB[bk][:, 256 * c + 128 * m_:256 * c + 128 * m_ + 128], vq[:, m_, 128 * c:128 * c + 128], idb[:, :]),
                        [a, bfree[bk]])
            tV = P.put("vector", lambda e, bk=bk: e.tensor_copy(Vq, PB[bk].rearrange("p (c n) -> p c n", c=4)), [tr, base])
            bfree[bk] = [tV]
            tkv = tV

            fq = {"qf": [], "Q3": [zq], "q3T": [[], []], "sq": [[], []], "m": [], "se": [[], []], "ee": [[] for _ in range(4)],
                  "ei": [[] for _ in range(3)], "aT": [[], []], "On": [], "OnT": [], "rs": []}
            n_e = [0]
            n_i = [0]
            n_a = [0]
            S_ = [dict() for _ in range(T)]

            def queries(t):
                bk = r1.take()
                tk = mms(PS[bk][:, 0:256], [(xnT[:, k, 128 * t:128 * t + 128], wq1[:, k, :]) for k in range(2)],
                         [xnT_wr[t], gt, bfree[bk]])
                xnT_rd[t] = [tk]
                yield
                a = P.put("vector", lambda e: e.tensor_tensor(qf, PS[bk][:, 0:256], bq1, ALU.add), [tk, fq["qf"], base])
                bfree[bk] = [a]
                s_ = sq[t % 2]
                q3 = qf.rearrange("p (h d) -> p h d", d=16)
                dst = Q3[:, :, 0:48].rearrange("p h (c d) -> p h c d", d=16)
                a = P.put("vector", lambda e: e.tensor_reduce(am, q3, AX, ALU.max, apply_absolute_value=True), [a, tkv])
                yield
                a = P.put("vector", lambda e: e.tensor_scalar(s4, am, 1.0 / 127.0, 4e-8, ALU.mult, ALU.max), [a])
                yield
                b1 = P.put("vector", lambda e: e.tensor_scalar(s_, s4, 0.25, None, ALU.mult), [a, fq["sq"][t % 2], base])
                b2 = P.put("vector", lambda e: e.tensor_scalar(nsq[t % 2], s4, -0.25, None, ALU.mult))
                S_[t]["nsq"] = b2
                a = P.put("vector", lambda e: e.reciprocal(rq, s4), [a])
                yield
                a = P.put("vector", lambda e: e.tensor_tensor(q3, q3, bc(rq, 2, 16), ALU.mult), [a])
                yield
                a = P.put("vector", lambda e: e.tensor_scalar(qf, qf, MAGIC, MAGIC, ALU.add, ALU.subtract), [a])
                yield
                a = P.put("vector", lambda e: e.tensor_scalar(dst, bc(q3, 2, 3), 127.0, -127.0, ALU.min, ALU.max), [a, fq["Q3"]])
                fq["qf"] = [a]
                yield
                bk2 = r1.take()
                for g in range(8):
                    tr = P.put("tensor", lambda e, g=g: e.transpose(
                        PB[bk2][:, 128 * g:128 * g + 128], Q3[:, 2 * g:2 * g + 2, :].rearrange("p h c -> p (h c)"), idb[:, :]),
                        [a, bfree[bk2]] if g == 0 else (), sig=g == 7)
                fq["Q3"] = [tr]
                ev = P.put("scalar", lambda e: e.copy(q3T[t % 2], PB[bk2].rearrange("p (g n) -> p g n", g=8)),
                           [tr, fq["q3T"][t % 2], base])
                bfree[bk2] = [ev]
                S_[t]["q"] = ev

            units = [(t, h) for t in range(T) for h in range(H)]
            U_ = {}

            def u_scores(t, h):
                bk = r2.take()
                tk = P.put("tensor", lambda e: e.matmul(PS[bk][:, :], q3T[t % 2][:, h // 2, :], kM[:, h, :], start=True, stop=True),
                           [S_[t]["q"], kMw, zk, bfree[bk]])
                if h == H - 1:
                    fq["q3T"][t % 2] = [tk]
                mx = P.put("vector", lambda e: e.tensor_reduce(mm_[:, h:h + 1], PS[bk][:, :], AX, ALU.max),
                           [tk, fq["m"][h] if fq["m"] else (), base])
                U_[t, h] = [bk, mx]

            def u_exp(t, h):
                bk, mx = U_[t, h]
                i = n_e[0] % 4
                n_e[0] += 1
                a = P.put("vector", lambda e: e.tensor_scalar(
                    nb[:, h:h + 1], mm_[:, h:h + 1], nsq[t % 2][:, h:h + 1], LN255, ALU.mult, ALU.add),
                    [mx, S_[t]["nsq"], fq["nb"][h] if "nb" in fq else ()])
                fm = fq.setdefault("mlist", {})
                fm[h] = [a]
                fq["m"] = [fm.get(i_, []) for i_ in range(H)]
                ex = P.put("scalar", lambda e: e.activation(
                    ee[i], PS[bk][:, :], ACT.Exp, bias=nb[:, h:h + 1], scale=sq[t % 2][:, h:h + 1],
                    accum_out=se[t % 2][:, h:h + 1]), [a, fq["ee"][i], fq["se"][t % 2]])
                fn = fq.setdefault("nlist", {})
                fn[h] = [ex]
                fq["nb"] = [fn.get(i_, []) for i_ in range(H)]
                bfree[bk] = [ex, mx]
                if h == H - 1:
                    fq["sq"][t % 2] = [ex]
                U_[t, h] = [i, None, ex]

            def u_round(t, h):
                i, _, ex = U_[t, h]
                k = n_i[0] % 3
                n_i[0] += 1
                ro2 = P.put("vector", lambda e: e.tensor_scalar(ei[k], ee[i], MAGIC, MAGIC, ALU.add, ALU.subtract), [ex, fq["ei"][k]])
                fq["ee"][i] = [ro2]
                U_[t, h] = [k, ro2, ex]

            def u_tr(t, h):
                if h % 2 == 0:
                    U_["bank"] = r3.take()
                bk = U_["bank"]
                i, ro2, ex = U_[t, h]
                for c in range(4):
                    tr = P.put("tensor", lambda e, c=c: e.transpose(
                        PB[bk][:, 512 * (h % 2) + 128 * c:512 * (h % 2) + 128 * c + 128], ei[i][:, 128 * c:128 * c + 128], idb[:, :]),
                        [ro2, bfree[bk] if h % 2 == 0 else ()], sig=c == 3)
                fq["ei"][i] = [tr]
                if h % 2 == 1:
                    i2 = n_a[0] % 2
                    n_a[0] += 1
                    ev = P.put("scalar", lambda e: e.copy(aT[i2], PB[bk]), [tr, fq["aT"][i2], base])
                    bfree[bk] = [ev]
                    U_["a", t, h // 2] = (i2, ev)

            def u_pv(t, hp):
                i2, ev = U_["a", t, hp]
                for h in (2 * hp, 2 * hp + 1):
                    for c in range(4):
                        pv = P.put("tensor", lambda e, h=h, c=c: e.matmul(
                            PS[bO][:, 16 * h:16 * h + 16], aT[i2][:, 512 * (h % 2) + 128 * c:512 * (h % 2) + 128 * c + 128],
                            Vq[:, c, 16 * h:16 * h + 16], start=h == 0 and c == 0, stop=c == 3, skip_group_check=True),
                            [ev, tV, bfree[bO] if h == 0 else ()], sig=c == 3 and h % 2 == 1)
                fq["aT"][i2] = [pv]
                if hp == 7:
                    d = done(t, pv)
                    next(d)
                    bg.append(d)

            def done(t, pv):
                ex = U_[t, H - 1][2]
                r = P.put("vector", lambda e: e.reciprocal(rs_, se[t % 2]), [ex, fq["rs"]])
                fq["se"][t % 2] = [r]
                o = P.put("vector", lambda e: e.tensor_tensor(
                    On.rearrange("p (h d) -> p h d", d=16), PS[bO][:, 0:256].rearrange("p (h d) -> p h d", d=16),
                    bc(rs_, 2, 16), ALU.mult), [r, pv, fq["On"]])
                fq["rs"] = [o]
                bfree[bO] = [o]
                xa = P.put("gpsimd", lambda e: e.tensor_tensor(x[:, t, :], x[:, t, :], bp1, ALU.add), [xt[t], gt, xnT_wr[t]])
                yield
                bk = r1.take()
                for k in range(2):
                    tr = P.put("tensor", lambda e, k=k: e.transpose(
                        PS[bk][:, 128 * k:128 * k + 128], On[:, 128 * k:128 * k + 128], idf[:, :]),
                        [o, bfree[bk]] if k == 0 else (), sig=k == 1)
                fq["On"] = [tr]
                yield
                for k in range(2):
                    ev = P.put("vector", lambda e, k=k: e.tensor_scalar(
                        OnT[:, k, :], PS[bk][:, 128 * k:128 * k + 128], sv[:, k:k + 1], None, ALU.mult), [tr, fq["OnT"]])
                bfree[bk] = [ev]
                yield
                bk2 = r1.take()
                mo = mms(PS[bk2][:, 0:256], [(OnT[:, k, :], wp1[:, k, :]) for k in range(2)], [ev, bfree[bk2]])
                fq["OnT"] = [mo]
                yield
                xt[t] = P.put("vector", lambda e: e.tensor_tensor(x[:, t, :], x[:, t, :], PS[bk2][:, 0:256], ALU.add), [mo, xa])
                bfree[bk2] = [xt[t]]

            bg = []

            def step(n=1):
                while n and bg:
                    if next(bg[0], "end") == "end":
                        bg.pop(0)
                    n -= 1

            layernorm(0, r1)
            for _ in queries(0):
                pass
            N = len(units)
            for i in range(N + 7):
                if i < N:
                    t, h = units[i]
                    if h == 0:
                        step(99)
                        if t + 1 < T:
                            bg.append(queries(t + 1))
                    if h == 8 and t % 2 == 0 and t + 2 < T:
                        bg.append(layernorm_steps(t // 2 + 1, r1))
                    u_scores(t, h)
                if 1 <= i <= N:
                    u_exp(*units[i - 1])
                if 3 <= i <= N + 2:
                    u_round(*units[i - 3])
                if 4 <= i <= N + 3:
                    u_tr(*units[i - 4])
                if i >= 7 and units[i - 7][1] % 2 == 1:
                    u_pv(units[i - 7][0], units[i - 7][1] // 2)
                step()
            step(99)
            prev["wk"] = [xt[t] for t in range(T)] + fq["q3T"][0] + fq["q3T"][1] + fq["OnT"]

        def out_all():
            go = P.group("out")
            od = out.rearrange("(t p) d -> p t d", p=128)
            for t in range(T):
                P.dma("sync", go, od[:, t, :], x[:, t, :], [xt[t]])
            P.wait("sync", [P.landed(go)])

        attn_phase(0)
        P.dma("sync", gm0, win0[:, 1, 4096:8192], win_d[:, 1, 4096:8192], [prev["wk"]])
        P.dma("sync", gm0, wout0, I["w_out0"].rearrange("(c p) n -> p c n", p=128))
        if upto >= 2:
            cross0()
        if upto >= 3:
            fU = experts(0)
            gm1 = P.group("m1")
            we1 = W[:, 0:4096].rearrange("p (k n) -> p k n", k=2)
            we3 = W[:, 4096:8192].rearrange("p (k n) -> p k n", k=2)
            we2 = W[:, 8192:12288].rearrange("p (c n) -> p c n", c=16)
            ws13 = W[:, 12288:14336].rearrange("p (k n) -> p k n", k=2)
            ws2 = W[:, 14336:15360].rearrange("p (c n) -> p c n", c=4)
            wr1 = W[:, 15360:15392].rearrange("p (k n) -> p k n", k=2)
            kMt = W[:, 19616:23712].bitcast(BF).rearrange("p (h n) -> p h n", h=H)
            P.dma("sync", gm1, we1, I["we1"].rearrange("(k p) n -> p k n", p=128), fU)
            P.dma("sync", gm1, we3, I["we3"].rearrange("(k p) n -> p k n", p=128))
            P.dma("sync", gm1, we2, I["we2"].rearrange("(c p) n -> p c n", p=128))
            P.dma("sync", gm1, ws13, I["ws13"].rearrange("(k p) n -> p k n", p=128))
            P.dma("sync", gm1, ws2, I["ws2"].rearrange("(c p) n -> p c n", p=128))
            P.dma("sync", gm1, wr1, I["w_r1"].rearrange("(k p) n -> p k n", p=128))
            o = 15392
            wq1 = W[:, o:o + 512].rearrange("p (k n) -> p k n", k=2)
            wkv = W[:, o + 512:o + 1536].rearrange("p (k n) -> p k n", k=2)
            wp1 = W[:, o + 1536:o + 2048].rearrange("p (k n) -> p k n", k=2)
            bq1, bkv, bp1 = W[:, o + 2048:o + 2304], W[:, o + 2304:o + 2816], W[:, o + 2816:o + 3072]
            P.dma("sync", gat1, wA[1], I["w_att1"].rearrange("(k p) n -> p k n", p=128))
            P.dma("sync", gat1, bA[1], bcast(I["b_att1"]))
            P.dma("sync", gx1, wq1, I["w_q1"].rearrange("(k p) n -> p k n", p=128))
            P.dma("sync", gx1, wkv, I["w_kv1"].rearrange("(k p) n -> p k n", p=128))
            P.dma("sync", gx1, wp1, I["w_p1"].rearrange("(k p) n -> p k n", p=128))
            for v, n in ((bq1, "b_q1"), (bkv, "b_kv1"), (bp1, "b_p1")):
                P.dma("sync", gx1, v, bcast(I[n]))
        if upto >= 4:
            attn_phase(1)
        if upto >= 5:
            cross1()
        if upto >= 6:
            experts(1)
        out_all()
        for g in P.groups:
            if g[2]:
                P.wait("sync", [P.landed(g)])
        P.emit()


def constants():
    i = np.arange(128)
    sq = np.zeros((128, 384), np.float32)
    sq[:, 0:128] = np.eye(128)
    sq[:, 128:256] = np.where(i[None, :] > i[:, None], -1e30, 0.0)
    sq[:, 256:384] = np.where(i[:, None] > i[None, :], -1e30, 0.0)
    E = np.zeros((48, H, 128), np.float32)
    for h in range(H):
        for c in range(3):
            E[16 * c + h, h, :] = 1.0

    def part(v):
        out, r = [], v.astype(np.float32)
        for _ in range(3):
            b = r.view(np.uint32)
            b = ((b + 0x7FFF + ((b >> 16) & 1)) & 0xFFFF0000).astype(np.uint32).view(np.float32)
            out.append(b)
            r = (r - b).astype(np.float32)
        return out

    start = 2.0 ** (-8.0 / H)
    slopes = np.array([start * start ** h for h in range(H)], np.float32) * np.float32(4)
    ali = np.zeros((128, 2, 2, H, 32), np.float32)
    for j in range(2):
        pos = (128 * j + i).astype(np.float32)
        for c in range(3):
            ali[:, 0, j, :, c] = 1.0
            ali[:, 0, j, :, 3 + c] = pos[:, None]
            ali[:, 1, j, :, c] = part(slopes[None, :] * pos[:, None])[c]
            ali[:, 1, j, :, 3 + c] = -part(slopes)[c][None, :]
    return {"c_sq": sq, "c_E": E.reshape(48, H * 128), "c_ali": ali.reshape(128, 2048)}


_OUT = ((2048, 256), "float32")


def layout(inp):
    c = np.ascontiguousarray
    cat = np.concatenate
    a = {k: np.asarray(v) for k, v in inp.items()}
    m = {"x": c(a["x"].reshape(2048, 256))}
    m["w_att0"] = cat([a["L0_attn_wq"], a["L0_attn_wk"], a["L0_attn_wv"]], 1)
    m["b_att0"] = cat([a["L0_attn_bq"], a["L0_attn_bk"], a["L0_attn_bv"]])
    m["w_o0"], m["b_o0"] = a["L0_attn_wo"], a["L0_attn_bo"]
    m["w_xa0"] = cat([a[f"L0_xattn_{n}"].T for n in ("wq", "wk", "wv", "wo")], 1)
    ctx = a["ctx_2048"]
    m["ctxT"] = c(ctx.reshape(512, 256).T)
    m["ctxN"] = c(ctx.transpose(1, 0, 2))
    m["w_in0"] = c(a["L0_ffn_w_in"].transpose(2, 0, 1).reshape(256, 8192))
    m["w_out0"] = c(a["L0_ffn_w_out"].transpose(0, 2, 1).reshape(4096, 256))
    m["w_r0"] = c(a["L0_ffn_router_weight"].T)
    m["b_m0"] = a["L0_ffn_bias"]
    flat = lambda w: w.transpose(1, 0, 2).reshape(256, -1)
    m["w_att1"] = cat([flat(a[f"L1_attn_W{n}"]) for n in "qkv"], 1)
    m["b_att1"] = cat([a[f"L1_attn_b{n}"].reshape(-1) for n in "qkv"])
    m["w_q1"], m["w_kv1"], m["w_p1"] = a["L1_xattn_Wq"], a["L1_xattn_Wkv"], a["L1_xattn_Wp"]
    m["b_q1"], m["b_kv1"], m["b_p1"] = a["L1_xattn_bq"], a["L1_xattn_bkv"], a["L1_xattn_bp"]
    m["we1"], m["we3"] = c(flat(a["L1_ffn_we1"])), c(flat(a["L1_ffn_we3"]))
    m["we2"] = a["L1_ffn_we2"].reshape(2048, 256)
    m["ws13"] = cat([a["L1_ffn_ws1"], a["L1_ffn_ws3"]], 1)
    m["ws2"] = a["L1_ffn_ws2"]
    m["w_r1"] = a["L1_ffn_w_router"]
    m.update(constants())
    return {k: c(v) for k, v in m.items()}


def kernel(**inputs):
    import concourse.bacc as _bacc
    from concourse.bass_utils import run_bass_kernel_spmd as _run

    nc = _bacc.Bacc("TRN2", target_bir_lowering=False, num_devices=1)
    arrays = layout(inputs)
    I = {k: nc.dram_tensor(f"in_{k}", v.shape, mybir.dt.from_np(v.dtype), kind="ExternalInput").ap()
         for k, v in arrays.items()}
    out = nc.dram_tensor("out_0", _OUT[0], F32, kind="ExternalOutput").ap()
    decoder(nc, I, out)
    r = _run(nc, [{f"in_{k}": v for k, v in arrays.items()}], core_ids=[0])
    return r.results[0]["out_0"].reshape(8, 256, 256)
```

```python
from contextlib import ExitStack

import numpy as np

import concourse.bass as bass
from concourse import mybir

F32 = mybir.dt.float32
BF = mybir.dt.bfloat16
I32 = mybir.dt.int32
ALU = mybir.AluOpType
ACT = mybir.ActivationFunctionType
AX = mybir.AxisListType.X
MAGIC = 12582912.0
BIG = 3.0e38
LN255 = float(np.log(255.0))

B, S, D, H, T = 8, 256, 256, 16, 16
POS = ((0, 3, 5), (1, 4), (2,))


class Prog:

    ENG = ("tensor", "vector", "scalar", "gpsimd", "sync")

    def __init__(self, nc, ctx):
        self.nc, self.ctx = nc, ctx
        self.q = {e: [] for e in self.ENG}
        self.sem = {e: ctx.enter_context(nc.semaphore("s_" + e)) for e in self.ENG}
        self.count = {e: 0 for e in self.ENG}
        self.seen = {e: {} for e in self.ENG}
        self.groups = []

    def wait(self, e, after):
        for t in after:
            if not t:
                continue
            if type(t) is list:
                self.wait(e, t)
                continue
            name, s, v = t
            if self.seen[e].get(name, 0) < v:
                self.seen[e][name] = v
                self.q[e].append(lambda eng, s=s, v=v: eng.wait_ge(s, v))

    def put(self, e, fn, after=(), sig=True):
        self.wait(e, after)
        if not sig:
            self.q[e].append(fn)
            return None
        self.count[e] += 1
        s = self.sem[e]
        self.q[e].append(lambda eng: fn(eng).then_inc(s, 1))
        return (e, s, self.count[e])

    def group(self, name):
        g = [name, self.ctx.enter_context(self.nc.semaphore("d_" + name)), 0]
        self.groups.append(g)
        return g

    def dma(self, e, g, out, in_, after=()):
        self.wait(e, after)
        g[2] += 16
        s = g[1]
        self.q[e].append(lambda eng: eng.dma_start(out, in_).then_inc(s, 16))

    def landed(self, g):
        return (g[0], g[1], g[2])

    def emit(self):
        with self.nc.Block() as block:
            def body(e):
                def run(eng):
                    for f in self.q[e]:
                        f(eng)
                return run
            block.tensor(body("tensor"))
            block.vector(body("vector"))
            block.scalar(body("scalar"))
            block.gpsimd(body("gpsimd"))
            block.sync(body("sync"))


def bc(ap, dim, n):
    shape = list(ap.shape)
    ix = tuple(slice(None) for _ in range(dim)) + (None,)
    return ap[ix].to_broadcast(shape[:dim] + [n] + shape[dim:])


def decoder(nc, I, out, upto=6):
    with ExitStack() as ctx:
        P = Prog(nc, ctx)

        def sb(name, shape, dt=F32):
            return ctx.enter_context(nc.sbuf_tensor(name, shape, dt))

        PS = [ctx.enter_context(nc.psum_tensor(f"ps{i}", [128, 512], F32)) for i in range(8)]
        PB = [p[:, :].bitcast(BF) for p in PS]
        bfree = [[] for _ in range(8)]
        taken = [None] * 8

        class Ring:
            def __init__(self, banks):
                self.banks, self.n = banks, 0

            def take(self):
                b = self.banks[self.n % len(self.banks)]
                self.n += 1
                assert bfree[b] is not taken[b], "the bank is still in use"
                taken[b] = bfree[b]
                return b

        x = sb("x", [128, T, D])
        xnT = sb("xnT", [128, 2, T * 128])
        xn = sb("xn", [128, 2, D])
        st = sb("st", [128, T, 6])
        mv = sb("mv", [128, T, 2])
        ve = sb("ve", [128, T])
        rstd = sb("rstd", [128, T])
        half = sb("half", [128, 1])
        upb = sb("upb", [128, 128], BF)
        oneb = sb("oneb", [128, 128], BF)
        lastb = sb("lastb", [128, 16], BF)
        slots = sb("slots", [128, 80])
        idf = sb("idf", [128, 128])
        idb = sb("idb", [128, 128], BF)
        maskQ = sb("maskQ", [128, 128], BF)
        maskK = sb("maskK", [128, 128], BF)
        E = sb("E", [48, H, 128], BF)
        W = sb("W", [128, 24576])
        ctxT = sb("ctxT", [128, 2, 512])
        ctxNw = sb("ctxN", [128, 8 * D])
        ctxN = ctxNw[0:64, :].rearrange("p (b d) -> p b d", b=8)
        work = sb("work", [128, 9700])
        wof = [0]

        def wk(n, dt=F32):
            a = wof[0]
            wof[0] += n
            assert wof[0] <= 9700, wof[0]
            v = work[:, a:a + n]
            return v if dt is F32 else v.bitcast(dt)

        gx = [P.group(f"x{i}") for i in range(4)]
        gc, gw0, gb = P.group("c"), P.group("w0"), P.group("b")
        xd = I["x"].rearrange("(t p) d -> p t d", p=128)
        P.dma("sync", gx[0], x[:, 0:4, :], xd[:, 0:4, :])
        SM = sb("SM", [128, 5392])
        so = [0]

        def small(name, g, shape, src, e="sync"):
            n = int(np.prod(shape))
            a = so[0]
            so[0] += n
            assert so[0] <= 5392
            P.dma(e, g, SM[:, a:a + n].rearrange("p (a b) -> p a b", b=shape[-1]) if len(shape) == 2 else SM[:, a:a + n], src)
            v = SM[:, a:a + n]
            return v.rearrange("p (a b) -> p a b", b=shape[-1]) if len(shape) == 2 else v

        def bcast(v):
            return bass.AP(v.tensor, v.offset, [[0, 128]] + [list(p) for p in v.ap])

        def weight(name, g, n):
            return small(name, g, [2, n], I[name].rearrange("(k p) n -> p k n", p=128))

        xf = W[:, 512:4608]
        gali, go0 = P.group("ali"), P.group("o0")
        P.dma("sync", gc, W[:, 0:512], I["c_sq"])
        wA = [weight("w_att0", gw0, 768)]
        bA = [small("b_att0", gb, [768], bcast(I["b_att0"]))]
        P.dma("sync", gali, xf[:, 0:2048], I["c_ali"])
        P.dma("sync", gali, xf[0:48, 2048:4096], I["c_E"])
        for i in range(1, 4):
            P.dma("sync", gx[i], x[:, 4 * i:4 * i + 4, :], xd[:, 4 * i:4 * i + 4, :])
        wo0 = weight("w_o0", go0, 256)
        bo0 = small("b_o0", go0, [256], bcast(I["b_o0"]))

        z0 = P.put("vector", lambda e: e.memset(half[:, :], -0.5))
        tid = P.put("vector", lambda e: e.tensor_copy(idf[:, :], W[:, 0:128]), [P.landed(gc)])
        P.put("vector", lambda e: e.tensor_copy(idb[:, :], W[:, 0:128]))
        P.put("vector", lambda e: e.tensor_copy(maskQ[:, :], W[:, 128:256]))
        P.put("vector", lambda e: e.tensor_copy(maskK[:, :], W[:, 256:384]))
        P.put("vector", lambda e: e.tensor_copy(upb[:, :], W[:, 384:512]))
        P.put("vector", lambda e: e.memset(oneb[:, :], 1.0))
        zt256, sloti = work[:, 9444:9700], work[:, 9364:9444].bitcast(I32)
        tsl = P.put("gpsimd", lambda e: e.iota(sloti, pattern=[[1, 80]], base=0, channel_multiplier=0))
        t_up = P.put("vector", lambda e: e.tensor_copy(slots[:, :], sloti), [tsl])
        t_ali = P.landed(gali)

        gxa = P.group("xa")
        wxa = weight("w_xa0", gxa, 1024)
        P.dma("sync", gxa, ctxT[:, :, :], I["ctxT"].rearrange("(k p) n -> p k n", p=128))
        P.dma("sync", gxa, ctxN, I["ctxN"])
        wr0 = weight("w_r0", gxa, 8)
        gm0 = P.group("m0")
        win0 = W[:, 0:16384].rearrange("p (k n) -> p k n", k=2)
        wout0 = W[:, 16384:24576].rearrange("p (c n) -> p c n", c=32)
        wout0f = W[:, 16384:24576]
        win_d = I["w_in0"].rearrange("(k p) n -> p k n", p=128)
        bm0 = small("b_m0", gm0, [256], bcast(I["b_m0"]))
        XS = nc.dram_tensor("xs_scratch", (79 * 128, D), F32, kind="Internal").ap()
        YS = nc.dram_tensor("ys_scratch", (79 * 128, D), F32, kind="Internal").ap()
        gf = P.group("fill")
        zf = P.put("vector", lambda e: e.memset(zt256, 0.0))
        for i in range(0, 79, 16):
            n = min(16, 79 - i)
            P.dma("sync", gf, XS[128 * i:128 * (i + n), :].rearrange("(n p) d -> p n d", p=128), bc(zt256, 1, n), [zf])
        t_fill = P.landed(gf)
        gat1 = P.group("at1")
        wA.append(W[:, 18464:19232].rearrange("p (k n) -> p k n", k=2))
        bA.append(W[:, 19232:19616])
        gx1 = P.group("cr1")

        xt = [P.landed(gx[t // 4]) for t in range(T)]
        xnT_rd = [[] for _ in range(T)]
        xnT_wr = [None] * T
        xn_rd = [None, None]
        xall_wr, lg_wr = [], []
        gm1_ = P.group("m1r")
        wr1 = W[:, 15360:15392].rearrange("p (k n) -> p k n", k=2)
        XL = [(xv.rearrange("p (t n) -> p t n", t=T), lv.rearrange("p (t n) -> p t n", t=T)) for xv, lv in
              ((work[:, 5604:9700], work[:, 5476:5604]), (W[:, 19616:23712], ctxNw[:, 1608:1864]))]
        prev_y = {"ys": []}
        prev = {"wk": []}
        kv_ = {}
        beside = []
        rows = {}

        def tick(n=1):
            while n and beside:
                if next(beside[0], "end") == "end":
                    beside.pop(0)
                n -= 1

        def layernorm_steps(pair, ring, keep=None):
            a2 = []
            for t in (2 * pair, 2 * pair + 1):
                a = P.put("vector", lambda e, t=t: e.bn_stats(st[:, t, :], x[:, t, :]), [xt[t]])
                a = P.put("vector", lambda e, t=t: e.bn_aggr(mv[:, t, :], st[:, t, :]), [a])
                a1 = P.put("vector", lambda e, t=t: e.tensor_scalar(ve[:, t:t + 1], mv[:, t, 1:2], 1e-5, None, ALU.add), [a])
                a2.append(P.put("gpsimd", lambda e, t=t: e.tensor_tensor(rstd[:, t:t + 1], ve[:, t:t + 1], half[:, :], ALU.pow), [a1, z0]))
            yield
            a3, src = [], []
            for j in (0, 1):
                t = 2 * pair + j
                xo = keep[:, t, :] if keep is not None else xn[:, j, :]
                src.append(xo)
                a3.append(P.put("vector", lambda e, t=t, xo=xo: e.tensor_scalar(
                    xo, x[:, t, :], mv[:, t, 0:1], rstd[:, t:t + 1], ALU.subtract, ALU.mult),
                    [a2[j], a1, xn_rd[j], prev["wk"] if keep is not None else None]))
            yield
            b = ring.take()
            for j in (0, 1):
                for k in (0, 1):
                    a4 = P.put("tensor", lambda e, j=j, k=k: e.transpose(
                        PS[b][:, 256 * k + 128 * j:256 * k + 128 * j + 128], src[j][:, 128 * k:128 * k + 128], idf[:, :]),
                        [a3[j], tid, bfree[b]])
                xn_rd[j] = a4
            xall_wr[:] = a3
            a5 = P.put("scalar", lambda e: e.copy(
                xnT[:, :, 256 * pair:256 * pair + 256], PS[b][:, :].rearrange("p (k n) -> p k n", k=2)),
                [a4, xnT_rd[2 * pair], xnT_rd[2 * pair + 1]])
            bfree[b] = [a5]
            for t in (2 * pair, 2 * pair + 1):
                xnT_wr[t], xnT_rd[t] = a5, []

        def routed(L, pair, ring):
            xall, Lg = XL[L]
            yield from layernorm_steps(pair, ring, xall)
            NE = 8 if L == 0 else 16
            w, gw = (wr0, P.landed(gxa)) if L == 0 else (wr1, P.landed(gm1_))
            yield
            bk = ring.take()
            for j in (0, 1):
                t = 2 * pair + j
                tk = mms(PS[bk][:, NE * j:NE * j + NE], [(xnT[:, k, 128 * t:128 * t + 128], w[:, k, :]) for k in range(2)],
                         [xnT_wr[t], gw, bfree[bk]])
                xnT_rd[t] = [tk]
            ev = P.put("scalar", lambda e: e.copy(
                Lg[:, 2 * pair:2 * pair + 2, :], PS[bk][:, 0:2 * NE].rearrange("p (j e) -> p j e", j=2)), [tk, prev["wk"]])
            bfree[bk] = [ev]
            lg_wr.append(ev)

        def layernorm(pair, ring):
            for _ in layernorm_steps(pair, ring):
                pass

        def mms(out_, pairs, after, start=True, **kw):
            n = len(pairs)
            for i, (l, r) in enumerate(pairs):
                tok = P.put("tensor", lambda e, l=l, r=r, i=i: e.matmul(
                    out_, l, r, start=start and i == 0, stop=i == n - 1, skip_group_check=True),
                    after if i == 0 else (), sig=i == n - 1)
            return tok

        def attn_phase(L):
            wof[0] = 0
            NK = 16 if L == 0 else 4
            per = H // NK
            NW = 768 if L == 0 else 384
            NR = H + NK
            QK = NR * 16
            Wt, bias = wA[L], bA[L]
            wtok = [P.landed(gw0), P.landed(gb)] if L == 0 else [P.landed(gat1)]
            base = prev["wk"]
            wo_ = [12288 if L == 0 else 19616]

            def wb(n, h):
                a = wo_[0]
                wo_[0] += n * h // 2
                return W[:, a:a + n * h // 2].bitcast(BF).rearrange("p (h c) -> p h c", h=h)

            if L == 0:
                R = [wb(128, NR) for _ in range(2)]
            else:
                R = [wk(NR * 64, BF).rearrange("p (h c) -> p h c", c=128) for _ in range(2)]
            qs = [wb(256, H) for _ in range(2)]
            ks = [wb(256, NK) if L == 0 or i == 0 else wk(NK * 128, BF).rearrange("p (h c) -> p h c", h=NK) for i in range(2)]
            qkf = [wk(512) for _ in range(2)]
            Vt = [[wk(NK * 32).rearrange("p (h c) -> p h c", c=32) for _ in range(2)] for _ in range(2)]
            m = wk(32).rearrange("p (j h) -> p j h", j=2)
            mr = wk(32).rearrange("p (j h) -> p j h", j=2)
            NP = wk(48, BF).rearrange("p (j c h) -> p j c h", j=2, c=3)
            mT = wk(128, BF)[0:48, :]
            PT = [wk(512) for _ in range(6)]
            OT = wk(1024).rearrange("p (g n) -> p g n", g=4)
            rc = [wk(16) for _ in range(2)]
            On = [wk(256) for _ in range(2)]
            OnT = [wk(256).rearrange("p (k n) -> p k n", k=2) if L == 0 else None for _ in range(2)]
            rp = Ring([0, 1, 6])
            rs = Ring([2, 3, 4, 5])
            ro = Ring([7])
            if L == 0:
                layernorm(0, rp)
            zt = []
            for j in range(2):
                z = P.put("vector", lambda e, j=j: e.memset(R[j][:, :, 96:128], 0.0), base)
                zt.append(z)
                if L == 0:
                    zt.append(P.put("vector", lambda e, j=j: e.tensor_copy(
                        R[j][:, 0:16, 96:128], xf[:, 512 * j:512 * j + 512].rearrange("p (h c) -> p h c", c=32)), [z, t_ali]))
                    zt.append(P.put("vector", lambda e, j=j: e.tensor_copy(
                        R[j][:, 16:32, 96:128], xf[:, 1024 + 512 * j:1536 + 512 * j].rearrange("p (h c) -> p h c", c=32)), [z]))
                for i in range(2):
                    z2 = P.put("gpsimd", lambda e, i=i, j=j: e.memset(Vt[i][j], 0.0), base)
                    zt.append(P.put("gpsimd", lambda e, i=i, j=j: e.memset(Vt[i][j][:, :, 16:17], 1.0), [z2]))
            if L == 0:
                zt.append(P.put("vector", lambda e: e.tensor_copy(
                    E[:, :, :], xf[0:48, 2048:4096].rearrange("p (h k) -> p h k", h=H))))
                P.dma("sync", gm0, win0[:, 0, :], win_d[:, 0, :], zt)
                P.dma("sync", gm0, win0[:, 1, 0:4096], win_d[:, 1, 0:4096])
            st_ = {"m": [], "NP": [], "mT": [], "PT": [[] for _ in PT], "OT": [], "On": [[], []], "OnT": [[], []],
                   "R": [[], []], "qs": [[], []], "V": [[[], []], [[], []]], "rc": [[], []], "qkf": [[], []]}
            nPT = [0]
            S_ = [dict() for _ in range(B)]

            def proj(b, j):
                t = 2 * b + j
                lh = [xnT[:, k, 128 * t:128 * t + 128] for k in range(2)]
                ba = rp.take()
                qk = mms(PS[ba][:, 0:min(NW, 512)], [(lh[k], Wt[:, k, 0:min(NW, 512)]) for k in range(2)],
                         [xnT_wr[t], wtok, bfree[ba]])
                if L == 0:
                    bb = rp.take()
                    vv = mms(PS[bb][:, 0:256], [(lh[k], Wt[:, k, 512:768]) for k in range(2)], [bfree[bb]])
                    S_[b]["pj", j] = (ba, qk, bb, vv, PS[bb][:, 0:256], 512)
                else:
                    vv = qk
                    S_[b]["pj", j] = (ba, qk, ba, vv, PS[ba][:, QK:NW], QK)
                xnT_rd[t] = [vv]

            def split_a(b, j):
                ba, qk, bb, vv, vp, vo = S_[b]["pj", j]
                f = qkf[j]
                a = P.put("vector", lambda e: e.tensor_tensor(f[:, 0:QK], PS[ba][:, 0:QK], bias[:, 0:QK], ALU.add),
                          [qk, wtok, st_["qkf"][j], base])
                v = P.put("vector", lambda e: e.tensor_tensor(
                    Vt[b % 2][j][:, :, 0:16], vp.rearrange("p (h d) -> p h d", d=16),
                    bias[:, vo:vo + NK * 16].rearrange("p (h d) -> p h d", d=16), ALU.add),
                    [vv, zt, st_["V"][b % 2][j]])
                bfree[ba] = [a, v]
                bfree[bb] = [a, v]
                S_[b]["V", j] = v
                R6 = R[j][:, :, 0:96].rearrange("p h (c d) -> p h c d", d=16)
                f3 = f[:, 0:QK].rearrange("p (h d) -> p h d", d=16)
                c1 = P.put("scalar", lambda e: e.copy(R6[:, :, 0, :], f3), [a, st_["R"][j], zt])
                S_[b]["c1", j] = c1

            def split_b(b, j):
                R6 = R[j][:, :, 0:96].rearrange("p h (c d) -> p h c d", d=16)
                f3 = qkf[j][:, 0:QK].rearrange("p (h d) -> p h d", d=16)
                c1 = S_[b]["c1", j]
                r1 = P.put("vector", lambda e: e.tensor_tensor(f3, f3, R6[:, :, 0, :], ALU.subtract), [c1])
                c2 = P.put("scalar", lambda e: e.copy(R6[:, :, 4, :], f3), [r1])
                w = [c1, c2]
                w.append(P.put("vector", lambda e: e.tensor_copy(R6[:, 0:16, 3:6:2, :], bc(R6[:, 0:16, 0, :], 2, 2)), [c1]))
                w.append(P.put("vector", lambda e: e.tensor_copy(R6[:, 16:NR, 1:3, :], bc(R6[:, 16:NR, 0, :], 2, 2))))
                S_[b]["w", j] = w

            def split_c(b, j):
                R6 = R[j][:, :, 0:96].rearrange("p h (c d) -> p h c d", d=16)
                f3 = qkf[j][:, 0:QK].rearrange("p (h d) -> p h d", d=16)
                w = S_[b]["w", j]
                c2 = w[1]
                w.append(P.put("gpsimd", lambda e: e.tensor_copy(R6[:, 0:16, 1, :], R6[:, 0:16, 4, :]), [c2]))
                w.append(P.put("gpsimd", lambda e: e.tensor_copy(R6[:, 16:NR, 3, :], R6[:, 16:NR, 4, :])))
                w.append(P.put("vector", lambda e: e.tensor_tensor(R6[:, 0:16, 2, :], f3[:, 0:16, :], R6[:, 0:16, 4, :], ALU.subtract), [c2]))
                w.append(P.put("vector", lambda e: e.tensor_tensor(R6[:, 16:NR, 5, :], f3[:, 16:NR, :], R6[:, 16:NR, 4, :], ALU.subtract)))
                st_["qkf"][j] = [w[-1], w[-2]]
                S_[b]["R", j] = w

            def stack(b, j, parts=(0, 1)):
                tk, rd = ([], []) if parts[0] == 0 else (S_[b]["qs", j], st_["R"][j])
                for h0, dst, n in [((0, qs, H), (H, ks, NK))[p_] for p_ in parts]:
                    for c in range(0, n, 8):
                        m_ = min(8, n - c)
                        bk = rp.take()
                        for h in range(m_):
                            tr = P.put("tensor", lambda e, c=c, h=h, bk=bk, h0=h0: e.transpose(
                                PB[bk][:, 128 * h:128 * h + 128], R[j][:, h0 + c + h, :], idb[:, :]),
                                [S_[b]["R", j], bfree[bk]] if h == 0 else (), sig=h == m_ - 1)
                        rd.append(tr)
                        src = PB[bk][:, 0:128 * m_].rearrange("p (h n) -> p h n", h=m_)
                        dd = dst[b % 2][:, c:c + m_, 128 * j:128 * j + 128]
                        if c == 0:
                            ev = P.put("scalar", lambda e, dd=dd, src=src: e.copy(dd, src), [tr, st_["qs"][b % 2]])
                        else:
                            ev = P.put("vector", lambda e, dd=dd, src=src: e.tensor_copy(dd, src), [tr, st_["qs"][b % 2]])
                        bfree[bk] = [ev]
                        tk.append(ev)
                st_["R"][j] = rd
                S_[b]["qs", j] = tk

            def scores(b, j):
                q, k_ = qs[b % 2], ks[b % 2]
                n = 4 if j == 0 else 2
                w_ = 512 // n
                for h0 in range(0, H, n):
                    bk = rs.take()
                    for i in range(n):
                        h = h0 + i
                        P.put("tensor", lambda e, h=h, i=i, bk=bk: e.matmul(
                            PS[bk][:, w_ * i:w_ * i + w_], q[:, h, 128 * j:128 * j + 128], k_[:, h // per, 0:w_],
                            start=i == 0, stop=False, skip_group_check=True),
                            [S_[b]["qs", 0], S_[b]["qs", j], bfree[bk]] if i == 0 else (), sig=False)
                    ov = PS[bk][:, :].rearrange("p (i n) -> p i n", i=n)
                    mm = P.put("tensor", lambda e, ov=ov: e.matmul(
                        ov[:, :, w_ - 128:w_], idb[:, :], bc(maskQ[:, :], 1, n), start=False, stop=True,
                        skip_group_check=True))
                    mx = P.put("vector", lambda e, ov=ov, h0=h0: e.tensor_reduce(
                        m[:, j, h0:h0 + n], ov, AX, ALU.max), [mm, st_["m"], base])
                    bfree[bk] = [mx]
                if j == 0:
                    return
                a = P.put("vector", lambda e: e.tensor_scalar(NP[:, :, 0, :], m, -1.0, None, ALU.mult), [mx, st_["NP"]])
                a = P.put("vector", lambda e: e.scalar_tensor_tensor(
                    out=mr, in0=m, scalar=-1.0, in1=NP[:, :, 0, :], op0=ALU.mult, op1=ALU.subtract), [a])
                st_["m"] = [a]
                a2 = P.put("vector", lambda e: e.tensor_copy(NP[:, :, 1, :], mr), [a])
                a3 = P.put("vector", lambda e: e.tensor_tensor(NP[:, :, 2, :], mr, NP[:, :, 1, :], ALU.subtract), [a2])
                S_[b]["NP"] = a3

            def fold(b):
                bk = rp.take()
                for j in range(2):
                    tr = P.put("tensor", lambda e, j=j: e.transpose(
                        PB[bk][0:48, 128 * j:128 * j + 128], NP[:, j, :, :].rearrange("p c h -> p (c h)"), idb[:, :]),
                        [S_[b]["NP"], bfree[bk]] if j == 0 else (), sig=j == 1)
                st_["NP"] = [tr]
                ev = P.put("vector", lambda e: e.tensor_copy(mT, PB[bk][0:48, 0:256]), [tr, st_["mT"], base])
                bfree[bk] = [ev]
                S_[b]["mT"] = ev

            def attend_s(b, g):
                q, k_ = qs[b % 2], ks[b % 2]
                pts = []
                for kind in range(3):
                    bk = rs.take()
                    hs = [4 * g + 2 * kind, 4 * g + 2 * kind + 1] if kind < 2 else [4 * g + i for i in range(4)]
                    w_, kt, q0 = (256, 0, 0) if kind < 2 else (128, 1, 128)
                    for i, h in enumerate(hs):
                        P.put("tensor", lambda e, h=h, i=i, bk=bk, w_=w_, kt=kt, q0=q0: e.matmul(
                            PS[bk][:, w_ * i:w_ * i + w_], k_[:, h // per, 128 * kt:128 * kt + 128], q[:, h, q0:256],
                            start=i == 0, stop=False, skip_group_check=True),
                            [S_[b]["mT"], zt, bfree[bk]] if i == 0 else (), sig=False)
                        P.put("tensor", lambda e, h=h, i=i, bk=bk, w_=w_, q0=q0: e.matmul(
                            PS[bk][:, w_ * i:w_ * i + w_], E[0:48, h, :], mT[:, q0:256],
                            start=False, stop=False, skip_group_check=True), sig=False)
                    ov = PS[bk][:, :].rearrange("p (i n) -> p i n", i=len(hs))
                    mm = P.put("tensor", lambda e, ov=ov, n=len(hs): e.matmul(
                        ov[:, :, 0:128], idb[:, :], bc(maskK[:, :], 1, n), start=False, stop=True,
                        skip_group_check=True))
                    pi = nPT[0] % 6
                    nPT[0] += 1
                    ex = P.put("scalar", lambda e, pi=pi, bk=bk: e.activation(
                        PT[pi], PS[bk][:, :], ACT.Exp, scale=0.25), [mm, st_["PT"][pi], base])
                    bfree[bk] = [ex]
                    pts.append((pi, ex))
                if g == 3:
                    st_["qs"][b % 2] = [mm]
                    st_["mT"] = [mm]
                S_[b]["pts", g] = pts

            def attend_v(b, g):
                pts = S_[b]["pts", g]
                if g % 2 == 0:
                    S_[b]["bo"] = ro.take()
                bo = S_[b]["bo"]
                o0 = 256 * (g % 2)
                for i in range(4):
                    h = 4 * g + i
                    pi, ex = pts[i // 2]
                    P.put("tensor", lambda e, i=i, h=h, pi=pi: e.matmul(
                        PS[bo][32 * i:32 * i + 32, o0:o0 + 256], Vt[b % 2][0][:, h // per, :],
                        PT[pi][:, 256 * (i % 2):256 * (i % 2) + 256], start=True, stop=False, skip_group_check=True),
                        [ex, S_[b]["V", 0], S_[b]["V", 1], bfree[bo] if g % 2 == 0 else ()], sig=False)
                pi2, ex2 = pts[2]
                for i in range(4):
                    h = 4 * g + i
                    pv = P.put("tensor", lambda e, i=i, h=h: e.matmul(
                        PS[bo][32 * i:32 * i + 32, o0 + 128:o0 + 256], Vt[b % 2][1][:, h // per, :],
                        PT[pi2][:, 128 * i:128 * i + 128], start=False, stop=True, skip_group_check=True),
                        [ex2], sig=i == 3)
                for pi, _ in pts:
                    st_["PT"][pi] = [pv]
                if g % 2 == 1:
                    ev = P.put("scalar", lambda e: e.copy(
                        OT[:, g - 1:g + 1, :], PS[bo][:, :].rearrange("p (g n) -> p g n", g=2)), [pv, st_["OT"], base])
                    bfree[bo] = [ev]
                    S_[b]["OT", g] = ev
                if g == 3:
                    st_["V"][b % 2] = [[pv], [pv]]

            def fin1(b, j):
                t = 2 * b + j
                bk = rp.take()
                for g in range(4):
                    tr = P.put("tensor", lambda e, g=g: e.transpose(
                        PS[bk][:, 128 * g:128 * g + 128], OT[:, g, 128 * j:128 * j + 128], idf[:, :]),
                        [S_[b]["OT", 1], S_[b]["OT", 3], bfree[bk]] if g == 0 else (), sig=g == 3)
                ov = PS[bk][:, :].rearrange("p (h c) -> p h c", c=32)
                r = P.put("vector", lambda e: e.reciprocal(rc[j], ov[:, :, 16]), [tr, st_["rc"][j], base])
                o = P.put("vector", lambda e: e.tensor_tensor(
                    On[j].rearrange("p (h d) -> p h d", d=16), ov[:, :, 0:16], bc(rc[j], 2, 16), ALU.mult),
                    [r, st_["On"][j]])
                st_["rc"][j] = [o]
                bfree[bk] = [o]
                if L == 1:
                    xt[t] = P.put("gpsimd", lambda e: e.tensor_tensor(x[:, t, :], x[:, t, :], On[j], ALU.add),
                                  [o, xt[t], xnT_wr[t]])
                    st_["On"][j] = [xt[t]]
                if j == 1:
                    st_["OT"] = [tr]
                S_[b]["f1", j] = o

            def fin2(b, j):
                bk = rp.take()
                for k in range(2):
                    tr = P.put("tensor", lambda e, k=k: e.transpose(
                        PS[bk][:, 128 * k:128 * k + 128], On[j][:, 128 * k:128 * k + 128], idf[:, :]),
                        [S_[b]["f1", j], bfree[bk]] if k == 0 else (), sig=k == 1)
                st_["On"][j] = [tr]
                ev = P.put("scalar", lambda e: e.copy(OnT[j], PS[bk][:, 0:256].rearrange("p (k n) -> p k n", k=2)),
                           [tr, st_["OnT"][j], base])
                bfree[bk] = [ev]
                S_[b]["f2", j] = ev
                t = 2 * b + j
                S_[b]["xa", j] = P.put("gpsimd", lambda e: e.tensor_tensor(x[:, t, :], x[:, t, :], bo0, ALU.add),
                                       [xt[t], P.landed(go0), xnT_wr[t]])

            def fin3(b, j):
                t = 2 * b + j
                bk = rp.take()
                mo = mms(PS[bk][:, 0:256], [(OnT[j][:, k, :], wo0[:, k, :]) for k in range(2)], [S_[b]["f2", j], P.landed(go0), bfree[bk]])
                st_["OnT"][j] = [mo]
                xt[t] = P.put("vector", lambda e: e.tensor_tensor(
                    x[:, t, :], x[:, t, :], PS[bk][:, 0:256], ALU.add), [mo, S_[b]["xa", j]])
                bfree[bk] = [xt[t]]

            if L == 1:
                for t in range(4):
                    rows["fetch"](t)
                beside.append(cross1_kv(rp, fU + base))
                rows["add"](0)
                rows["add"](1)
                layernorm(0, rp)
            proj(0, 0)
            split_a(0, 0)
            proj(0, 1)
            split_b(0, 0)
            split_c(0, 0)
            split_a(0, 1)
            split_b(0, 1)
            stack(0, 0)
            split_c(0, 1)
            stack(0, 1)
            if L == 1:
                rows["add"](2)
                rows["add"](3)
                rows["fetch"](4)
                rows["fetch"](5)
                experts1_weights()
            layernorm(1, rp)
            for b in range(B + 1):
                n, f = b + 1 < B, b >= 1

                def fin(step, b=b, f=f):
                    if f and (L == 0 or step is fin1):
                        step(b - 1, 0)
                        step(b - 1, 1)
                if b == B:
                    for step in (fin1, fin2, fin3):
                        fin(step)
                    break
                if b == 0:
                    scores(0, 0)
                scores(b, 1)
                if L == 1:
                    fin(fin1)
                if n:
                    proj(b + 1, 0)
                fold(b)
                if n:
                    split_a(b + 1, 0)
                attend_s(b, 0)
                if L == 0:
                    fin(fin1)
                if n:
                    split_b(b + 1, 0)
                attend_s(b, 1)
                fin(fin2)
                tick(2)
                attend_v(b, 0)
                tick(2)
                if n:
                    split_c(b + 1, 0)
                    proj(b + 1, 1)
                if L == 1 and b + 2 < B:
                    rows["add"](2 * b + 4)
                    rows["add"](2 * b + 5)
                    if b + 3 < B:
                        rows["fetch"](2 * b + 6)
                        rows["fetch"](2 * b + 7)
                ln = layernorm_steps((b + 2) % B, rp)
                next(ln)
                attend_s(b, 2)
                if n:
                    split_a(b + 1, 1)
                tick()
                attend_v(b, 1)
                next(ln)
                tick()
                fin(fin3)
                if n:
                    split_b(b + 1, 1)
                attend_s(b, 3)
                tick()
                next(ln, None)
                if n:
                    split_c(b + 1, 1)
                    stack(b + 1, 0, (0,))
                attend_v(b, 2)
                if n:
                    stack(b + 1, 0, (1,))
                    stack(b + 1, 1, (0,))
                tick()
                if n:
                    scores(b + 1, 0)
                    stack(b + 1, 1, (1,))
                attend_v(b, 3)
                tick()
            tick(999)
            prev["wk"] = [xt[t] for t in range(T)] + [st_["OT"][0], st_["qs"][1][0]] + st_["PT"][0] + st_["PT"][5]

        def cross0():
            wof[0] = 0
            base = prev["wk"]
            qT_, kT_, V_ = [[wk(512).rearrange("p (k n) -> p k n", k=2) for _ in range(2)] for _ in range(3)]
            Pm = [wk(320) for _ in range(2)]
            PTn = wk(512).rearrange("p (c n) -> p c n", c=2)
            PTc = wk(256)[0:64, :]
            OTs = wk(512).rearrange("p (m n) -> p m n", m=2)
            sm = wk(16)
            st_ = {k: [] for k in ("PTn", "OTs", "sm0", "sm1", "P0", "P1")}
            st_.update({(k, i): [] for k in ("qT", "kT", "V") for i in range(2)})
            r1, r2 = Ring([0, 1, 2, 3]), Ring([4, 5, 6, 7])
            wt = P.landed(gxa)
            S_ = [dict() for _ in range(B)]

            def front(b):
                qT, kT, V = qT_[b % 2], kT_[b % 2], V_[b % 2]
                xs = [xnT[:, k, 256 * b:256 * b + 256] for k in range(2)]
                wx = [xnT_wr[2 * b], wt]
                for o, dst, nm in ((0, qT, "qT"), (256, kT, "kT")):
                    bk = r1.take()
                    for mt in range(2):
                        tk = mms(PS[bk][:, 256 * mt:256 * mt + 256],
                                 [(wxa[:, k, o + 128 * mt:o + 128 * mt + 128], xs[k]) for k in range(2)], [wx, bfree[bk]])
                    src = PS[bk][:, :].rearrange("p (k n) -> p k n", k=2)
                    ev = P.put("scalar", lambda e, dst=dst, src=src: e.copy(dst, src), [tk, st_[nm, b % 2], base])
                    bfree[bk] = [ev]
                    S_[b][nm] = ev
                bk = r1.take()
                for j in range(2):
                    t = 2 * b + j
                    tk = mms(PS[bk][:, 256 * j:256 * j + 256],
                             [(xnT[:, k, 128 * t:128 * t + 128], wxa[:, k, 512:768]) for k in range(2)], [wx, bfree[bk]])
                    xnT_rd[t] = [tk]
                ev = P.put("vector", lambda e, bk=bk: e.tensor_copy(V, PS[bk][:, :].rearrange("p (k n) -> p k n", k=2)),
                           [tk, st_["V", b % 2], base])
                bfree[bk] = [ev]
                S_[b]["V"] = ev

            def back(b):
                qT, kT, V = qT_[b % 2], kT_[b % 2], V_[b % 2]
                if b + 2 < B:
                    beside.append(layernorm_steps(b + 2, r1))
                if b:
                    beside.append(routed(0, b - 1, r1))
                tick()
                for j in range(2):
                    bk = r2.take()
                    lq = [qT[:, k, 128 * j:128 * j + 128] for k in range(2)]
                    for k in range(2):
                        P.put("tensor", lambda e, k=k, bk=bk, lq=lq: e.matmul(
                            PS[bk][:, 0:64], lq[k], ctxT[:, k, 64 * b:64 * b + 64], start=k == 0, stop=False,
                            skip_group_check=True), [S_[b]["qT"], S_[b]["kT"], bfree[bk]], sig=False)
                        tk = P.put("tensor", lambda e, k=k, bk=bk, lq=lq: e.matmul(
                            PS[bk][:, 64:320], lq[k], kT[:, k, :], start=False, stop=k == 1,
                            skip_group_check=True), sig=k == 1)
                    o = 8 * j
                    mx = P.put("vector", lambda e, bk=bk, o=o: e.tensor_reduce(sm[:, o:o + 1], PS[bk][:, 0:320], AX, ALU.max),
                               [tk, st_[f"sm{j}"], base])
                    nb = P.put("vector", lambda e, o=o: e.tensor_scalar(sm[:, o + 1:o + 2], sm[:, o:o + 1], -0.0625, None, ALU.mult), [mx])
                    ex = P.put("scalar", lambda e, bk=bk, o=o, j=j: e.activation(
                        Pm[j], PS[bk][:, 0:320], ACT.Exp, bias=sm[:, o + 1:o + 2], scale=0.0625,
                        accum_out=sm[:, o + 2:o + 3]), [nb, st_[f"P{j}"]])
                    bfree[bk] = [ex, mx]
                    S_[b]["rc", j] = P.put("vector", lambda e, o=o: e.reciprocal(sm[:, o + 3:o + 4], sm[:, o + 2:o + 3]), [ex])
                    S_[b]["P", j] = ex
                st_["qT", b % 2] = st_["kT", b % 2] = [tk]
                tick()
                if b + 1 < B:
                    front(b + 1)
                tick()
                bn, bc_ = r2.take(), r2.take()
                for j in range(2):
                    P.put("tensor", lambda e, j=j: e.transpose(
                        PS[bc_][0:64, 128 * j:128 * j + 128], Pm[j][:, 0:64], idf[:, :]),
                        [S_[b]["P", j], bfree[bc_]], sig=False)
                    for c in range(2):
                        tr = P.put("tensor", lambda e, j=j, c=c: e.transpose(
                            PS[bn][:, 256 * c + 128 * j:256 * c + 128 * j + 128], Pm[j][:, 64 + 128 * c:192 + 128 * c], idf[:, :]),
                            [bfree[bn]], sig=c == 1)
                    st_[f"P{j}"] = [tr]
                e1 = P.put("scalar", lambda e: e.copy(PTn, PS[bn][:, :].rearrange("p (c n) -> p c n", c=2)), [tr, st_["PTn"], base])
                e2 = P.put("vector", lambda e: e.tensor_copy(PTc, PS[bc_][0:64, 0:256]), [tr, st_["PTn"], base])
                bfree[bn], bfree[bc_] = [e1], [e2]
                tick()
                bk = r2.take()
                for mt in range(2):
                    ms = slice(128 * mt, 128 * mt + 128)
                    tk = mms(PS[bk][:, 256 * mt:256 * mt + 256],
                             [(ctxN[0:64, b, ms], PTc), (V[:, 0, ms], PTn[:, 0, :]), (V[:, 1, ms], PTn[:, 1, :])],
                             [e1, e2, S_[b]["V"], bfree[bk]])
                st_["V", b % 2] = st_["PTn"] = [tk]
                ev = P.put("scalar", lambda e, bk=bk: e.copy(OTs, PS[bk][:, :].rearrange("p (k n) -> p k n", k=2)),
                           [tk, st_["OTs"], base])
                bfree[bk] = [ev]
                bk = r2.take()
                for j in range(2):
                    tk = mms(PS[bk][:, 256 * j:256 * j + 256],
                             [(OTs[:, mt, 128 * j:128 * j + 128], wxa[:, mt, 768:1024]) for mt in range(2)], [ev, bfree[bk]])
                st_["OTs"] = [tk]
                tick(99)
                for j in range(2):
                    t = 2 * b + j
                    xt[t] = P.put("vector", lambda e, j=j, t=t, bk=bk: e.scalar_tensor_tensor(
                        out=x[:, t, :], in0=PS[bk][:, 256 * j:256 * j + 256], scalar=sm[:, 8 * j + 3:8 * j + 4],
                        in1=x[:, t, :], op0=ALU.mult, op1=ALU.add), [tk, S_[b]["rc", j], xt[t], xnT_wr[t]])
                    st_[f"sm{j}"] = [xt[t]]
                bfree[bk] = [xt[2 * b], xt[2 * b + 1]]

            front(0)
            for b in range(B):
                back(b)
            prev["wk"] = [xt[t] for t in range(T)] + [st_["OTs"][0]] + prev["wk"]

        def experts(L):
            wof[0] = 0
            NE, K, NT, NC = (8, 2, 39, 4) if L == 0 else (16, 4, 79, 1)
            HD = 128 * NC
            gm = P.landed(gm0 if L == 0 else gm1)
            base = prev["wk"]

            def te(n=NE, dt=F32):
                return wk(T * n, dt).rearrange("p (t e) -> p t e", e=n)

            G, Sel, Ia, Ib_ = te(), te(), te(), te()
            xall, Lg = XL[L]
            v8, rep = te(8), te(8)
            s1 = wk(2 * T).rearrange("p (a t) -> p a t", a=2)
            if L == 0:
                gk = ctxNw[:, 1544:1576].rearrange("p (t e) -> p t e", e=K)
                idx = ctxNw[:, 1576:1608].rearrange("p (t e) -> p t e", e=K).bitcast(I32)
            else:
                gk, idx = te(K), te(K).bitcast(I32)
            selb, cb = [wk(T * NE // 2, BF).rearrange("p (t e) -> p t e", e=NE) for _ in range(2)]
            ce, cf = wk(NE), wk(NE)
            endt, startt = wk(NE), wk(NE)
            sl = wk(NT)
            offs = wk(NT).bitcast(I32)
            NX, NY = (3, 2) if L == 0 else (5, 4)
            XB = [wk(256) for _ in range(NX)]
            XT = [wk(256).rearrange("p (k n) -> p k n", k=2) for _ in range(2)]
            cmp_ = wk(NT * NE)
            if L == 0:
                YG = [SM[:, 4096 + 256 * i:4352 + 256 * i] for i in range(4)] + [ctxNw[:, 256 * i:256 * i + 256] for i in range(4)]
            else:
                YG = [xall[:, i, :] for i in range(8)]
            Ub = [wk(HD) for _ in range(2)]
            UT = [wk(HD) for _ in range(2)]
            YB = [wk(256) for _ in range(NY)]
            assert L == 1 or wof[0] <= 5476
            rl = Ring([0, 1])

            for _ in routed(L, B - 1, rl):
                pass
            tl = list(lg_wr)
            lg_wr.clear()
            zr = P.put("vector", lambda e: e.memset(rep, BIG), base)
            for t in range(T):
                m8 = P.put("vector", lambda e, t=t: e.max(v8[:, t, :], Lg[:, t, :]), [tl])
            c = P.put("vector", lambda e: e.tensor_copy(rep[:, :, 0:K], v8[:, :, 0:K]), [m8, zr])
            for t in range(T):
                mr_ = P.put("vector", lambda e, t=t: e.match_replace(
                    out=Sel[:, t, :], in_to_replace=rep[:, t, :], in_values=Lg[:, t, :], imm_value=-BIG), [c])
            se = P.put("vector", lambda e: e.tensor_tensor(Sel, Sel, Lg, ALU.not_equal), [mr_])
            su = P.put("vector", lambda e: e.tensor_tensor(Lg, Lg, v8[:, :, 0:1].to_broadcast([128, T, NE]), ALU.subtract), [se])
            ex = P.put("scalar", lambda e: e.activation(Lg, Lg, ACT.Exp), [su])

            cur, oth = Ia, Ib_
            a = P.put("vector", lambda e: e.tensor_copy(Ia, Sel), [se])
            s_ = 1
            while s_ < T:
                a1 = P.put("vector", lambda e, cur=cur, oth=oth, s_=s_: e.tensor_tensor(
                    oth[:, s_:T, :], cur[:, s_:T, :], cur[:, 0:T - s_, :], ALU.add), [a])
                a = P.put("vector", lambda e, cur=cur, oth=oth, s_=s_: e.tensor_copy(oth[:, 0:s_, :], cur[:, 0:s_, :]))
                cur, oth = oth, cur
                s_ *= 2
            b1 = P.put("vector", lambda e: e.tensor_copy(selb, Sel))
            b2 = P.put("vector", lambda e: e.tensor_tensor(cb, cur, Sel, ALU.subtract), [a])
            b3 = P.put("vector", lambda e: e.tensor_copy(lastb[:, 0:NE], cur[:, T - 1, :]))
            bk = 3
            P.put("tensor", lambda e: e.matmul(PS[3][:, 0:T * NE], upb[:, :], selb.rearrange("p t e -> p (t e)"),
                                               start=True, stop=False, skip_group_check=True), [b3, t_up, bfree[3]], sig=False)
            r1_ = P.put("tensor", lambda e: e.matmul(PS[3][:, 0:T * NE], oneb[:, :], cb.rearrange("p t e -> p (t e)"),
                                                     start=False, stop=True, skip_group_check=True))
            r2_ = P.put("tensor", lambda e: e.matmul(PS[2][:, 0:NE], oneb[:, :], lastb[:, 0:NE], start=True, stop=True), [bfree[2]])
            a = P.put("vector", lambda e: e.tensor_scalar(ce, PS[2][:, 0:NE], 1.0 / 128.0, 127.0 / 128.0 - 0.5 + 1.0 / 512.0,
                                                          ALU.mult, ALU.add), [r2_, base])
            bfree[2] = [a]
            a = P.put("vector", lambda e: e.tensor_scalar(ce, ce, MAGIC, MAGIC, ALU.add, ALU.subtract), [a])
            cu, ot = ce, cf
            s_ = 1
            a = P.put("vector", lambda e: e.tensor_copy(startt, ce), [a])
            while s_ < NE:
                a = P.put("vector", lambda e, cu=cu, ot=ot, s_=s_: e.tensor_tensor(
                    ot[:, s_:NE], cu[:, s_:NE], cu[:, 0:NE - s_], ALU.add), [a])
                a = P.put("vector", lambda e, cu=cu, ot=ot, s_=s_: e.tensor_copy(ot[:, 0:s_], cu[:, 0:s_]))
                cu, ot = ot, cu
                s_ *= 2
            a = P.put("vector", lambda e: e.tensor_copy(endt, cu), [a])
            a = P.put("vector", lambda e: e.tensor_tensor(startt, endt, startt, ALU.subtract), [a])
            a = P.put("vector", lambda e: e.tensor_scalar(startt, startt, 128.0, 1.0, ALU.mult, ALU.add), [a])
            a = P.put("vector", lambda e: e.tensor_tensor(
                Ia, PS[3][:, 0:T * NE].rearrange("p (t e) -> p t e", e=NE), bc(startt, 1, T), ALU.add), [a, r1_])
            bfree[3] = [a]
            tv = P.put("vector", lambda e: e.tensor_tensor(Ia, Ia, Sel, ALU.mult), [a])
            for t in range(T):
                a = P.put("vector", lambda e, t=t: e.max(v8[:, t, :], Ia[:, t, :]), [tv])
            ti = P.put("vector", lambda e: e.tensor_scalar(idx, v8[:, :, 0:K], -1.0, None, ALU.add), [a])

            XSv, YSv = XS[0:128 * NT, :], YS[0:128 * NT, :]
            gsc = P.group(f"sc{L}")
            P.wait("gpsimd", [ti, t_fill, xall_wr, prev_y["ys"]])
            for t in range(T):
                for j in range(K):
                    gsc[2] += 16
                    P.q["gpsimd"].append(lambda e, t=t, j=j: e.indirect_dma_start(
                        XSv, bass.IndirectOffsetOnAxis(ap=idx[:, t, j:j + 1], axis=0), xall[:, t, :], None).then_inc(gsc[1], 16))

            if L == 0:
                kv_["zk"] = P.put("gpsimd", lambda e: e.memset(kMt, 0.0), base)
                for t in range(T):
                    xt[t] = P.put("gpsimd", lambda e, t=t: e.tensor_tensor(x[:, t, :], x[:, t, :], bm0, ALU.add),
                                  [xt[t], gm, xall_wr, xnT_wr[t]])

            mu = P.put("vector", lambda e: e.tensor_tensor(G, Lg, Sel, ALU.mult), [ex])
            sm_ = P.put("vector", lambda e: e.tensor_reduce(s1[:, 0, :], G, AX, ALU.add), [mu])
            rc_ = P.put("vector", lambda e: e.reciprocal(s1[:, 1, :], s1[:, 0, :]), [sm_])
            tg = P.put("vector", lambda e: e.scalar_tensor_tensor(
                out=G, in0=G, scalar=1.0 if L == 0 else 0.8, in1=bc(s1[:, 1, :], 2, NE), op0=ALU.mult, op1=ALU.mult), [rc_])
            for j in range(K):
                a = P.put("vector", lambda e, j=j: e.tensor_tensor(Ib_, Ia, v8[:, :, j:j + 1].to_broadcast([128, T, NE]), ALU.is_equal), [a, tg])
                a = P.put("vector", lambda e: e.tensor_tensor(Ib_, Ib_, G, ALU.mult), [a])
                a = P.put("vector", lambda e, j=j: e.tensor_reduce(gk[:, :, j], Ib_, AX, ALU.add), [a])
            tgk = a
            cv = cmp_.rearrange("p (s e) -> p s e", e=NE)
            a = P.put("vector", lambda e: e.tensor_tensor(
                cv, bc(slots[:, 0:NT], 2, NE), bc(endt, 1, NT), ALU.is_ge),
                [t_up, base])
            a = P.put("vector", lambda e: e.tensor_reduce(sl, cv, AX, ALU.add), [a, base])
            toff = P.put("vector", lambda e: e.tensor_scalar(offs, sl, NE - 1.0, 1024.0 if L == 0 else 256.0, ALU.min, ALU.mult), [a])

            gl = [P.group(f"l{L}{i}") for i in range(NX)]
            gs = [P.group(f"s{L}{i}") for i in range(NY)]
            st_ = {"XB": [[]] * NX, "XT": [[]] * 2, "U": [[]] * 2, "UT": [[]] * 2}
            st_ = {k: list(v) for k, v in st_.items()}
            rh = Ring([1, 2, 3, 4]) if L == 0 else Ring([1, 2, 3])
            ra, rt, ro_ = Ring([0]), Ring([5]), Ring([6, 7])
            S_ = [dict() for _ in range(NT)]

            def load(s):
                i = s % NX
                P.dma("sync", gl[i], XB[i], XSv[128 * s:128 * s + 128, :], [P.landed(gsc), st_["XB"][i], base])
                S_[s]["l"] = P.landed(gl[i])

            def turn(s):
                bk = ra.take()
                for k in range(2):
                    tr = P.put("tensor", lambda e, k=k: e.transpose(
                        PS[bk][:, 128 * k:128 * k + 128], XB[s % NX][:, 128 * k:128 * k + 128], idf[:, :]),
                        [S_[s]["l"], bfree[bk]] if k == 0 else (), sig=k == 1)
                st_["XB"][s % NX] = [tr]
                ev = P.put("scalar", lambda e: e.copy(XT[s % 2], PS[bk][:, 0:256].rearrange("p (k n) -> p k n", k=2)),
                           [tr, st_["XT"][s % 2], base])
                bfree[bk] = [ev]
                S_[s]["x"] = ev

            def up(s):
                n = 2 if L == 0 else 1
                bks = [rh.take() for _ in range(n)]
                P.wait("tensor", [S_[s]["x"], toff] + [bfree[b_] for b_ in bks])
                xt_ = XT[s % 2]

                def reg(e):
                    regs[s] = e.value_load(offs[0:1, s:s + 1], min_val=0, max_val=7168 if L == 0 else 3840)
                P.put("tensor", reg, sig=False)
                for q in range(n):
                    for k in range(2):
                        w_ = win0[:, k, :] if L == 0 else we13[:, k, :]
                        N_ = 512 if L == 0 else 256
                        tk = P.put("tensor", lambda e, q=q, k=k, w_=w_, N_=N_: e.matmul(
                            PS[bks[q]][:, 0:N_], xt_[:, k, :], w_[:, bass.ds(regs[s] + 512 * q if q else regs[s], N_)],
                            start=k == 0, stop=k == 1, skip_group_check=True), sig=k == 1 and q == n - 1)
                st_["XT"][s % 2] = [tk]
                pa = PS[bks[0]][:, 0:HD]
                pb_ = PS[bks[1]][:, 0:HD] if L == 0 else PS[bks[0]][:, HD:2 * HD]
                u = Ub[s % 2]
                si = P.put("scalar", lambda e: e.activation(u, pa, ACT.Silu), [tk, st_["U"][s % 2], base])
                mu_ = P.put("vector", lambda e: e.tensor_tensor(u, u, pb_, ALU.mult), [si])
                for b_ in bks:
                    bfree[b_] = [mu_]
                S_[s]["u"] = mu_

            def turn_u(s):
                bk = rt.take()
                for c in range(NC):
                    tr = P.put("tensor", lambda e, c=c: e.transpose(
                        PS[bk][:, 128 * c:128 * c + 128], Ub[s % 2][:, 128 * c:128 * c + 128], idf[:, :]),
                        [S_[s]["u"], bfree[bk]] if c == 0 else (), sig=c == NC - 1)
                st_["U"][s % 2] = [tr]
                ev = P.put("vector", lambda e: e.tensor_copy(UT[s % 2], PS[bk][:, 0:HD]), [tr, st_["UT"][s % 2], base])
                bfree[bk] = [ev]
                S_[s]["ut"] = ev

            def down(s):
                bk = ro_.take()
                P.wait("tensor", [S_[s]["ut"], bfree[bk]])
                for c in range(NC):
                    w_ = wout0f if L == 0 else we2f
                    tk = P.put("tensor", lambda e, c=c, w_=w_: e.matmul(
                        PS[bk][:, 0:256], UT[s % 2][:, 128 * c:128 * c + 128],
                        w_[:, bass.ds(regs[s] + 256 * c if c else regs[s], 256)],
                        start=c == 0, stop=c == NC - 1, skip_group_check=True), sig=c == NC - 1)
                st_["UT"][s % 2] = [tk]
                i = s % NY
                ev = P.put("vector" if L == 1 or s % 2 else "scalar",
                           (lambda e: e.tensor_copy(YB[i], PS[bk][:, 0:256])) if L == 1 or s % 2 else
                           (lambda e: e.copy(YB[i], PS[bk][:, 0:256])),
                           [tk, P.landed(gs[i]) if gs[i][2] else None, base])
                bfree[bk] = [ev]
                P.dma("sync", gs[i], YSv[128 * s:128 * s + 128, :], YB[i], [ev])

            if L == 1:
                sU = [wk(512) for _ in range(4)]
                sS = [wk(512) for _ in range(2)]
                fU, fS = [[]], [[], []]
                rsh, rso = Ring([1, 2, 3, 4]), Ring([5, 6, 7])

                def shared(blk):
                    toks = []
                    for c in range(4):
                        ba, bb = rsh.take(), rsh.take()
                        xs = [xnT[:, k, 512 * blk:512 * blk + 512] for k in range(2)]
                        dep = [xnT_wr[4 * blk], xnT_wr[4 * blk + 2], gm]
                        ta = mms(PS[ba][:, :], [(ws13[:, k, 128 * c:128 * c + 128], xs[k]) for k in range(2)], [dep, bfree[ba]])
                        tb = mms(PS[bb][:, :], [(ws13[:, k, 512 + 128 * c:640 + 128 * c], xs[k]) for k in range(2)], [bfree[bb]])
                        s2 = P.put("scalar", lambda e, c=c, ba=ba: e.activation(sS[c % 2], PS[ba][:, :], ACT.Silu), [ta, fS[c % 2], base])
                        m2 = P.put("vector", lambda e, c=c, bb=bb: e.tensor_tensor(sU[c], sS[c % 2], PS[bb][:, :], ALU.mult), [s2, tb, fU[0], base])
                        bfree[ba], bfree[bb] = [s2], [m2]
                        fS[c % 2] = [m2]
                        toks.append(m2)
                        yield
                    for tl_ in range(4):
                        t = 4 * blk + tl_
                        xnT_rd[t] = [tb]
                        bk = rso.take()
                        tk = mms(PS[bk][:, 0:256], [(sU[c][:, 128 * tl_:128 * tl_ + 128], ws2[:, c, :]) for c in range(4)],
                                 [toks, bfree[bk]])
                        xt[t] = P.put("vector", lambda e, t=t, bk=bk: e.scalar_tensor_tensor(
                            out=x[:, t, :], in0=PS[bk][:, 0:256], scalar=0.2, in1=x[:, t, :], op0=ALU.mult, op1=ALU.add),
                            [tk, xt[t], xnT_wr[t]])
                        bfree[bk] = [xt[t]]
                        fU[0] = [tk]
                        yield
            regs = {}
            if L == 1:
                for blk in range(3):
                    for _ in shared(blk):
                        pass
            for i in range(NX - 1):
                load(i)
            for i in range(NT + 3):
                if i + NX - 1 < NT:
                    load(i + NX - 1)
                if i < NT:
                    turn(i)
                if 1 <= i <= NT:
                    up(i - 1)
                if 2 <= i <= NT + 1:
                    turn_u(i - 2)
                if i >= 3:
                    down(i - 3)
            wend = [st_["UT"][0], st_["UT"][1]]
            if L == 1:
                last = shared(3)

            ys = [P.landed(g_) for g_ in gs]
            gg = [P.group(f"g{L}{i}") for i in range(8)]
            fY = [[] for _ in range(8)]

            def fetch(t):
                P.wait("gpsimd", ys + [P.landed(gsc), toff])
                for j in range(K):
                    i = (K * t + j) % 8
                    P.wait("gpsimd", [fY[i]])
                    gg[i][2] += 16
                    P.q["gpsimd"].append(lambda e, j=j, i=i: e.indirect_dma_start(
                        YG[i], None, YSv, bass.IndirectOffsetOnAxis(ap=idx[:, t, j:j + 1], axis=0)).then_inc(gg[i][1], 16))

            def add(t):
                for j in range(K):
                    i = (K * t + j) % 8
                    xt[t] = P.put("vector", lambda e, j=j, i=i: e.scalar_tensor_tensor(
                        out=x[:, t, :], in0=YG[i], scalar=gk[:, t, j:j + 1], in1=x[:, t, :], op0=ALU.mult, op1=ALU.add),
                        [(gg[i][0], gg[i][1], 16 * ((K * t + j) // 8 + 1)), tgk, xt[t]])
                    fY[i] = [xt[t]]

            prev_y["ys"] = [(g_[0], g_[1], 16 * (T * K // 8)) for g_ in gg] + ys
            if L == 0:
                rows["fetch"], rows["add"] = fetch, add
                prev["wk"] = [xt[t] for t in range(T)] + wend + ys + st_["XT"] + st_["U"] + st_["XB"]
            else:
                for t in range(T):
                    fetch(t)
                    next(last, None)
                    if t:
                        add(t - 1)
                add(T - 1)
            return wend

        def quant(src, am, s, r, dst, after, rd_dst):
            h3 = src.rearrange("p (h d) -> p h d", d=16)
            a = P.put("vector", lambda e: e.tensor_reduce(am, h3, AX, ALU.max, apply_absolute_value=True), after)
            yield
            a = P.put("vector", lambda e: e.tensor_scalar(s, am, 1.0 / 127.0, 1e-8, ALU.mult, ALU.max), [a])
            yield
            a = P.put("vector", lambda e: e.reciprocal(r, s), [a])
            yield
            a = P.put("vector", lambda e: e.tensor_tensor(h3, h3, bc(r, 2, 16), ALU.mult), [a])
            yield
            a = P.put("vector", lambda e: e.tensor_scalar(src, src, MAGIC, MAGIC, ALU.add, ALU.subtract), [a])
            yield
            return P.put("vector", lambda e: e.tensor_scalar(dst, src, 127.0, -127.0, ALU.min, ALU.max), [a] + rd_dst)

        def cross1_kv(ring, base):
            gt = P.landed(gx1)
            kM = kMt
            o_ = [0]

            def w(n, dt=F32):
                o_[0] += n
                v = W[:, o_[0] - n:o_[0]]
                return v if dt is F32 else v.bitcast(dt)

            kv, am, sk, rk = w(512), w(16), w(16), w(16)
            K3 = w(512, BF).rearrange("p (h c) -> p h c", c=64)
            vT = w(1024).rearrange("p (m n) -> p m n", m=2)
            vq = w(512, BF).rearrange("p (m n) -> p m n", m=2)
            zk = kv_["zk"]
            z3 = P.put("vector", lambda e: e.memset(K3, 0.0), base)
            fK3, fkv, kMw, tvs = [z3], [], [], []
            for c in range(4):
                bk = ring.take()
                tk = mms(PS[bk][:, :], [(ctxT[:, k, 128 * c:128 * c + 128], wkv[:, k, :]) for k in range(2)],
                         [gt, P.landed(gxa), bfree[bk]])
                a = P.put("vector", lambda e, bk=bk: e.tensor_tensor(kv, PS[bk][:, :], bkv, ALU.add), [tk, fkv, base])
                bfree[bk] = [a]
                yield
                bk = ring.take()
                for m_ in range(2):
                    tv = P.put("tensor", lambda e, m_=m_, bk=bk: e.transpose(
                        PS[bk][:, 128 * m_:128 * m_ + 128], kv[:, 256 + 128 * m_:384 + 128 * m_], idf[:, :]),
                        [a, bfree[bk]])
                tvs = [P.put("scalar", lambda e, bk=bk, c=c: e.copy(
                    vT[:, :, 128 * c:128 * c + 128], PS[bk][:, 0:256].rearrange("p (m n) -> p m n", m=2)), [tv, base])]
                bfree[bk] = tvs
                yield
                kk = kv[:, 0:256]
                a = yield from quant(kk, am, sk, rk, kk, [a], [])
                yield
                k3 = kk.rearrange("p (h d) -> p h d", d=16)
                a = P.put("vector", lambda e: e.tensor_tensor(k3, k3, bc(sk, 2, 16), ALU.mult), [a])
                yield
                a = P.put("vector", lambda e: e.tensor_copy(K3[:, :, 0:16], k3), [a] + fK3)
                yield
                a = P.put("vector", lambda e: e.tensor_tensor(k3, k3, K3[:, :, 0:16], ALU.subtract), [a])
                yield
                a = P.put("vector", lambda e: e.tensor_copy(K3[:, :, 16:32], k3), [a])
                yield
                a = P.put("vector", lambda e: e.tensor_tensor(K3[:, :, 32:48], k3, K3[:, :, 16:32], ALU.subtract), [a])
                fkv = [a, tv]
                yield
                bk = ring.take()
                for g in range(8):
                    tr = P.put("tensor", lambda e, g=g, bk=bk: e.transpose(
                        PB[bk][:, 128 * g:128 * g + 128], K3[:, 2 * g:2 * g + 2, :].rearrange("p h c -> p (h c)"), idb[:, :]),
                        [a, bfree[bk]] if g == 0 else (), sig=g == 7)
                fK3 = [tr]
                evs = []
                for o in range(2):
                    evs.append(P.put("vector", lambda e, o=o, bk=bk, c=c: e.tensor_copy(
                        kM[64 * o:64 * o + 64, o::2, 128 * c:128 * c + 128],
                        PB[bk][64 * o:64 * o + 64, :].rearrange("p (g n) -> p g n", g=8)), [tr, zk]))
                bfree[bk] = evs
                kMw += evs
                yield
            a = P.put("vector", lambda e: e.tensor_reduce(sv[:, 0:2], vT, AX, ALU.max, apply_absolute_value=True), tvs)
            yield
            a = P.put("vector", lambda e: e.tensor_scalar(sv[:, 0:2], sv[:, 0:2], 1.0 / 127.0, 1e-8, ALU.mult, ALU.max), [a])
            yield
            tsv = P.put("vector", lambda e: e.reciprocal(sv[:, 2:4], sv[:, 0:2]), [a])
            yield
            for m_ in range(2):
                a = P.put("vector", lambda e, m_=m_: e.tensor_scalar(vT[:, m_, :], vT[:, m_, :], sv[:, 2 + m_:3 + m_], None, ALU.mult), [tsv])
            yield
            for f in range(2):
                a = P.put("vector", lambda e, f=f: e.tensor_scalar(vT[:, f, :], vT[:, f, :], MAGIC, MAGIC, ALU.add, ALU.subtract), [a])
            yield
            a = P.put("vector", lambda e: e.tensor_scalar(vq, vT, 127.0, -127.0, ALU.min, ALU.max), [a, base])
            yield
            bk = ring.take()
            for c in range(4):
                for m_ in range(2):
                    tr = P.put("tensor", lambda e, m_=m_, c=c, bk=bk: e.transpose(
                        PB[bk][:, 256 * c + 128 * m_:256 * c + 128 * m_ + 128], vq[:, m_, 128 * c:128 * c + 128], idb[:, :]),
                        [a, bfree[bk]])
            tV = P.put("vector", lambda e, bk=bk: e.tensor_copy(Vq, PB[bk].rearrange("p (c n) -> p c n", c=4)), [tr, base])
            bfree[bk] = [tV]
            kv_["k"], kv_["v"] = kMw, [tV]
            P.dma("sync", gm1, we13, I["we13"].rearrange("(k p) n -> p k n", p=128), [tV, tr, kMw, fkv])

        def cross1():
            wof[0] = 0
            base = prev["wk"]
            gt = P.landed(gx1)
            kM = kMt
            am = wk(16)
            qf = wk(256)
            Q3 = wk(512, BF).rearrange("p (h c) -> p h c", c=64)
            q3T = [wk(512, BF).rearrange("p (g n) -> p g n", g=8) for _ in range(2)]
            sq = [wk(16) for _ in range(2)]
            nsq = [wk(16) for _ in range(2)]
            rq = wk(16)
            s4 = wk(16)
            mm_ = wk(16)
            nb = wk(16)
            se = [wk(16) for _ in range(2)]
            rs_ = wk(16)
            ee = [wk(512) for _ in range(4)]
            ei = [wk(256, BF) for _ in range(3)]
            aT = [wk(512, BF) for _ in range(2)]
            On = wk(256)
            OnT = wk(256).rearrange("p (k n) -> p k n", k=2)
            r1, r2, r3 = Ring([0, 1]), Ring([2, 3, 4]), Ring([5, 6])
            bO = 7

            zq = P.put("vector", lambda e: e.memset(Q3, 0.0), base)
            tkv = tV = kv_["v"]
            kMw = zk = kv_["k"]

            fq = {"qf": [], "Q3": [zq], "q3T": [[], []], "sq": [[], []], "m": [], "se": [[], []], "ee": [[] for _ in range(4)],
                  "ei": [[] for _ in range(3)], "aT": [[], []], "On": [], "OnT": [], "rs": []}
            n_e = [0]
            n_i = [0]
            n_a = [0]
            S_ = [dict() for _ in range(T)]

            def queries(t):
                bk = r1.take()
                tk = mms(PS[bk][:, 0:256], [(xnT[:, k, 128 * t:128 * t + 128], wq1[:, k, :]) for k in range(2)],
                         [xnT_wr[t], gt, bfree[bk]])
                xnT_rd[t] = [tk]
                yield
                a = P.put("vector", lambda e: e.tensor_tensor(qf, PS[bk][:, 0:256], bq1, ALU.add), [tk, fq["qf"], base])
                bfree[bk] = [a]
                s_ = sq[t % 2]
                q3 = qf.rearrange("p (h d) -> p h d", d=16)
                dst = Q3[:, :, 0:48].rearrange("p h (c d) -> p h c d", d=16)
                a = P.put("vector", lambda e: e.tensor_reduce(am, q3, AX, ALU.max, apply_absolute_value=True), [a, tkv])
                yield
                a = P.put("vector", lambda e: e.tensor_scalar(s4, am, 1.0 / 127.0, 4e-8, ALU.mult, ALU.max), [a])
                yield
                b1 = P.put("vector", lambda e: e.tensor_scalar(s_, s4, 0.25, None, ALU.mult), [a, fq["sq"][t % 2], base])
                b2 = P.put("vector", lambda e: e.tensor_scalar(nsq[t % 2], s4, -0.25, None, ALU.mult))
                S_[t]["nsq"] = b2
                a = P.put("vector", lambda e: e.reciprocal(rq, s4), [a])
                yield
                a = P.put("vector", lambda e: e.tensor_tensor(q3, q3, bc(rq, 2, 16), ALU.mult), [a])
                yield
                a = P.put("vector", lambda e: e.tensor_scalar(qf, qf, MAGIC, MAGIC, ALU.add, ALU.subtract), [a])
                yield
                a = P.put("vector", lambda e: e.tensor_scalar(dst, bc(q3, 2, 3), 127.0, -127.0, ALU.min, ALU.max), [a, fq["Q3"]])
                fq["qf"] = [a]
                yield
                bk2 = r1.take()
                for g in range(8):
                    tr = P.put("tensor", lambda e, g=g: e.transpose(
                        PB[bk2][:, 128 * g:128 * g + 128], Q3[:, 2 * g:2 * g + 2, :].rearrange("p h c -> p (h c)"), idb[:, :]),
                        [a, bfree[bk2]] if g == 0 else (), sig=g == 7)
                fq["Q3"] = [tr]
                ev = P.put("scalar", lambda e: e.copy(q3T[t % 2], PB[bk2].rearrange("p (g n) -> p g n", g=8)),
                           [tr, fq["q3T"][t % 2], base])
                bfree[bk2] = [ev]
                S_[t]["q"] = ev

            units = [(t, h) for t in range(T) for h in range(H)]
            U_ = {}

            def u_scores(t, h):
                bk = r2.take()
                tk = P.put("tensor", lambda e: e.matmul(PS[bk][:, :], q3T[t % 2][:, h // 2, :], kM[:, h, :], start=True, stop=True),
                           [S_[t]["q"], kMw, zk, bfree[bk]])
                if h == H - 1:
                    fq["q3T"][t % 2] = [tk]
                U_[t, h] = [bk, tk]

            def u_exp(t, h):
                bk, tk = U_[t, h]
                mx = P.put("vector", lambda e: e.tensor_reduce(mm_[:, h:h + 1], PS[bk][:, :], AX, ALU.max),
                           [tk, fq["m"][h] if fq["m"] else (), base])
                i = n_e[0] % 4
                n_e[0] += 1
                a = P.put("gpsimd", lambda e: e.tensor_scalar(
                    nb[:, h:h + 1], mm_[:, h:h + 1], nsq[t % 2][:, h:h + 1], LN255, ALU.mult, ALU.add),
                    [mx, S_[t]["nsq"], fq["nb"][h] if "nb" in fq else ()])
                fm = fq.setdefault("mlist", {})
                fm[h] = [a]
                fq["m"] = [fm.get(i_, []) for i_ in range(H)]
                ex = P.put("scalar", lambda e: e.activation(
                    ee[i], PS[bk][:, :], ACT.Exp, bias=nb[:, h:h + 1], scale=sq[t % 2][:, h:h + 1],
                    accum_out=se[t % 2][:, h:h + 1]), [a, fq["ee"][i], fq["se"][t % 2]])
                fn = fq.setdefault("nlist", {})
                fn[h] = [ex]
                fq["nb"] = [fn.get(i_, []) for i_ in range(H)]
                bfree[bk] = [ex, mx]
                if h == H - 1:
                    fq["sq"][t % 2] = [ex]
                U_[t, h] = [i, None, ex]

            def u_round(t, h):
                i, _, ex = U_[t, h]
                k = n_i[0] % 3
                n_i[0] += 1
                ro2 = P.put("vector", lambda e: e.tensor_scalar(ei[k], ee[i], MAGIC, MAGIC, ALU.add, ALU.subtract), [ex, fq["ei"][k]])
                fq["ee"][i] = [ro2]
                U_[t, h] = [k, ro2, ex]

            def u_tr(t, h):
                if h % 2 == 0:
                    U_["bank"] = r3.take()
                bk = U_["bank"]
                i, ro2, ex = U_[t, h]
                for c in range(4):
                    tr = P.put("tensor", lambda e, c=c: e.transpose(
                        PB[bk][:, 512 * (h % 2) + 128 * c:512 * (h % 2) + 128 * c + 128], ei[i][:, 128 * c:128 * c + 128], idb[:, :]),
                        [ro2, bfree[bk] if h % 2 == 0 else ()], sig=c == 3)
                fq["ei"][i] = [tr]
                if h % 2 == 1:
                    i2 = n_a[0] % 2
                    n_a[0] += 1
                    ev = P.put("scalar", lambda e: e.copy(aT[i2], PB[bk]), [tr, fq["aT"][i2], base])
                    bfree[bk] = [ev]
                    U_["a", t, h // 2] = (i2, ev)

            def u_pv(t, hp):
                i2, ev = U_["a", t, hp]
                for h in (2 * hp, 2 * hp + 1):
                    for c in range(4):
                        pv = P.put("tensor", lambda e, h=h, c=c: e.matmul(
                            PS[bO][:, 16 * h:16 * h + 16], aT[i2][:, 512 * (h % 2) + 128 * c:512 * (h % 2) + 128 * c + 128],
                            Vq[:, c, 16 * h:16 * h + 16], start=h == 0 and c == 0, stop=c == 3, skip_group_check=True),
                            [ev, tV, bfree[bO] if h == 0 else ()], sig=c == 3 and h % 2 == 1)
                fq["aT"][i2] = [pv]
                if hp == 7:
                    d = done(t, pv)
                    next(d)
                    bg.append(d)
                    if t % 2 == 1 and t < T - 1:
                        bg.append(routed(1, t // 2, r1))

            def done(t, pv):
                ex = U_[t, H - 1][2]
                r = P.put("vector", lambda e: e.reciprocal(rs_, se[t % 2]), [ex, fq["rs"]])
                fq["se"][t % 2] = [r]
                o = P.put("vector", lambda e: e.tensor_tensor(
                    On.rearrange("p (h d) -> p h d", d=16), PS[bO][:, 0:256].rearrange("p (h d) -> p h d", d=16),
                    bc(rs_, 2, 16), ALU.mult), [r, pv, fq["On"]])
                fq["rs"] = [o]
                bfree[bO] = [o]
                xa = P.put("gpsimd", lambda e: e.tensor_tensor(x[:, t, :], x[:, t, :], bp1, ALU.add), [xt[t], gt, xnT_wr[t]])
                yield
                bk = r1.take()
                for k in range(2):
                    tr = P.put("tensor", lambda e, k=k: e.transpose(
                        PS[bk][:, 128 * k:128 * k + 128], On[:, 128 * k:128 * k + 128], idf[:, :]),
                        [o, bfree[bk]] if k == 0 else (), sig=k == 1)
                fq["On"] = [tr]
                yield
                for k in range(2):
                    ev = P.put("vector", lambda e, k=k: e.tensor_scalar(
                        OnT[:, k, :], PS[bk][:, 128 * k:128 * k + 128], sv[:, k:k + 1], None, ALU.mult), [tr, fq["OnT"]])
                bfree[bk] = [ev]
                yield
                bk2 = r1.take()
                mo = mms(PS[bk2][:, 0:256], [(OnT[:, k, :], wp1[:, k, :]) for k in range(2)], [ev, bfree[bk2]])
                fq["OnT"] = [mo]
                yield
                xt[t] = P.put("vector", lambda e: e.tensor_tensor(x[:, t, :], x[:, t, :], PS[bk2][:, 0:256], ALU.add), [mo, xa])
                bfree[bk2] = [xt[t]]

            bg = []

            def step(n=1):
                while n and bg:
                    if next(bg[0], "end") == "end":
                        bg.pop(0)
                    n -= 1

            for _ in queries(0):
                pass
            N = len(units)
            for i in range(N + 8):
                if i < N:
                    t, h = units[i]
                    if h == 0:
                        step(99)
                        if t + 1 < T:
                            bg.append(queries(t + 1))
                    if h == 8 and t % 2 == 0 and 0 < t < T - 2:
                        bg.append(layernorm_steps(t // 2 + 1, r1))
                    u_scores(t, h)
                if 1 <= i <= N:
                    u_exp(*units[i - 1])
                if 3 <= i < N + 3:
                    u_round(*units[i - 3])
                if i >= 8 and units[i - 8][1] % 2 == 1:
                    u_pv(units[i - 8][0], units[i - 8][1] // 2)
                if 5 <= i < N + 5:
                    u_tr(*units[i - 5])
                step()
            step(99)
            prev["wk"] = [xt[t] for t in range(T)] + fq["q3T"][0] + fq["q3T"][1] + fq["OnT"]

        def out_all():
            go = P.group("out")
            od = out.rearrange("(t p) d -> p t d", p=128)
            for t in range(T):
                P.dma("sync", go, od[:, t, :], x[:, t, :], [xt[t]])
            P.wait("sync", [P.landed(go)])

        attn_phase(0)
        prev["wk"] = prev["wk"] + [t_fill, t_up]
        P.dma("sync", gm0, win0[:, 1, 4096:8192], win_d[:, 1, 4096:8192], [prev["wk"]])
        P.dma("sync", gm0, wout0, I["w_out0"].rearrange("(c p) n -> p c n", p=128))
        if upto >= 2:
            cross0()
        kMt = SM[:, 0:4096].bitcast(BF).rearrange("p (h n) -> p h n", h=H)
        if upto >= 3:
            fU = experts(0)
            gm1 = P.group("m1")
            we13 = W[:, 0:8192].rearrange("p (k n) -> p k n", k=2)
            we2f = W[:, 8192:12288]
            we2 = we2f.rearrange("p (c n) -> p c n", c=16)
            ws13 = W[:, 12288:14336].rearrange("p (k n) -> p k n", k=2)
            ws2 = W[:, 14336:15360].rearrange("p (c n) -> p c n", c=4)
            o = 15392
            wq1 = W[:, o:o + 512].rearrange("p (k n) -> p k n", k=2)
            wkv = W[:, o + 512:o + 1536].rearrange("p (k n) -> p k n", k=2)
            wp1 = W[:, o + 1536:o + 2048].rearrange("p (k n) -> p k n", k=2)
            bq1, bkv, bp1 = W[:, o + 2048:o + 2304], W[:, o + 2304:o + 2816], W[:, o + 2816:o + 3072]
            P.dma("sync", gat1, wA[1], I["w_att1"].rearrange("(k p) n -> p k n", p=128), fU)
            P.dma("sync", gat1, bA[1], bcast(I["b_att1"]))
            P.dma("sync", gx1, wq1, I["w_q1"].rearrange("(k p) n -> p k n", p=128))
            P.dma("sync", gx1, wkv, I["w_kv1"].rearrange("(k p) n -> p k n", p=128))
            P.dma("sync", gx1, wp1, I["w_p1"].rearrange("(k p) n -> p k n", p=128))
            for v, n in ((bq1, "b_q1"), (bkv, "b_kv1"), (bp1, "b_p1")):
                P.dma("sync", gx1, v, bcast(I[n]))

            def experts1_weights():
                P.wait("sync", [xt[3]])
                P.dma("sync", gm1, we2, I["we2"].rearrange("(c p) n -> p c n", p=128))
                P.dma("sync", gm1, ws13, I["ws13"].rearrange("(k p) n -> p k n", p=128))
                P.dma("sync", gm1, ws2, I["ws2"].rearrange("(c p) n -> p c n", p=128))
                P.dma("sync", gm1_, wr1, I["w_r1"].rearrange("(k p) n -> p k n", p=128))
            Vq = ctxNw[:, 1024:1536].bitcast(BF).rearrange("p (c n) -> p c n", c=4)
            sv = ctxNw[:, 1536:1540]
            if upto == 3:
                for t in range(T):
                    rows["fetch"](t)
                    rows["add"](t)
        if upto >= 4:
            attn_phase(1)
        if upto >= 5:
            cross1()
        if upto >= 6:
            experts(1)
        out_all()
        for g in P.groups:
            if g[2]:
                P.wait("sync", [P.landed(g)])
        P.emit()


def constants():
    i = np.arange(128)
    sq = np.zeros((128, 512), np.float32)
    sq[:, 384:512] = np.where(i[:, None] < i[None, :], 1.0, 0.0)
    sq[:, 0:128] = np.eye(128)
    sq[:, 128:256] = np.where(i[None, :] > i[:, None], -1e30, 0.0)
    sq[:, 256:384] = np.where(i[:, None] > i[None, :], -1e30, 0.0)
    E = np.zeros((48, H, 128), np.float32)
    for h in range(H):
        for c in range(3):
            E[16 * c + h, h, :] = 1.0

    def part(v):
        out, r = [], v.astype(np.float32)
        for _ in range(3):
            b = r.view(np.uint32)
            b = ((b + 0x7FFF + ((b >> 16) & 1)) & 0xFFFF0000).astype(np.uint32).view(np.float32)
            out.append(b)
            r = (r - b).astype(np.float32)
        return out

    start = 2.0 ** (-8.0 / H)
    slopes = np.array([start * start ** h for h in range(H)], np.float32) * np.float32(4)
    ali = np.zeros((128, 2, 2, H, 32), np.float32)
    for j in range(2):
        pos = (128 * j + i).astype(np.float32)
        for c in range(3):
            ali[:, 0, j, :, c] = 1.0
            ali[:, 0, j, :, 3 + c] = pos[:, None]
            ali[:, 1, j, :, c] = part(slopes[None, :] * pos[:, None])[c]
            ali[:, 1, j, :, 3 + c] = -part(slopes)[c][None, :]
    return {"c_sq": sq, "c_E": E.reshape(48, H * 128), "c_ali": ali.reshape(128, 2048)}


_OUT = ((2048, 256), "float32")


def layout(inp):
    c = np.ascontiguousarray
    cat = np.concatenate
    a = {k: np.asarray(v) for k, v in inp.items()}
    m = {"x": c(a["x"].reshape(2048, 256))}
    m["w_att0"] = cat([a["L0_attn_wq"], a["L0_attn_wk"], a["L0_attn_wv"]], 1)
    m["b_att0"] = cat([a["L0_attn_bq"], a["L0_attn_bk"], a["L0_attn_bv"]])
    m["w_o0"], m["b_o0"] = a["L0_attn_wo"], a["L0_attn_bo"]
    m["w_xa0"] = cat([a[f"L0_xattn_{n}"].T for n in ("wq", "wk", "wv", "wo")], 1)
    ctx = a["ctx_2048"]
    m["ctxT"] = c(ctx.reshape(512, 256).T)
    m["ctxN"] = c(ctx.transpose(1, 0, 2))
    m["w_in0"] = c(a["L0_ffn_w_in"].transpose(2, 0, 1).reshape(256, 8192))
    m["w_out0"] = c(a["L0_ffn_w_out"].transpose(0, 2, 1).reshape(4096, 256))
    m["w_r0"] = c(a["L0_ffn_router_weight"].T)
    m["b_m0"] = a["L0_ffn_bias"]
    flat = lambda w: w.transpose(1, 0, 2).reshape(256, -1)
    m["w_att1"] = cat([flat(a[f"L1_attn_W{n}"]) for n in "qkv"], 1)
    m["b_att1"] = cat([a[f"L1_attn_b{n}"].reshape(-1) for n in "qkv"])
    m["w_q1"], m["w_kv1"], m["w_p1"] = a["L1_xattn_Wq"], a["L1_xattn_Wkv"], a["L1_xattn_Wp"]
    m["b_q1"], m["b_kv1"], m["b_p1"] = a["L1_xattn_bq"], a["L1_xattn_bkv"], a["L1_xattn_bp"]
    m["we13"] = flat(cat([a["L1_ffn_we1"], a["L1_ffn_we3"]], 2))
    m["we2"] = a["L1_ffn_we2"].reshape(2048, 256)
    m["ws13"] = cat([a["L1_ffn_ws1"], a["L1_ffn_ws3"]], 1)
    m["ws2"] = a["L1_ffn_ws2"]
    m["w_r1"] = a["L1_ffn_w_router"]
    m.update(constants())
    return {k: c(v) for k, v in m.items()}


def kernel(**inputs):
    import concourse.bacc as _bacc
    from concourse.bass_utils import run_bass_kernel_spmd as _run

    nc = _bacc.Bacc("TRN2", target_bir_lowering=False, num_devices=1)
    arrays = layout(inputs)
    I = {k: nc.dram_tensor(f"in_{k}", v.shape, mybir.dt.from_np(v.dtype), kind="ExternalInput").ap()
         for k, v in arrays.items()}
    out = nc.dram_tensor("out_0", _OUT[0], F32, kind="ExternalOutput").ap()
    decoder(nc, I, out)
    r = _run(nc, [{f"in_{k}": v for k, v in arrays.items()}], core_ids=[0])
    return r.results[0]["out_0"].reshape(8, 256, 256)
```
